# Optimizing a Trainium2 kernel written in Bass

```python
import numpy as np
import jax
import jax.numpy as jnp

def _softmax(x, axis=-1):
    return jax.nn.softmax(x, axis=axis)

def _gelu(x):
    return jax.nn.gelu(x, approximate=True)

def _silu(x):
    return jax.nn.silu(x)

def _sigmoid(x):
    return jax.nn.sigmoid(x)

def _layernorm(x, axis=-1, eps=1e-05):
    m = jnp.mean(x, axis=axis, keepdims=True)
    v = jnp.var(x, axis=axis, keepdims=True)
    return (x - m) / jnp.sqrt(v + eps)

def _scatter_add(tgt, idx, src, axis=0):
    return tgt.at[idx].add(src)

def _segment_sum(src, seg, n):
    return jax.ops.segment_sum(src, seg, n)
kernel_name = 'mk_conv_seq_d2_conv_nchw96_r2_2b335a'

def setup_inputs(seed: int=0):
    np.random.seed(seed)
    _w = jnp.asarray

    def _rec_inputs():
        import jax
        import jax.numpy as jnp
        _gk = jax.random.key(seed)
        x = -0.0001476 + 0.9999 * jax.random.normal(jax.random.fold_in(_gk, 1), (8, 48, 112, 112), jnp.float32)
        return x
    x = _rec_inputs()

    def _L0_conv_setup():
        import jax, jax.numpy as jnp
        import numpy as np
        WS = 7
        SHIFT = 3
        HEADS = 3
        EPS = 1e-05

        def _rel_index():
            coords = np.stack(np.meshgrid(np.arange(WS), np.arange(WS), indexing='ij')).reshape(2, -1)
            rel = (coords[:, :, None] - coords[:, None, :]).transpose(1, 2, 0) + (WS - 1)
            return jnp.asarray(rel[..., 0] * (2 * WS - 1) + rel[..., 1])

        def _layernorm(x, g, b):
            mu = jnp.mean(x, axis=-1, keepdims=True)
            var = jnp.mean(jnp.square(x - mu), axis=-1, keepdims=True)
            return (x - mu) * jax.lax.rsqrt(var + EPS) * g + b
        key = jax.random.key(seed)
        ks = jax.random.split(key, 6)
        C, HID = (48, 192)
        s = 0.02
        return {'x': jax.random.normal(ks[0], (8, C, 112, 112), jnp.float32), 'norm1_g': jnp.ones((C,), jnp.float32), 'norm1_b': jnp.zeros((C,), jnp.float32), 'qkv_w': jax.random.normal(ks[1], (C, 3 * C), jnp.float32) * s, 'qkv_b': jnp.zeros((3 * C,), jnp.float32), 'proj_w': jax.random.normal(ks[2], (C, C), jnp.float32) * s, 'proj_b': jnp.zeros((C,), jnp.float32), 'rel_bias_table': jax.random.normal(ks[3], ((2 * WS - 1) ** 2, HEADS), jnp.float32) * s, 'norm2_g': jnp.ones((C,), jnp.float32), 'norm2_b': jnp.zeros((C,), jnp.float32), 'fc1_w': jax.random.normal(ks[4], (C, HID), jnp.float32) * s, 'fc1_b': jnp.zeros((HID,), jnp.float32), 'fc2_w': jax.random.normal(ks[5], (HID, C), jnp.float32) * s, 'fc2_b': jnp.zeros((C,), jnp.float32)}
    _L0_conv_all = _L0_conv_setup()
    _L0_conv_in = {k: v for k, v in _L0_conv_all.items() if k in ('norm1_g', 'norm1_b', 'qkv_w', 'qkv_b', 'proj_w', 'proj_b', 'rel_bias_table', 'norm2_g', 'norm2_b', 'fc1_w', 'fc1_b', 'fc2_w', 'fc2_b')}
    del _L0_conv_all

    def _L1_conv_setup():
        import jax, jax.numpy as jnp
        import numpy as np
        from jax import lax
        DIM = 48
        KS = 7
        EPS = 1e-06
        key = jax.random.key(seed)
        ks = jax.random.split(key, 12)
        N, C, H, W = (32, DIM, 56, 56)
        s = 0.02
        x = jax.random.normal(ks[0], (N, C, H, W), dtype=jnp.float32)
        dw_w = jax.random.normal(ks[1], (C, 1, KS, KS), dtype=jnp.float32) * s
        dw_b = jnp.zeros((C,), dtype=jnp.float32)
        ln_g = jnp.ones((C,), dtype=jnp.float32)
        ln_b = jnp.zeros((C,), dtype=jnp.float32)
        w1 = jax.random.normal(ks[2], (4 * C, C), dtype=jnp.float32) * s
        b1 = jnp.zeros((4 * C,), dtype=jnp.float32)
        grn_g = jnp.zeros((4 * C,), dtype=jnp.float32)
        grn_b = jnp.zeros((4 * C,), dtype=jnp.float32)
        w2 = jax.random.normal(ks[3], (C, 4 * C), dtype=jnp.float32) * s
        b2 = jnp.zeros((C,), dtype=jnp.float32)
        return {'x': x, 'dw_w': dw_w, 'dw_b': dw_b, 'ln_g': ln_g, 'ln_b': ln_b, 'w1': w1, 'b1': b1, 'grn_g': grn_g, 'grn_b': grn_b, 'w2': w2, 'b2': b2}
    _L1_conv_all = _L1_conv_setup()
    _L1_conv_in = {k: v for k, v in _L1_conv_all.items() if k in ('dw_w', 'dw_b', 'ln_g', 'ln_b', 'w1', 'b1', 'grn_g', 'grn_b', 'w2', 'b2')}
    del _L1_conv_all
    return {'x': x, 'L0_conv_norm1_g': _L0_conv_in['norm1_g'], 'L0_conv_norm1_b': _L0_conv_in['norm1_b'], 'L0_conv_qkv_w': _L0_conv_in['qkv_w'], 'L0_conv_qkv_b': _L0_conv_in['qkv_b'], 'L0_conv_proj_w': _L0_conv_in['proj_w'], 'L0_conv_proj_b': _L0_conv_in['proj_b'], 'L0_conv_rel_bias_table': _L0_conv_in['rel_bias_table'], 'L0_conv_norm2_g': _L0_conv_in['norm2_g'], 'L0_conv_norm2_b': _L0_conv_in['norm2_b'], 'L0_conv_fc1_w': _L0_conv_in['fc1_w'], 'L0_conv_fc1_b': _L0_conv_in['fc1_b'], 'L0_conv_fc2_w': _L0_conv_in['fc2_w'], 'L0_conv_fc2_b': _L0_conv_in['fc2_b'], 'L1_conv_dw_w': _L1_conv_in['dw_w'], 'L1_conv_dw_b': _L1_conv_in['dw_b'], 'L1_conv_ln_g': _L1_conv_in['ln_g'], 'L1_conv_ln_b': _L1_conv_in['ln_b'], 'L1_conv_w1': _L1_conv_in['w1'], 'L1_conv_b1': _L1_conv_in['b1'], 'L1_conv_grn_g': _L1_conv_in['grn_g'], 'L1_conv_grn_b': _L1_conv_in['grn_b'], 'L1_conv_w2': _L1_conv_in['w2'], 'L1_conv_b2': _L1_conv_in['b2']}

def reference(x, L0_conv_norm1_g, L0_conv_norm1_b, L0_conv_qkv_w, L0_conv_qkv_b, L0_conv_proj_w, L0_conv_proj_b, L0_conv_rel_bias_table, L0_conv_norm2_g, L0_conv_norm2_b, L0_conv_fc1_w, L0_conv_fc1_b, L0_conv_fc2_w, L0_conv_fc2_b, L1_conv_dw_w, L1_conv_dw_b, L1_conv_ln_g, L1_conv_ln_b, L1_conv_w1, L1_conv_b1, L1_conv_grn_g, L1_conv_grn_b, L1_conv_w2, L1_conv_b2):
    import jax
    import jax.numpy as jnp

    def _L0_conv_ref(x, norm1_g, norm1_b, qkv_w, qkv_b, proj_w, proj_b, rel_bias_table, norm2_g, norm2_b, fc1_w, fc1_b, fc2_w, fc2_b):
        import jax, jax.numpy as jnp
        import numpy as np
        WS = 7
        SHIFT = 3
        HEADS = 3
        EPS = 1e-05

        def _rel_index():
            coords = np.stack(np.meshgrid(np.arange(WS), np.arange(WS), indexing='ij')).reshape(2, -1)
            rel = (coords[:, :, None] - coords[:, None, :]).transpose(1, 2, 0) + (WS - 1)
            return jnp.asarray(rel[..., 0] * (2 * WS - 1) + rel[..., 1])

        def _layernorm(x, g, b):
            mu = jnp.mean(x, axis=-1, keepdims=True)
            var = jnp.mean(jnp.square(x - mu), axis=-1, keepdims=True)
            return (x - mu) * jax.lax.rsqrt(var + EPS) * g + b
        B, C, H, W = x.shape
        N = WS * WS
        dh = C // HEADS
        xt = x.reshape(B, C, H * W).transpose(0, 2, 1)
        xn = _layernorm(xt, norm1_g, norm1_b)
        xs = xn.transpose(0, 2, 1).reshape(B, C, H, W)
        xs = jnp.roll(xs, (-SHIFT, -SHIFT), axis=(2, 3))
        xw = xs.reshape(B, C, H // WS, WS, W // WS, WS)
        xw = xw.transpose(0, 2, 4, 3, 5, 1).reshape(-1, N, C)
        Bw = xw.shape[0]
        qkv = (xw @ qkv_w + qkv_b).reshape(Bw, N, 3, HEADS, dh).transpose(2, 0, 3, 1, 4)
        q, k, v = (qkv[0], qkv[1], qkv[2])
        attn = jnp.einsum('bhnd,bhmd->bhnm', q, k) * dh ** (-0.5)
        bias = rel_bias_table[_rel_index().reshape(-1)].reshape(N, N, HEADS).transpose(2, 0, 1)
        attn = jax.nn.softmax(attn + bias, axis=-1)
        out = jnp.einsum('bhnm,bhmd->bhnd', attn, v).transpose(0, 2, 1, 3).reshape(Bw, N, C)
        out = out @ proj_w + proj_b
        xr = out.reshape(B, H // WS, W // WS, WS, WS, C)
        xr = xr.transpose(0, 5, 1, 3, 2, 4).reshape(B, C, H, W)
        xr = jnp.roll(xr, (SHIFT, SHIFT), axis=(2, 3))
        x = x + xr
        xt = x.reshape(B, C, H * W).transpose(0, 2, 1)
        xn = _layernorm(xt, norm2_g, norm2_b)
        h = jax.nn.gelu(xn @ fc1_w + fc1_b, approximate=False)
        h = h @ fc2_w + fc2_b
        return x + h.transpose(0, 2, 1).reshape(B, C, H, W)

    def _L1_conv_ref(x, dw_w, dw_b, ln_g, ln_b, w1, b1, grn_g, grn_b, w2, b2):
        import jax, jax.numpy as jnp
        import numpy as np
        from jax import lax
        DIM = 48
        KS = 7
        EPS = 1e-06
        C = x.shape[1]
        pad = KS // 2
        y = lax.conv_general_dilated(x, dw_w, window_strides=(1, 1), padding=[(pad, pad), (pad, pad)], dimension_numbers=('NCHW', 'OIHW', 'NCHW'), feature_group_count=C)
        y = y + dw_b[None, :, None, None]
        y = jnp.transpose(y, (0, 2, 3, 1))
        mu = jnp.mean(y, axis=-1, keepdims=True)
        var = jnp.mean(jnp.square(y - mu), axis=-1, keepdims=True)
        y = (y - mu) * lax.rsqrt(var + EPS) * ln_g + ln_b
        y = jnp.einsum('nhwc,fc->nhwf', y, w1) + b1
        y = jax.nn.gelu(y, approximate=False)
        gx = jnp.sqrt(jnp.sum(jnp.square(y), axis=(1, 2), keepdims=True))
        nx = gx / (jnp.mean(gx, axis=-1, keepdims=True) + EPS)
        y = grn_g * (y * nx) + grn_b + y
        y = jnp.einsum('nhwf,cf->nhwc', y, w2) + b2
        y = jnp.transpose(y, (0, 3, 1, 2))
        return x + y

    def _gn(v, G=32, eps=1e-05):
        B_, C_, H_, W_ = v.shape
        g = v.reshape(B_, G, C_ // G, H_, W_)
        m = jnp.mean(g, axis=(2, 3, 4), keepdims=True)
        s = jnp.var(g, axis=(2, 3, 4), keepdims=True)
        return ((g - m) / jnp.sqrt(s + eps)).reshape(v.shape)

    def _ln_c(v, eps=1e-06):
        m = jnp.mean(v, axis=1, keepdims=True)
        s = jnp.var(v, axis=1, keepdims=True)
        return (v - m) / jnp.sqrt(s + eps)

    def _ln_t(v, eps=1e-05):
        m = jnp.mean(v, axis=-1, keepdims=True)
        s = jnp.var(v, axis=-1, keepdims=True)
        return (v - m) / jnp.sqrt(s + eps)

    def _to_tokens(v):
        B_, C_, H_, W_ = v.shape
        return v.reshape(B_, C_, H_ * W_).transpose(0, 2, 1)

    def _from_tokens(t, like):
        B_, C_, H_, W_ = like.shape
        return t.transpose(0, 2, 1).reshape(B_, C_, H_, W_)
    x = _L0_conv_ref(x, L0_conv_norm1_g, L0_conv_norm1_b, L0_conv_qkv_w, L0_conv_qkv_b, L0_conv_proj_w, L0_conv_proj_b, L0_conv_rel_bias_table, L0_conv_norm2_g, L0_conv_norm2_b, L0_conv_fc1_w, L0_conv_fc1_b, L0_conv_fc2_w, L0_conv_fc2_b)
    x = _L1_conv_ref(x, L1_conv_dw_w, L1_conv_dw_b, L1_conv_ln_g, L1_conv_ln_b, L1_conv_w1, L1_conv_b1, L1_conv_grn_g, L1_conv_grn_b, L1_conv_w2, L1_conv_b2)
    return x

_drawn_inputs = setup_inputs


def setup_inputs(seed=0):
    import zlib

    import numpy as np

    out = dict(_drawn_inputs(seed))
    spreads = {'L0_conv_norm1_g': (1.0, 0.6),
     'L0_conv_norm1_b': (0.0, 0.8),
     'L0_conv_qkv_b': (0.0, 0.722),
     'L0_conv_proj_b': (0.0, 0.1),
     'L0_conv_norm2_g': (1.0, 0.6),
     'L0_conv_norm2_b': (0.0, 0.8),
     'L0_conv_fc1_b': (0.0, 0.45),
     'L0_conv_fc2_b': (0.0, 0.1),
     'L1_conv_dw_b': (0.0, 0.662),
     'L1_conv_ln_g': (1.0, 0.6),
     'L1_conv_ln_b': (0.0, 0.8),
     'L1_conv_b1': (0.0, 0.475),
     'L1_conv_grn_g': (0.0, 0.8),
     'L1_conv_grn_b': (0.0, 0.393),
     'L1_conv_b2': (0.0, 0.1)}
    factors = {'L0_conv_qkv_w': 8.0,
     'L0_conv_proj_w': 5.55,
     'L0_conv_rel_bias_table': 8.0,
     'L0_conv_fc1_w': 2.796,
     'L1_conv_dw_w': 3.283}
    for name, (base, spread) in spreads.items():
        noise = np.random.default_rng([zlib.crc32(name.encode()), seed]).standard_normal(out[name].shape)
        drawn = base * np.exp(spread * noise) if base else spread * noise
        out[name] = jnp.asarray(drawn.astype(out[name].dtype))
    for name, factor in factors.items():
        out[name] = (out[name] * factor).astype(out[name].dtype)
    return out
```

```python
from contextlib import ExitStack

import concourse.bass as bass
from concourse import mybir

F32 = mybir.dt.float32
BF16 = mybir.dt.bfloat16
ALU = mybir.AluOpType
ACT = mybir.ActivationFunctionType
AX_X = mybir.AxisListType.X

C = 48
HID = 192
IMG = 112
WS = 7
TOK = WS * WS
HEADS = 3
DH = C // HEADS
SHIFT = WS // 2
PLANE = IMG * IMG
STRIP = WS * IMG
WINS = IMG // WS
STRIPS = IMG // WS // 2
HALF = STRIP // 2
QUADS = 4
QP = WINS // QUADS
HQ = HEADS * TOK
ROWB = 64
ONE = C
R = ROWB + C + 1
KEYS = 2 * TOK
F1 = 128
F2 = HID - F1
EPS0 = 1e-5
EPS1 = 1e-6
PAD = IMG + 2 * SHIFT
SPAN = 2 * WS - 1
REL = SPAN ** 2
RUN = SPAN * (WS - 1) + WS


def wait(eng, sem, value):
    if not isinstance(value, int) or value > 0:
        eng.wait_ge(sem, value)


class Strip:

    def __init__(self, i, raw, total):
        self.i, self.raw, self.total = i, raw, total

    def at(self, d):
        return Strip(self.i, self.raw + d, self.total)

    @property
    def n(self):
        return 4 * self.i + self.raw

    @property
    def real(self):
        return not isinstance(self.i, int) or 0 <= self.raw < self.total

    def slot(self, ring):
        return self.raw % ring

    def turn(self, ring):
        return (4 // ring) * self.i + self.raw // ring


def attention_phase(nc, x_in, prm, con, tables, table_runs, x2_dram, strips):
    with ExitStack() as ctx:
        def sb(name, shape, dt=F32):
            return ctx.enter_context(nc.sbuf_tensor(name, shape, dt))

        def sem(name):
            return ctx.enter_context(nc.semaphore(name))

        ps_s = ctx.enter_context(nc.psum_tensor("ps_s", [128, 2, 512], F32))
        ps_t = ctx.enter_context(nc.psum_tensor("ps_t", [128, 2, 512], F32))
        ps_v = ctx.enter_context(nc.psum_tensor("ps_v", [128, 512], F32))
        ps_o = ctx.enter_context(nc.psum_tensor("ps_o", [128, 512], F32))
        ps_m = ctx.enter_context(nc.psum_tensor("ps_m", [128, 2, 512], F32))

        center = sb("center", [R, R])
        spread = sb("spread", [R, R])
        eye_c = sb("eye_c", [C, C + 1])
        last_row = sb("last_row", [1, C + 1])
        const_f = sb("const_f", [R, R + KEYS + KEYS + TOK])
        const_b = sb("const_b", [R, R + KEYS + KEYS + TOK], BF16)
        pick_q = const_b[:, 0:R]
        pick_k = const_b[:, R:R + KEYS]
        group_ones = const_b[:, R + KEYS:R + 2 * KEYS]
        minus_eye = const_b[:, R + 2 * KEYS:R + 2 * KEYS + TOK]
        key_ones = sb("key_ones", [KEYS, 2 * DH])
        qkv_w = sb("qkv_w", [C, 3 * C])
        fc1_w = sb("fc1_w", [C, HID])
        rows = sb("rows", [1, 3 * C + HID])
        norms = sb("norms", [C, 4])
        aug = sb("aug", [C, 2, C + 1])
        qk_aug = sb("qk_aug", [DH, 2 * HEADS, C + 1])
        gram = [sb(f"gram_{p}", [R, HEADS, R], BF16) for p in "hl"]
        wv = [sb(f"wv_{p}", [R, 2 * C], BF16) for p in "hl"]
        w1_own = [sb(f"w1_own_{p}", [R, F1], BF16) for p in "hl"]
        w1_both = [sb(f"w1_both_{p}", [R, 2 * F2], BF16) for p in "hl"]
        proj_w = sb("proj_w", [2 * C, R])
        proj_b = sb("proj_b", [R, 1])
        fc2_b = sb("fc2_b", [R, 1])
        out_b = sb("out_b", [R, 1])
        centred_b = sb("centred_b", [R, 1])
        w2_own = sb("w2_own", [F1, C])
        w2_both = sb("w2_both", [2 * F2, ROWB + C])
        bias_f = sb("bias_f", [R, 2, HQ])
        bias = sb("bias", [R, 2, HQ], BF16)
        eps = sb("eps", [R, 1])

        X = sb("X", [R, 4, STRIP])
        x1 = sb("x1", [R, 2, STRIP])
        x2 = sb("x2", [R, 2, STRIP])
        xc = [sb(f"xc{a}", [R, STRIP]) for a in range(2)]
        sq = [sb(f"sq{a}", [R, STRIP]) for a in range(2)]
        lnv = [sb(f"lnv{a}", [R, STRIP]) for a in range(2)]
        rs = [sb(f"rs{a}", [R, STRIP]) for a in range(2)]
        xh = [sb(f"xh{a}", [R, STRIP]) for a in range(2)]
        xm = [[sb(f"xm{a}_{p}", [R, 2, STRIP], BF16) for p in "hl"] for a in range(2)]
        xs = [sb(f"xs_{p}", [R, 2, WINS, KEYS], BF16) for p in "hl"]
        U = [sb(f"u_{p}", [R, 2, HEADS, STRIP], BF16) for p in "hl"]
        qmax = sb("qmax", [R, 2, QP * HEADS])
        shift = sb("shift", [R, 2, QP * HEADS, TOK], BF16)
        P = sb("P", [KEYS, 2, QP, HEADS, TOK])
        V = sb("V", [KEYS, 2, QP, 2 * C])
        lden = sb("lden", [2 * C, QP * TOK])
        rden = sb("rden", [2 * C, 2, QP * TOK])
        O = sb("O", [2 * C, 2, STRIP])
        G = sb("G", [128, 2, 3, STRIP])

        loaded = sem("loaded")
        table_turned = sem("table_turned")
        runs_made = sem("runs_made")
        setup_v = sem("setup_v")
        setup_t = sem("setup_t")
        cleared = sem("cleared")
        x_loaded = [sem(f"x_loaded{r}") for r in range(4)]
        x2_stored = [sem(f"x2_stored{r}") for r in range(2)]
        names = ("cen var uu s_q st_q v_q pv_q proj f1 f2 xc xh hi xs_copied u_lo mx nrm x1_made "
                 "x2_made sq ln rs u_hi ex vev lnd rdn ge lo md").split()
        pair = {"cen", "var", "xc", "xh", "hi", "sq", "ln", "rs", "lo"}
        S = {}
        for nm in names:
            S[nm] = [sem(f"{nm}{a}_done") for a in range(2)] if nm in pair else sem(f"{nm}_done")

        def halves(ap):
            return ap.rearrange("p (b n) -> p b n", b=2)

        N = strips
        CLEARS = 17
        SETUP_V = 9 + 2 + 2 + 16

        LOOPED = 4
        TURNS = (N - 2 - LOOPED) // 4

        def steps(eng, step, first, last):
            for raw in range(first, LOOPED):
                step(Strip(0, raw, N))
            with eng.Fori(0, TURNS) as i:
                for u in range(4):
                    step(Strip(i, LOOPED + u, N))
            for raw in range(LOOPED + 4 * TURNS, last):
                step(Strip(0, raw, N))

        x2_strips = x2_dram.rearrange("b c (g s n) -> b s g c n", g=2, s=STRIPS)

        loads = [
            (center[:], con["center"]), (spread[:], con["spread0"]), (eye_c[:], con["eye_c"]),
            (last_row[:], con["last_row"]), (const_f[:], con["picks"]), (key_ones[:], con["key_ones"]),
            (qkv_w[:], prm["qkv_w"]), (fc1_w[:], prm["fc1_w"]), (w2_own[:], prm["fc2_w"][0:F1, :]),
            (rows[0:1, 0:3 * C], prm["qkv_b"].unsqueeze(0)), (rows[0:1, 3 * C:], prm["fc1_b"].unsqueeze(0)),
        ]
        loads += [(norms[:, k:k + 1], prm[nm].unsqueeze(1))
                  for k, nm in enumerate(("norm1_g", "norm1_b", "norm2_g", "norm2_b"))]
        for g in range(2):
            lo = ROWB * g
            loads += [(proj_b[lo:lo + C, :], prm["proj_b"].unsqueeze(1)),
                      (fc2_b[lo:lo + C, :], prm["fc2_b"].unsqueeze(1)),
                      (w2_both[F2 * g:F2 * g + F2, lo:lo + C], prm["fc2_w"][F1:HID, :])]
            loads += [(proj_w[2 * DH * h + DH * g:2 * DH * h + DH * g + DH, lo:lo + C],
                       prm["proj_w"][DH * h:DH * h + DH, :]) for h in range(HEADS)]
        runs_of_rows = []
        for side in range(2):
            for a in range(WS):
                src = bass.AP(tensor=tables[side].tensor, offset=(WS - 1 - a) * SPAN + WS - 1,
                              ap=[[REL, HEADS], [-1, WS], [1, RUN]])
                runs_of_rows.append((table_runs[side][:, WS * a:WS * a + WS, :], src))
        blocks = []
        for side in range(2):
            for h in range(HEADS):
                src = bass.AP(tensor=table_runs[side].tensor, offset=h * TOK * RUN,
                              ap=[[RUN, TOK], [SPAN, WS], [1, WS]])
                dst = bias_f[0:TOK, side, TOK * h:TOK * h + TOK]
                blocks.append((dst.rearrange("p (a b) -> p a b", a=WS), src))

        block = ctx.enter_context(nc.Block())

        @block.sync
        def _(sp):
            sp.wait_ge(cleared, CLEARS)
            for dst, src in loads:
                sp.dma_start(dst, src).then_inc(loaded, 16)

            def x_load(s):
                if s.real:
                    wait(sp, S["x1_made"], 2 * (s.n - 3))
                    for g in range(2):
                        sp.dma_start(X[ROWB * g:ROWB * g + C, s.slot(4), :],
                                     x_in[s.n, g]).then_inc(x_loaded[s.slot(4)], 16)

            def x2_store(s):
                if s.real:
                    wait(sp, S["x2_made"], 2 * s.n + 2)
                    for g in range(2):
                        dst = x2_strips[s.n // STRIPS, s.n % STRIPS, g]
                        sp.dma_start(dst, x2[ROWB * g:ROWB * g + C, s.slot(2), :]
                                     ).then_inc(x2_stored[s.slot(2)], 16)

            for raw in range(2):
                x_load(Strip(0, raw, N))
            for tab, first, sign in ((tables[0], (REL - 1) * HEADS, -1), (tables[1], 0, 1)):
                sp.dma_start(tab, bass.AP(tensor=prm["rel_bias_table"].tensor, offset=first,
                                          ap=[[1, HEADS], [sign * HEADS, REL], [1, 1]]),
                             allow_slow_non_contiguous=True).then_inc(table_turned, 16)
            sp.wait_ge(table_turned, 32)
            for dst, src in runs_of_rows:
                sp.dma_start(dst, src).then_inc(runs_made, 16)
            sp.wait_ge(runs_made, 16 * len(runs_of_rows))
            for dst, src in blocks:
                sp.dma_start(dst, src).then_inc(loaded, 16)

            def step(s):
                x_load(s.at(2))
                x2_store(s.at(-2))

            steps(sp, step, 0, N + 2)
            for r in range(2):
                sp.wait_ge(x2_stored[r], 32 * (N // 2))

        @block.gpsimd
        def _(pool):
            for t in (*gram, *wv, *w1_own, *w1_both, xs[0], xs[1]):
                nc.gpsimd.memset(t[:], 0.0).then_inc(cleared, 1)
            for t in (proj_w, proj_b, fc2_b, w2_both, bias_f):
                nc.gpsimd.memset(t[:], 0.0).then_inc(cleared, 1)
            nc.gpsimd.memset(eps[:], EPS0).then_inc(cleared, 1)
            nc.gpsimd.memset(X[:], 1.0).then_inc(cleared, 1)

            def low(a, s):
                if s.real:
                    wait(pool, S["hi"][a], s.n + 1)
                    wait(pool, (S["uu"], S["f1"])[a], 6 * (s.n - 1))
                    if a == 0:
                        wait(pool, S["xs_copied"], 4 * (s.n - 1))
                    r = s.slot(2)
                    nc.gpsimd.tensor_tensor(xm[a][1][:, r, :], xh[a][:], xm[a][0][:, r, :],
                                            ALU.subtract).then_inc(S["lo"][a], 1)

            def make_shift(s, j):
                if s.real:
                    q = 4 * s.n + j
                    wait(pool, S["mx"], q + 1)
                    wait(pool, S["st_q"], q - 1)
                    m = qmax[:, j % 2, :].unsqueeze(2).to_broadcast([R, QP * HEADS, TOK])
                    e = minus_eye.unsqueeze(1).to_broadcast([R, QP * HEADS, TOK])
                    nc.gpsimd.tensor_tensor(shift[:, j % 2], e, m, ALU.mult).then_inc(S["md"], 1)

            def step(s):
                if s.real:
                    make_shift(s, 1)
                low(0, s.at(1))
                if s.real:
                    make_shift(s, 2)
                    make_shift(s, 3)
                low(1, s.at(-1))
                make_shift(s.at(1), 0)

            steps(pool, step, -1, N + 1)

        @block.vector
        def _(dve):
            chain = [0]

            def link(ins):
                chain[0] += 1
                ins.then_inc(setup_v, 1)
                return chain[0]

            dve.wait_ge(cleared, CLEARS)
            dve.wait_ge(loaded, 16 * (len(loads) + len(blocks)))
            link(nc.vector.tensor_copy(const_b[:], const_f[:]))
            for a in range(2):
                link(nc.vector.tensor_scalar(aug[:, a, 0:C], eye_c[:, 0:C], norms[:, 2 * a:2 * a + 1], None, ALU.mult))
                link(nc.vector.tensor_copy(aug[:, a, C:C + 1], norms[:, 2 * a + 1:2 * a + 2]))
            k = link(nc.vector.tensor_copy(bias_f[ROWB:ROWB + TOK], bias_f[0:TOK]))
            dve.wait_ge(setup_v, k)
            link(nc.vector.tensor_copy(bias[:], bias_f[:]))
            dve.wait_ge(setup_v, k + 1)
            k = link(nc.vector.tensor_tensor(bias_f[ROWB:R], bias_f[ROWB:R], bias[ROWB:R], ALU.subtract))
            dve.wait_ge(setup_v, k)
            k = link(nc.vector.tensor_copy(bias[ROWB:R], bias_f[ROWB:R]))
            dve.wait_ge(setup_t, 1)
            qk = ps_m[0:DH, 0, 0:6 * (C + 1)].rearrange("p (a c) -> p a c", a=6)
            k = link(nc.vector.tensor_scalar(qk_aug[:, 0:HEADS, :], qk[:, 0:HEADS, :], DH ** -0.5, None, ALU.mult))
            k = link(nc.vector.tensor_copy(qk_aug[:, HEADS:, :], qk[:, HEADS:, :]))
            dve.wait_ge(setup_t, 2)
            link(nc.vector.tensor_scalar(centred_b[:], ps_v[0:R, 0:1], -1.0, None, ALU.mult))
            link(nc.vector.tensor_tensor(out_b[:], proj_b[:], fc2_b[:], ALU.add))
            splits = []
            for g in range(2):
                lo = ROWB * g
                src_g = ps_s[lo:lo + C + 1, 0, 0:HEADS * (C + 1)].rearrange("p (h c) -> p h c", h=HEADS)
                splits.append((gram, lambda t, lo=lo: t[lo:lo + C + 1, :, lo:lo + C + 1], src_g))
                src_v = ps_s[lo:lo + C + 1, 1, 0:C].rearrange("p (h d) -> p h d", h=HEADS)
                splits.append((wv, lambda t, lo=lo, g=g: t[lo:lo + C + 1, :].rearrange(
                    "p (h g d) -> p h g d", h=HEADS, g=2)[:, :, g, :], src_v))
                splits.append((w1_own, lambda t, lo=lo: t[lo:lo + C + 1, :], ps_s[lo:lo + C + 1, 1, C:C + F1]))
                splits.append((w1_both, lambda t, lo=lo, g=g: t[lo:lo + C + 1, F2 * g:F2 * g + F2],
                               ps_s[lo:lo + C + 1, 1, C + F1:C + HID]))
            for pair_, view, src in splits:
                k = link(nc.vector.tensor_copy(view(pair_[0]), src))
                dve.wait_ge(setup_v, k)
                k = link(nc.vector.tensor_tensor(view(pair_[1]), src, view(pair_[0]), ALU.subtract))

            def copy_centered(a, s):
                if s.real:
                    for b in range(2):
                        wait(dve, S["cen"][a], 2 * s.n + b + 1)
                        cols = slice(HALF * b, HALF * b + HALF)
                        if a == 0:
                            ins = nc.vector.tensor_copy(xc[0][:, cols], ps_m[0:R, b, 0:HALF])
                        else:
                            ins = nc.vector.tensor_scalar(xc[1][:, cols], ps_m[0:R, b, 0:HALF], centred_b[:, 0:1],
                                                          None, ALU.add)
                        ins.then_inc(S["xc"][a], 1)

            def normalise(a, s):
                if s.real:
                    wait(dve, S["rs"][a], s.n + 1)
                    wait(dve, S["lo"][a], s.n)
                    nc.vector.tensor_tensor(xh[a][:], xc[a][:], rs[a][:], ALU.mult).then_inc(S["xh"][a], 1)
                    wait(dve, S["xh"][a], s.n + 1)
                    if a == 0:
                        wait(dve, S["s_q"], 4 * (s.n - 1))
                    else:
                        wait(dve, S["f1"], 6 * (s.n - 1))
                    nc.vector.tensor_copy(xm[a][0][:, s.slot(2), :], xh[a][:]).then_inc(S["hi"][a], 1)

            def block_diagonal(p, s):
                if s.real:
                    wait(dve, (S["hi"], S["lo"])[p][0], s.n + 1)
                    wait(dve, S["st_q"], 4 * (s.n - 1))
                    wait(dve, S["v_q"], 4 * (s.n - 1))
                    for g in range(2):
                        lo = ROWB * g
                        nc.vector.tensor_copy(
                            xs[p][lo:lo + C + 1, s.slot(2), :, TOK * g:TOK * g + TOK],
                            xm[0][p][lo:lo + C + 1, s.slot(2), :].rearrange("p (w t) -> p w t", t=TOK),
                        ).then_inc(S["xs_copied"], 1)

            def u_low(s, h):
                if s.real:
                    r = s.slot(2)
                    for b in range(2):
                        wait(dve, S["u_hi"], 6 * s.n + 2 * h + b + 1)
                        cols = slice(HALF * b, HALF * b + HALF)
                        nc.vector.tensor_tensor(U[1][:, r, h, cols], ps_m[0:R, b, 0:HALF], U[0][:, r, h, cols],
                                                ALU.subtract).then_inc(S["u_lo"], 1)

            def query_max(s, j):
                if s.real:
                    q = 4 * s.n + j
                    wait(dve, S["s_q"], q + 1)
                    wait(dve, S["md"], q - 1)
                    nc.vector.tensor_reduce(
                        qmax[:, j % 2, :].rearrange("p (b n) -> p b n", b=2),
                        ps_s[0:R, :, 0:2 * HQ].rearrange("p b (n t) -> p b n t", t=TOK),
                        AX_X, ALU.max).then_inc(S["mx"], 1)

            def divide(s, j):
                if s.real:
                    q = 4 * s.n + j
                    wait(dve, S["rdn"], q + 1)
                    wait(dve, S["proj"], 2 * (s.n - 1))
                    W = QP * TOK
                    nc.vector.tensor_tensor(O[:, s.slot(2), W * j:W * j + W], ps_o[0:2 * C, 0:W],
                                            rden[:, j % 2, :], ALU.mult).then_inc(S["nrm"], 1)

            def first_residual(s):
                if s.real:
                    wait(dve, S["cen"][1], 2 * (s.n - 1))
                    for b in range(2):
                        wait(dve, S["proj"], 2 * s.n + b + 1)
                        cols = slice(HALF * b, HALF * b + HALF)
                        nc.vector.scalar_tensor_tensor(
                            out=x1[:, s.slot(2), cols], in0=ps_m[0:R, b, 0:HALF], scalar=out_b[:, 0:1],
                            in1=X[:, s.slot(4), cols], op0=ALU.add, op1=ALU.add).then_inc(S["x1_made"], 1)

            def second_residual(s):
                if s.real:
                    wait(dve, x2_stored[s.slot(2)], 32 * s.turn(2))
                    n = ROWB + C
                    for b in range(2):
                        wait(dve, S["f2"], 2 * s.n + b + 1)
                        win = slice(WINS // 2 * b, WINS // 2 * b + WINS // 2)
                        out = x2[0:n, s.slot(2), :].rearrange("p (i w j) -> p w i j", i=WS, j=WS)[:, win]
                        nc.vector.tensor_tensor(
                            out, ps_m[0:n, b, 0:HALF].rearrange("p (w i j) -> p w i j", i=WS, j=WS),
                            x1[0:n, s.slot(2), :].rearrange("p (w i j) -> p w i j", i=WS, j=WS)[:, win],
                            ALU.add).then_inc(S["x2_made"], 1)

            def step(s):
                nxt, prv = s.at(1), s.at(-1)
                if s.real:
                    query_max(s, 1)
                copy_centered(0, nxt)
                divide(prv, 3)
                second_residual(s.at(-2))
                normalise(0, nxt)
                first_residual(prv)
                block_diagonal(0, nxt)
                if s.real:
                    query_max(s, 2)
                copy_centered(1, prv)
                divide(s, 0)
                block_diagonal(1, nxt)
                u_low(nxt, 0)
                if s.real:
                    query_max(s, 3)
                u_low(nxt, 1)
                normalise(1, prv)
                divide(s, 1)
                u_low(nxt, 2)
                divide(s, 2)
                query_max(nxt, 0)

            steps(dve, step, -1, N + 2)

        @block.scalar
        def _(act):
            act.wait_ge(cleared, CLEARS)

            def square(a, s):
                if s.real:
                    for b in range(2):
                        wait(act, S["xc"][a], 2 * s.n + b + 1)
                        cols = slice(HALF * b, HALF * b + HALF)
                        nc.scalar.activation(sq[a][:, cols], xc[a][:, cols], ACT.Square).then_inc(S["sq"][a], 1)

            def root(a, s):
                if s.real:
                    for b in range(2):
                        wait(act, S["var"][a], 2 * s.n + b + 1)
                        nc.scalar.activation(lnv[a][:, HALF * b:HALF * b + HALF], ps_m[0:R, b, 0:HALF], ACT.Ln,
                                             bias=eps[:, 0:1]).then_inc(S["ln"][a], 1)
                    wait(act, S["ln"][a], 2 * s.n + 2)
                    nc.scalar.activation(rs[a][:], lnv[a][:], ACT.Exp, scale=-0.5).then_inc(S["rs"][a], 1)

            def u_high(s, h):
                if s.real:
                    wait(act, S["st_q"], 4 * (s.n - 1))
                    for b in range(2):
                        wait(act, S["uu"], 6 * s.n + 2 * h + b + 1)
                        nc.scalar.copy(U[0][:, s.slot(2), h, HALF * b:HALF * b + HALF], ps_m[0:R, b, 0:HALF]
                                       ).then_inc(S["u_hi"], 1)

            def exp_scores(s, j):
                q = 4 * s.n + j
                wait(act, S["st_q"], q + 1)
                wait(act, S["pv_q"], q - 1)
                nc.scalar.activation(P[:, j % 2].rearrange("p (b n) h t -> p b (n h t)", b=2),
                                     ps_t[0:KEYS, :, 0:2 * HQ], ACT.Exp).then_inc(S["ex"], 1)

            def keep_values(s, j):
                q = 4 * s.n + j
                wait(act, S["v_q"], q + 1)
                wait(act, S["pv_q"], q - 1)
                nc.scalar.copy(V[:, j % 2].rearrange("p n c -> p (n c)"),
                               ps_v[0:KEYS, 0:QP * 2 * C]).then_inc(S["vev"], 1)

            def invert_sums(s, j):
                if s.real:
                    q = 4 * s.n + j
                    W = QP * TOK
                    wait(act, S["pv_q"], q + 1)
                    nc.scalar.activation(lden[:], ps_o[0:2 * C, W:2 * W], ACT.Ln).then_inc(S["lnd"], 1)
                    wait(act, S["lnd"], q + 1)
                    wait(act, S["nrm"], q - 1)
                    nc.scalar.activation(rden[:, j % 2, :], lden[:], ACT.Exp, scale=-1.0).then_inc(S["rdn"], 1)

            def gelu(s, t):
                if s.real:
                    wait(act, S["f2"], 2 * (s.n - 1))
                    r = s.slot(2)
                    for b in range(2):
                        wait(act, S["f1"], 6 * s.n + 2 * t + b + 1)
                        if t < 2:
                            out = G[:, r, b, HALF * t:HALF * t + HALF]
                        else:
                            out = G[:, r, 2, HALF * b:HALF * b + HALF]
                        nc.scalar.activation(out, ps_m[:, b, 0:HALF], ACT.Gelu).then_inc(S["ge"], 1)

            def step(s):
                nxt, prv = s.at(1), s.at(-1)
                gelu(s.at(-2), 2)
                nc.scalar.preload_act_table_set("natural_log_exp_and_others")
                if s.real:
                    exp_scores(s, 0)
                square(0, nxt)
                if s.real:
                    keep_values(s, 0)
                invert_sums(prv, 3)
                root(0, nxt)
                if s.real:
                    exp_scores(s, 1)
                    keep_values(s, 1)
                    invert_sums(s, 0)
                square(1, prv)
                u_high(nxt, 0)
                if s.real:
                    exp_scores(s, 2)
                root(1, prv)
                u_high(nxt, 1)
                if s.real:
                    keep_values(s, 2)
                invert_sums(s, 1)
                u_high(nxt, 2)
                if s.real:
                    exp_scores(s, 3)
                invert_sums(s, 2)
                if prv.real:
                    nc.scalar.preload_act_table_set("gelu_and_others")
                gelu(prv, 0)
                if s.real:
                    keep_values(s, 3)
                gelu(prv, 1)

            steps(act, step, -1, N + 2)

        @block.tensor
        def _(pe):
            mm = nc.tensor.matmul
            pe.wait_ge(setup_v, 5)
            for k in range(2 * HEADS):
                out = ps_m[0:DH, 0, (C + 1) * k:(C + 1) * (k + 1)]
                mm(out, qkv_w[:, DH * k:DH * k + DH], aug[:, 0, :], start=True, stop=False)
                ins = mm(out, rows[0:1, DH * k:DH * k + DH], last_row[:], start=False, stop=True)
            ins.then_inc(setup_t, 1)
            pe.wait_ge(setup_v, 11)
            mm(ps_v[0:R, 0:1], center[:], fc2_b[:], start=True, stop=True)
            for g in range(2):
                lo = ROWB * g
                for h in range(HEADS):
                    mm(ps_s[lo:lo + C + 1, 0, (C + 1) * h:(C + 1) * (h + 1)], qk_aug[:, h, :],
                       qk_aug[:, HEADS + h, :], start=True, stop=True)
                out = ps_s[lo:lo + C + 1, 1, 0:C]
                mm(out, aug[:, 0, :], qkv_w[:, 2 * C:3 * C], start=True, stop=False)
                mm(out, last_row[:], rows[0:1, 2 * C:3 * C], start=False, stop=True)
                out = ps_s[lo:lo + C + 1, 1, C:C + HID]
                mm(out, aug[:, 1, :], fc1_w[:], start=True, stop=False)
                ins = mm(out, last_row[:], rows[0:1, 3 * C:], start=False, stop=True)
            ins.then_inc(setup_t, 1)
            pe.wait_ge(setup_v, SETUP_V)

            last = [None, None]

            def free_m(b):
                if last[b] is not None:
                    wait(pe, *last[b])

            def per_strip(w, src, done, s, feeder, emptied):
                for b in range(2):
                    if feeder is not None:
                        wait(pe, feeder, 2 * s.n + b + 1)
                    free_m(b)
                    mm(ps_m[0:R, b, 0:HALF], w, src[:, HALF * b:HALF * b + HALF], start=True, stop=True
                       ).then_inc(done, 1)
                    last[b] = (emptied, 2 * s.n + b + 1)

            def centre(a, s):
                if s.real:
                    if a == 0:
                        wait(pe, x_loaded[s.slot(4)], 32 * (s.turn(4) + 1))
                        per_strip(center[:], X[:, s.slot(4), :], S["cen"][0], s, None, S["xc"][0])
                    else:
                        per_strip(center[:], x1[:, s.slot(2), :], S["cen"][1], s, S["x1_made"], S["xc"][1])

            def variance(a, s):
                if s.real:
                    per_strip(spread[:], sq[a][:], S["var"][a], s, S["sq"][a], S["ln"][a])

            def u_product(s, h):
                if s.real:
                    wait(pe, S["hi"][0], s.n + 1)
                    wait(pe, S["lo"][0], s.n + 1)
                    r = s.slot(2)
                    for b in range(2):
                        free_m(b)
                        for k, (w, m) in enumerate(((0, 0), (0, 1), (1, 0))):
                            ins = mm(ps_m[0:R, b, 0:HALF], gram[w][:, h, :],
                                     xm[0][m][:, r, HALF * b:HALF * b + HALF], start=(k == 0), stop=(k == 2))
                        ins.then_inc(S["uu"], 1)
                        last[b] = (S["u_lo"], 6 * s.n + 2 * h + b + 1)

            def scores_q(s, j):
                if s.real:
                    q = 4 * s.n + j
                    if j == 0:
                        wait(pe, S["u_hi"], 6 * s.n + 6)
                        wait(pe, S["hi"][0], s.n + 1)
                    wait(pe, S["mx"], q)
                    r = s.slot(2)
                    for b in range(2):
                        mm(ps_s[0:R, b, 0:2 * HQ], pick_q,
                           bias[:, 0, :].unsqueeze(1).to_broadcast([R, 2, HQ]), start=True, stop=False)
                        for k in range(2):
                            w = QP * j + 2 * b + k
                            for h in range(HEADS):
                                for g in range(2):
                                    lo = ROWB * g
                                    at = HQ * k + TOK * h
                                    ins = mm(ps_s[lo:lo + TOK, b, at:at + TOK],
                                             U[0][lo:lo + C + 1, r, h, TOK * w:TOK * w + TOK],
                                             xm[0][0][lo:lo + C + 1, r, TOK * w:TOK * w + TOK],
                                             start=False, stop=(k == 1 and h == HEADS - 1))
                    ins.then_inc(S["s_q"], 1)

            def scores_k(s, j):
                q = 4 * s.n + j
                if j == 0:
                    wait(pe, S["u_lo"], 6 * s.n + 6)
                    wait(pe, S["xs_copied"], 4 * s.n + 4)
                wait(pe, S["ex"], q)
                r = s.slot(2)
                for b in range(2):
                    mm(ps_t[0:KEYS, b, 0:2 * HQ], pick_k,
                       bias[:, 1, :].unsqueeze(1).to_broadcast([R, 2, HQ]), start=True, stop=False)
                    for k in range(2):
                        w = QP * j + 2 * b + k
                        for ws, ms in ((0, 0), (0, 1), (1, 0)):
                            mm(ps_t[0:KEYS, b, HQ * k:HQ * k + HQ], xs[ws][:, r, w, :],
                               U[ms][:, r, :, TOK * w:TOK * w + TOK], start=False, stop=False)
                wait(pe, S["md"], q + 1)
                for b in range(2):
                    ins = mm(ps_t[0:KEYS, b, 0:2 * HQ], group_ones,
                             shift[:, j % 2, 2 * HEADS * b:2 * HEADS * (b + 1), :], start=False, stop=True)
                ins.then_inc(S["st_q"], 1)

            def values(s, j):
                q = 4 * s.n + j
                wait(pe, S["vev"], q)
                r = s.slot(2)
                for k in range(QP):
                    for n, (ws, ms) in enumerate(((0, 0), (1, 0), (0, 1))):
                        ins = mm(ps_v[0:KEYS, 2 * C * k:2 * C * (k + 1)], xs[ws][:, r, QP * j + k, :], wv[ms][:],
                                 start=(n == 0), stop=(n == 2))
                ins.then_inc(S["v_q"], 1)

            def weigh(s, j):
                if s.real:
                    q = 4 * s.n + j
                    wait(pe, S["ex"], q + 1)
                    wait(pe, S["vev"], q + 1)
                    wait(pe, S["nrm"], q)
                    W = QP * TOK
                    for k in range(QP):
                        for h in range(HEADS):
                            lo = 2 * DH * h
                            mm(ps_o[lo:lo + 2 * DH, TOK * k:TOK * k + TOK], V[:, j % 2, k, lo:lo + 2 * DH],
                               P[:, j % 2, k, h, :], start=True, stop=True)
                    for h in range(HEADS):
                        lo = 2 * DH * h
                        ins = mm(ps_o[lo:lo + 2 * DH, W:2 * W], key_ones[:], P[:, j % 2, :, h, :],
                                 start=True, stop=True)
                    ins.then_inc(S["pv_q"], 1)

            def project(s):
                if s.real:
                    wait(pe, S["nrm"], 4 * s.n + 4)
                    per_strip(proj_w[:], O[:, s.slot(2), :], S["proj"], s, None, S["x1_made"])

            def fc1(s, t):
                if s.real:
                    if t == 0:
                        wait(pe, S["hi"][1], s.n + 1)
                        wait(pe, S["lo"][1], s.n + 1)
                    r = s.slot(2)
                    for b in range(2):
                        free_m(b)
                        for k, (w, m) in enumerate(((0, 0), (0, 1), (1, 0))):
                            if t < 2:
                                lo = ROWB * b
                                ins = mm(ps_m[:, b, 0:HALF], w1_own[w][lo:lo + C + 1, :],
                                         xm[1][m][lo:lo + C + 1, r, HALF * t:HALF * t + HALF],
                                         start=(k == 0), stop=(k == 2))
                            else:
                                ins = mm(ps_m[:, b, 0:HALF], w1_both[w][:],
                                         xm[1][m][:, r, HALF * b:HALF * b + HALF],
                                         start=(k == 0), stop=(k == 2))
                        ins.then_inc(S["f1"], 1)
                        last[b] = (S["ge"], 6 * s.n + 2 * t + b + 1)

            def fc2(s):
                if s.real:
                    wait(pe, S["ge"], 6 * s.n + 6)
                    r = s.slot(2)
                    for b in range(2):
                        free_m(b)
                        cols = slice(HALF * b, HALF * b + HALF)
                        mm(ps_m[0:ROWB + C, b, 0:HALF], w2_both[:], G[:, r, 2, cols], start=True, stop=False)
                        for g in range(2):
                            lo = ROWB * g
                            ins = mm(ps_m[lo:lo + C, b, 0:HALF], w2_own[:], G[:, r, g, cols],
                                     start=False, stop=True)
                        ins.then_inc(S["f2"], 1)
                        last[b] = (S["x2_made"], 2 * s.n + b + 1)

            def step(s):
                nxt, prv = s.at(1), s.at(-1)
                old = s.at(-2)
                if old.real:
                    for b in range(2):
                        last[b] = (S["ge"], 6 * old.n + 2 + b + 1)
                if s.real:
                    scores_k(s, 0)
                fc1(old, 2)
                if s.real:
                    scores_q(s, 1)
                centre(0, nxt)
                if s.real:
                    values(s, 0)
                weigh(prv, 3)
                fc2(old)
                variance(0, nxt)
                if s.real:
                    scores_k(s, 1)
                project(prv)
                if s.real:
                    scores_q(s, 2)
                    values(s, 1)
                centre(1, prv)
                if s.real:
                    weigh(s, 0)
                u_product(nxt, 0)
                if s.real:
                    scores_k(s, 2)
                    scores_q(s, 3)
                variance(1, prv)
                if s.real:
                    values(s, 2)
                u_product(nxt, 1)
                if s.real:
                    weigh(s, 1)
                u_product(nxt, 2)
                if s.real:
                    scores_k(s, 3)
                    weigh(s, 2)
                fc1(prv, 0)
                scores_q(nxt, 0)
                if s.real:
                    values(s, 3)
                fc1(prv, 1)

            steps(pe, step, -1, N + 2)


def convolution_phase(nc, dw_w, bands, x2_dram, y_dram, images):
    with ExitStack() as ctx:
        def sb(name, shape, dt=F32):
            return ctx.enter_context(nc.sbuf_tensor(name, shape, dt))

        def sem(name):
            return ctx.enter_context(nc.semaphore(name))

        PIECES = 3
        ROWS = 32 * (PIECES - 1) + WS
        THIRDS = 3
        GROUP = C * WS // THIRDS
        PER = 4
        FILLS = THIRDS * IMG // PER
        half = images // 2
        back = IMG - SHIFT

        ps = [ctx.enter_context(nc.psum_tensor(f"conv_ps{r}", [128, 2, 512], F32)) for r in range(4)]
        hot = sb("hot", [ROWS, IMG, IMG], BF16)
        taps = sb("taps", [ROWS, C * WS])
        rest = sb("rest", [ROWS, C * WS])
        piece = [sb(f"piece{k}", [ROWS, C * WS], BF16) for k in range(PIECES)]
        split = sb("split", [ROWS, C * WS], BF16)
        band = [sb(f"band_{p}", [IMG, C * WS, IMG], BF16) for p in "hl"]
        xin = sb("xin", [IMG, 2, images, IMG])
        xp = [sb(f"xp_{p}", [IMG, 2, images, PAD], BF16) for p in "hl"]
        y = sb("y", [IMG, 2, images, IMG])

        taps_loaded = sem("taps_loaded")
        conv_cleared = sem("conv_cleared")
        split_made = sem("split_made")
        band_filled = sem("band_filled")
        band_high = sem("band_high")
        band_low = sem("band_low")
        xin_loaded = [sem(f"xin_loaded{r}") for r in range(2)]
        xp_high = sem("xp_high")
        xp_low = sem("xp_low")
        convolved = sem("convolved")
        y_made = sem("y_made")
        y_stored = [sem(f"y_stored{r}") for r in range(2)]
        block = ctx.enter_context(nc.Block())

        def channels(eng, step):
            for c in range(4):
                step(c, c % 2, c // 2)
            with eng.Fori(2, C // 2) as i:
                for r in range(2):
                    step(2 * i + r, r, i)

        def runs(r, padded, rolled):
            return ((padded[:, r, :, 2 * SHIFT:2 * SHIFT + back], rolled[:, r, :, 0:back]),
                    (padded[:, r, :, SHIFT:2 * SHIFT], rolled[:, r, :, back:IMG]))

        @block.sync
        def _(sp):
            sp.wait_ge(conv_cleared, 4)
            for k in range(PIECES):
                sp.dma_start(hot[32 * k:32 * k + WS], bands.bitcast(BF16)).then_inc(taps_loaded, 16)
                sp.dma_start(taps[32 * k:32 * k + WS, :].rearrange("p (c b) -> p c b", b=WS),
                             dw_w.rearrange("c o a b -> a (c o) b")).then_inc(taps_loaded, 16)

            def load(c, r, turn):
                wait(sp, xp_low, 2 * c - 2)
                sp.dma_start(xin[:, r], x2_dram[:, c].rearrange("b (h w) -> h b w", h=IMG)
                             ).then_inc(xin_loaded[r], 16)

            channels(sp, load)

        @block.gpsimd
        def _(pool):
            nc.gpsimd.memset(hot[:], 0.0).then_inc(conv_cleared, 1)
            nc.gpsimd.memset(taps[:], 0.0).then_inc(conv_cleared, 1)
            for p in range(2):
                nc.gpsimd.memset(xp[p][:], 0.0).then_inc(conv_cleared, 1)

            def store(c, r, turn):
                wait(pool, y_made, 2 * c + 2)
                pool.dma_start(y_dram[:, c].rearrange("b (h w) -> h b w", h=IMG), y[:, r]
                               ).then_inc(y_stored[r], 16)

            channels(pool, store)
            for r in range(2):
                pool.wait_ge(y_stored[r], 16 * (C // 2))

        @block.vector
        def _(dve):
            dve.wait_ge(taps_loaded, 32 * PIECES)
            k = 0
            for n in range(PIECES):
                src = taps if n == 0 else rest
                nc.vector.tensor_copy(piece[n][:], src[:]).then_inc(split_made, 1)
                k += 1
                dve.wait_ge(split_made, k)
                if n < PIECES - 1:
                    nc.vector.tensor_tensor(rest[:], src[:], piece[n][:], ALU.subtract).then_inc(split_made, 1)
                    k += 1
                    dve.wait_ge(split_made, k)
            for n in range(PIECES):
                lo, hi = 32 * n, min(32 * n + 32, ROWS)
                nc.vector.tensor_copy(split[lo:hi], piece[n][lo:hi]).then_inc(split_made, 1)
            for f in range(FILLS):
                dve.wait_ge(band_high, f + 1)
                at = band[0][:, GROUP * (f % THIRDS):GROUP * (f % THIRDS + 1), PER * (f // THIRDS):PER * (f // THIRDS + 1)]
                al = band[1][:, GROUP * (f % THIRDS):GROUP * (f % THIRDS + 1), PER * (f // THIRDS):PER * (f // THIRDS + 1)]
                nc.vector.tensor_tensor(al.rearrange("i k o -> i o k"),
                                        ps[f // 2 % 4][0:IMG, f % 2, 0:PER * GROUP].rearrange("i (o k) -> i o k", o=PER),
                                        at.rearrange("i k o -> i o k"), ALU.subtract).then_inc(band_low, 1)

            def low(c, r, turn):
                wait(dve, xp_high, 2 * c + 2)
                wait(dve, convolved, c - 1)
                for k, (dst, src) in enumerate(runs(r, xp[1], xin)):
                    nc.vector.tensor_tensor(dst, src, runs(r, xp[0], xin)[k][0], ALU.subtract).then_inc(xp_low, 1)

            channels(dve, low)

        @block.scalar
        def _(act):
            for f in range(FILLS):
                act.wait_ge(band_filled, f + 1)
                at = band[0][:, GROUP * (f % THIRDS):GROUP * (f % THIRDS + 1), PER * (f // THIRDS):PER * (f // THIRDS + 1)]
                nc.scalar.copy(at.rearrange("i k o -> i o k"),
                               ps[f // 2 % 4][0:IMG, f % 2, 0:PER * GROUP].rearrange("i (o k) -> i o k", o=PER)
                               ).then_inc(band_high, 1)

            def high(c, r, turn):
                wait(act, xin_loaded[r], 16 * (turn + 1))
                wait(act, convolved, c - 1)
                for dst, src in runs(r, xp[0], xin):
                    nc.scalar.copy(dst, src).then_inc(xp_high, 1)

            def keep(c, r, turn):
                wait(act, convolved, c + 1)
                wait(act, y_stored[r], 16 * turn)
                full = ps[r][0:IMG, :, 0:half * IMG].rearrange("h k (b w) -> h k b w", w=IMG)
                out = y[:, r].rearrange("h (k b) w -> h k b w", k=2)
                nc.scalar.copy(out[:, :, :, 0:back], full[:, :, :, SHIFT:IMG]).then_inc(y_made, 1)
                nc.scalar.copy(out[:, :, :, back:IMG], full[:, :, :, 0:SHIFT]).then_inc(y_made, 1)

            high(0, 0, 0)
            high(1, 1, 0)
            keep(0, 0, 0)

            def two(i):
                high(2 * i, 0, i)
                keep(2 * i - 1, 1, i - 1)
                high(2 * i + 1, 1, i)
                keep(2 * i, 0, i)

            two(1)
            with act.Fori(2, C // 2) as i:
                two(i)
            keep(C - 1, 1, C // 2 - 1)

        @block.tensor
        def _(pe):
            mm = nc.tensor.matmul
            pe.wait_ge(split_made, 8)
            for f in range(FILLS):
                wait(pe, band_low, f - 7)
                for o in range(PER):
                    ins = mm(ps[f // 2 % 4][0:IMG, f % 2, GROUP * o:GROUP * (o + 1)],
                             hot[:, PER * (f // THIRDS) + o, :],
                             split[:, GROUP * (f % THIRDS):GROUP * (f % THIRDS + 1)], start=True, stop=True)
                ins.then_inc(band_filled, 1)
            pe.wait_ge(band_low, FILLS)

            def convolve(c, r, turn):
                wait(pe, xp_low, 2 * c + 2)
                wait(pe, y_made, 2 * c - 2)
                parts = ((0, 0), (0, 1), (1, 0))
                for dx in range(WS):
                    for n, (w, m) in enumerate(parts):
                        for k in range(2):
                            ins = mm(ps[r][0:IMG, k, 0:half * IMG], band[w][:, c * WS + dx, :],
                                     xp[m][:, r, half * k:half * (k + 1), dx:dx + IMG],
                                     start=(dx == 0 and n == 0), stop=(dx == WS - 1 and n == 2))
                ins.then_inc(convolved, 1)

            channels(pe, convolve)


def response_phase(nc, prm, con, x2_dram, y_dram, out_dram, strips):
    with ExitStack() as ctx:
        def sb(name, shape, dt=F32):
            return ctx.enter_context(nc.sbuf_tensor(name, shape, dt))

        def sem(name):
            return ctx.enter_context(nc.semaphore(name))

        N = strips
        RING = 2 * STRIPS
        LAG = STRIPS + 1
        by_strip = [t.rearrange("b c (g s n) -> b s g c n", g=2, s=STRIPS) for t in (y_dram, x2_dram, out_dram)]

        ps_m = ctx.enter_context(nc.psum_tensor("r_ps_m", [128, 2, 512], F32))
        ps_f = [ctx.enter_context(nc.psum_tensor(f"r_ps_f{r}", [128, 2, 512], F32)) for r in range(2)]
        ps_o = ctx.enter_context(nc.psum_tensor("r_ps_o", [128, 2, 512], F32))

        center = sb("r_center", [R, R])
        spread = sb("r_spread", [R, R])
        eye_c = sb("r_eye_c", [C, C + 1])
        last_row = sb("r_last_row", [1, C + 1])
        eye = sb("r_eye", [128, 128])
        twins = sb("r_twins", [128, 128])
        mean_all = sb("r_mean_all", [128, 128])
        mean_top = sb("r_mean_top", [128, 128])
        w1 = sb("r_w1", [128, 2, C])
        w1t = sb("r_w1t", [C, HID])
        w2 = sb("r_w2", [C, 2 * F1])
        rows = sb("r_rows", [1, HID])
        norm = sb("r_norm", [C, 2])
        aug = sb("r_aug", [C, C + 1])
        dw_b = sb("r_dw_b", [R, 1])
        shift_c = sb("r_shift_c", [R, 1])
        w1_own = [sb(f"r_w1_own_{p}", [R, F1], BF16) for p in "hl"]
        w1_both = [sb(f"r_w1_both_{p}", [R, 2 * F2], BF16) for p in "hl"]
        w2_own = sb("r_w2_own", [F1, C])
        w2_both = sb("r_w2_both", [2 * F2, ROWB + C])
        w2s_own = sb("r_w2s_own", [F1, 2, C])
        w2s_both = sb("r_w2s_both", [2 * F2, 2, ROWB + C])
        grn_g = sb("r_grn_g", [128, 2])
        grn_b = sb("r_grn_b", [128, 2])
        out_b = sb("r_out_b", [ROWB + C, 1])
        b2 = sb("r_b2", [ROWB + C, 1])
        eps = sb("r_eps", [R, 1])

        Y = sb("r_Y", [R, 2, STRIP])
        X2 = sb("r_X2", [ROWB + C, 2, STRIP])
        OUT = sb("r_OUT", [ROWB + C, 2, STRIP])
        xc = sb("r_xc", [R, STRIP])
        sq = sb("r_sq", [R, STRIP])
        lnv = sb("r_lnv", [R, STRIP])
        rs = sb("r_rs", [R, STRIP])
        xh = sb("r_xh", [R, STRIP])
        xm = [sb(f"r_xm_{p}", [R, 2, STRIP], BF16) for p in "hl"]
        G = sb("r_G", [128, RING, 3, STRIP])
        junk = sb("r_junk", [128, STRIP])
        sums = sb("r_sums", [128, 3, RING])
        total = sb("r_total", [128, 3])
        both = sb("r_both", [128, 2])
        gx = sb("r_gx", [128, 2])
        mean = sb("r_mean", [128, 1])
        inv = sb("r_inv", [128, 1])
        scale = sb("r_scale", [128, 2])

        def sems(text):
            return {nm: sem("r_" + nm) for nm in text.split()}

        S = sems("loaded cleared setup_v setup_t cen var f1 f2 pairs mean_ps xc xh hi summed totals both_made "
                 "gx_made inv_made scaled w2_scaled out_made sq ln rs ge lo")
        y_loaded = [sem(f"r_y_loaded{r}") for r in range(2)]
        x2_loaded = [sem(f"r_x2_loaded{r}") for r in range(2)]
        stored = [sem(f"r_stored{r}") for r in range(2)]
        block = ctx.enter_context(nc.Block())

        loads = [
            (center[:], con["center"]), (spread[:], con["spread1"]), (eye_c[:], con["eye_c"]),
            (last_row[:], con["last_row"]), (eye[:], con["eye"]), (twins[:], con["twins"]),
            (mean_all[:], con["mean_all"]), (mean_top[:], con["mean_top"]),
            (w1[:, 0, :], prm["w1"][0:F1, :]), (w1[0:F2, 1, :], prm["w1"][F1:HID, :]),
            (w2[:, 0:HID], prm["w2"]), (w2[:, HID:], prm["w2"][:, F1:HID]),
            (rows[:], prm["b1"].unsqueeze(0)), (norm[:, 0:1], prm["ln_g"].unsqueeze(1)),
            (norm[:, 1:2], prm["ln_b"].unsqueeze(1)),
        ]
        for t, nm in ((grn_g, "grn_g"), (grn_b, "grn_b")):
            loads += [(t[0:F1, 0:1], prm[nm][0:F1].unsqueeze(1)), (t[0:F2, 1:2], prm[nm][F1:HID].unsqueeze(1)),
                      (t[F2:2 * F2, 1:2], prm[nm][F1:HID].unsqueeze(1))]
        for g in range(2):
            loads += [(dw_b[ROWB * g:ROWB * g + C, :], prm["dw_b"].unsqueeze(1)),
                      (b2[ROWB * g:ROWB * g + C, :], prm["b2"].unsqueeze(1))]
        CLEARS = 11
        SETUP_V = 17

        def halves(ap):
            return ap.rearrange("p (b n) -> p b n", b=2)

        def steps(eng, step, last):
            turns = max((N - RING - 2) // RING, 0)
            for raw in range(-2, RING):
                step(Strip(0, raw, N))
            if turns:
                with eng.Fori(0, turns) as i:
                    for u in range(RING):
                        step(Strip(RING // 4 * i, RING + u, N))
            for raw in range(RING + RING * turns, last):
                step(Strip(0, raw, N))

        @block.sync
        def _(sp):
            sp.wait_ge(S["cleared"], CLEARS)
            for dst, src in loads:
                sp.dma_start(dst, src).then_inc(S["loaded"], 16)

            def step(s):
                nxt, old = s.at(2), s.at(-LAG)
                if nxt.real:
                    wait(sp, S["cen"], nxt.n - 1)
                    for g in range(2):
                        sp.dma_start(Y[ROWB * g:ROWB * g + C, nxt.slot(2), :],
                                     by_strip[0][nxt.n // STRIPS, nxt.n % STRIPS, g]
                                     ).then_inc(y_loaded[nxt.slot(2)], 16)
                if old.real:
                    wait(sp, S["out_made"], old.n - 1)
                    for g in range(2):
                        sp.dma_start(X2[ROWB * g:ROWB * g + C, old.slot(2), :],
                                     by_strip[1][old.n // STRIPS, old.n % STRIPS, g]
                                     ).then_inc(x2_loaded[old.slot(2)], 16)

            steps(sp, step, N + LAG)

        @block.gpsimd
        def _(pool):
            for t in (*w1_own, *w1_both, w2_both, dw_b, b2, out_b, X2):
                nc.gpsimd.memset(t[:], 0.0).then_inc(S["cleared"], 1)
            nc.gpsimd.memset(eps[:], EPS1).then_inc(S["cleared"], 1)
            nc.gpsimd.memset(Y[:], 1.0).then_inc(S["cleared"], 1)

            def step(s):
                nxt, old = s.at(2), s.at(-LAG)
                if nxt.real:
                    wait(pool, S["hi"], nxt.n + 1)
                    wait(pool, S["f1"], 3 * (nxt.n - 1))
                    nc.gpsimd.tensor_tensor(xm[1][:, nxt.slot(2), :], xh[:], xm[0][:, nxt.slot(2), :],
                                            ALU.subtract).then_inc(S["lo"], 1)
                if old.real:
                    wait(pool, S["out_made"], old.n + 1)
                    for g in range(2):
                        pool.dma_start(by_strip[2][old.n // STRIPS, old.n % STRIPS, g],
                                       OUT[ROWB * g:ROWB * g + C, old.slot(2), :]
                                       ).then_inc(stored[old.slot(2)], 16)

            steps(pool, step, N + LAG)
            for r in range(2):
                pool.wait_ge(stored[r], 32 * (N // 2))

        @block.vector
        def _(dve):
            chain = [0]

            def link(ins):
                chain[0] += 1
                ins.then_inc(S["setup_v"], 1)
                return chain[0]

            dve.wait_ge(S["cleared"], CLEARS)
            dve.wait_ge(S["loaded"], 16 * len(loads))
            link(nc.vector.tensor_scalar(aug[:, 0:C], eye_c[:, 0:C], norm[:, 0:1], None, ALU.mult))
            link(nc.vector.tensor_copy(aug[:, C:C + 1], norm[:, 1:2]))
            dve.wait_ge(S["setup_t"], 1)
            link(nc.vector.tensor_copy(w1t[:], ps_f[0][0:C, 0, 0:HID]))
            link(nc.vector.tensor_copy(w2_own[:], ps_f[0][:, 1, 0:C]))
            for g in range(2):
                at = F2 * g
                link(nc.vector.tensor_copy(w2_both[at:at + F2, ROWB * g:ROWB * g + C],
                                           ps_f[0][at:at + F2, 1, C:2 * C]))
            dve.wait_ge(S["setup_t"], 2)
            link(nc.vector.tensor_copy(shift_c[:], ps_m[0:R, 0, 0:1]))
            link(nc.vector.tensor_tensor(out_b[0:C, :], ps_m[0:C, 1, 0:1], b2[0:C, :], ALU.add))
            link(nc.vector.tensor_tensor(out_b[ROWB:ROWB + C, :], ps_m[ROWB:ROWB + C, 1, 0:1], b2[ROWB:ROWB + C, :], ALU.add))
            for g in range(2):
                lo = ROWB * g
                for pair_, view, src in (
                        (w1_own, lambda t: t[lo:lo + C + 1, :], ps_f[1][lo:lo + C + 1, 0, 0:F1]),
                        (w1_both, lambda t: t[lo:lo + C + 1, F2 * g:F2 * g + F2], ps_f[1][lo:lo + C + 1, 0, F1:HID])):
                    k = link(nc.vector.tensor_copy(view(pair_[0]), src))
                    dve.wait_ge(S["setup_v"], k)
                    k = link(nc.vector.tensor_tensor(view(pair_[1]), src, view(pair_[0]), ALU.subtract))

            def copy_centered(s):
                if s.real:
                    wait(dve, S["cen"], s.n + 1)
                    nc.vector.tensor_scalar(halves(xc[:]), ps_m[0:R, :, 0:HALF], shift_c[:, 0:1], None,
                                            ALU.add).then_inc(S["xc"], 1)

            def normalise(s):
                if s.real:
                    wait(dve, S["rs"], s.n + 1)
                    wait(dve, S["lo"], s.n)
                    nc.vector.tensor_tensor(xh[:], xc[:], rs[:], ALU.mult).then_inc(S["xh"], 1)
                    wait(dve, S["xh"], s.n + 1)
                    wait(dve, S["f1"], 3 * (s.n - 1))
                    nc.vector.tensor_copy(xm[0][:, s.slot(2), :], xh[:]).then_inc(S["hi"], 1)

            def sum_squares(s, t):
                if s.real:
                    wait(dve, S["ge"], 3 * s.n + (2 if t < 2 else 3))
                    g = G[:, s.raw % RING, t, :]
                    wait(dve, S["summed"], 3 * s.n + t)
                    nc.vector.tensor_tensor_reduce(out=junk[:], in0=g, in1=g, scale=1.0, scalar=0.0, op0=ALU.mult,
                                                   op1=ALU.add, accum_out=sums[:, t, s.raw % RING:s.raw % RING + 1]
                                                   ).then_inc(S["summed"], 1)

            def respond(s):
                if s.real and s.raw % STRIPS == 0:
                    m = s.raw // STRIPS if isinstance(s.i, int) else None
                    img = s.i // 2 + s.raw // STRIPS if m is None else m
                    p = s.raw // STRIPS % 2
                    wait(dve, S["summed"], 3 * (s.n + STRIPS))
                    nc.vector.tensor_reduce(total[:], sums[:, :, STRIPS * p:STRIPS * (p + 1)], AX_X, ALU.add).then_inc(S["totals"], 1)
                    wait(dve, S["totals"], 2 * img + 1)
                    nc.vector.tensor_tensor(total[:, 0:1], total[:, 0:1], total[:, 1:2], ALU.add).then_inc(S["totals"], 1)
                    wait(dve, S["mean_ps"], img + 1)
                    nc.vector.tensor_scalar(mean[:], ps_o[:, 0, HALF + 2:HALF + 3], EPS1, None, ALU.add).then_inc(S["inv_made"], 1)
                    wait(dve, S["inv_made"], 2 * img + 1)
                    nc.vector.reciprocal(inv[:], mean[:]).then_inc(S["inv_made"], 1)
                    wait(dve, S["inv_made"], 2 * img + 2)
                    nc.vector.scalar_tensor_tensor(out=scale[:], in0=gx[:], scalar=inv[:, 0:1], in1=grn_g[:],
                                                   op0=ALU.mult, op1=ALU.mult).then_inc(S["scaled"], 1)
                    wait(dve, S["scaled"], 2 * img + 1)
                    nc.vector.tensor_scalar(scale[:], scale[:], 1.0, None, ALU.add).then_inc(S["scaled"], 1)
                    wait(dve, S["scaled"], 2 * img + 2)
                    nc.vector.tensor_scalar(w2s_own[:, p, :], w2_own[:], scale[:, 0:1], None, ALU.mult
                                            ).then_inc(S["w2_scaled"], 1)
                    nc.vector.tensor_scalar(w2s_both[:, p, :], w2_both[:], scale[:, 1:2], None, ALU.mult
                                            ).then_inc(S["w2_scaled"], 1)

            def finish(s):
                if s.real:
                    wait(dve, S["f2"], s.n + 1)
                    wait(dve, x2_loaded[s.slot(2)], 32 * (s.turn(2) + 1))
                    wait(dve, stored[s.slot(2)], 32 * s.turn(2))
                    n = ROWB + C
                    nc.vector.scalar_tensor_tensor(
                        out=halves(OUT[:, s.slot(2), :]), in0=ps_o[0:n, :, 0:HALF], scalar=out_b[:, 0:1],
                        in1=halves(X2[:, s.slot(2), :]), op0=ALU.add, op1=ALU.add).then_inc(S["out_made"], 1)

            def step(s):
                nxt, old = s.at(2), s.at(-LAG)
                copy_centered(nxt)
                respond(old)
                sum_squares(s.at(-1), 2)
                sum_squares(s, 0)
                sum_squares(s, 1)
                normalise(nxt)
                finish(old)

            steps(dve, step, N + LAG)

        @block.scalar
        def _(act):
            act.wait_ge(S["cleared"], CLEARS)

            def features(s, t):
                if s.real:
                    wait(act, S["f1"], 3 * s.n + t + 1)
                    if t == 0:
                        wait(act, S["f2"], s.n - RING + 1)
                        wait(act, S["summed"], 3 * (s.n - RING + 1))
                    src = ps_f[(s.raw + t) % 2][:, :, 0:HALF]
                    slot = s.raw % RING
                    out = G[:, slot, 0:2, HALF * t:HALF * t + HALF] if t < 2 else halves(G[:, slot, 2, :])
                    nc.scalar.activation(out, src, ACT.Gelu).then_inc(S["ge"], 1)

            def step(s):
                nxt, old = s.at(2), s.at(-LAG)
                if old.real and old.raw % STRIPS == 0:
                    img = old.raw // STRIPS if isinstance(old.i, int) else old.i // 2 + old.raw // STRIPS
                    wait(act, S["pairs"], img + 1)
                    nc.scalar.activation(gx[:], ps_o[:, 0, HALF:HALF + 2], ACT.Sqrt).then_inc(S["gx_made"], 1)
                features(s.at(-1), 2)
                if nxt.real:
                    wait(act, S["xc"], nxt.n + 1)
                    nc.scalar.activation(sq[:], xc[:], ACT.Square).then_inc(S["sq"], 1)
                features(s, 0)
                features(s, 1)
                if nxt.real:
                    nc.scalar.preload_act_table_set("natural_log_exp_and_others")
                    wait(act, S["var"], nxt.n + 1)
                    nc.scalar.activation(halves(lnv[:]), ps_m[0:R, :, 0:HALF], ACT.Ln, bias=eps[:, 0:1]
                                         ).then_inc(S["ln"], 1)
                    wait(act, S["ln"], nxt.n + 1)
                    nc.scalar.activation(rs[:], lnv[:], ACT.Exp, scale=-0.5).then_inc(S["rs"], 1)

            steps(act, step, N + LAG)

        @block.tensor
        def _(pe):
            mm = nc.tensor.matmul
            pe.wait_ge(S["loaded"], 16 * len(loads))
            nc.tensor.transpose(ps_f[0][0:C, 0, 0:F1], w1[:, 0, :], eye[:])
            nc.tensor.transpose(ps_f[0][0:C, 0, F1:HID], w1[0:F2, 1, :], eye[0:F2, 0:F2])
            nc.tensor.transpose(ps_f[0][:, 1, 0:C], w2[:, 0:F1], eye[0:C, 0:C])
            nc.tensor.transpose(ps_f[0][:, 1, C:2 * C], w2[:, F1:2 * F1], eye[0:C, 0:C]).then_inc(S["setup_t"], 1)
            pe.wait_ge(S["setup_v"], 6)
            mm(ps_m[0:R, 0, 0:1], center[:], dw_b[:], start=True, stop=True)
            for g in range(2):
                lo = ROWB * g
                out = ps_m[lo:lo + C, 1, 0:1]
                mm(out, w2_own[:], grn_b[:, 0:1], start=True, stop=False)
                mm(out, w2_both[0:F2, 0:C], grn_b[0:F2, 1:2], start=False, stop=True)
                out = ps_f[1][lo:lo + C + 1, 0, 0:HID]
                mm(out, aug[:], w1t[:], start=True, stop=False)
                ins = mm(out, last_row[:], rows[:], start=False, stop=True)
            ins.then_inc(S["setup_t"], 1)
            pe.wait_ge(S["setup_v"], SETUP_V)

            def centre(s):
                if s.real:
                    wait(pe, y_loaded[s.slot(2)], 32 * (s.turn(2) + 1))
                    wait(pe, S["ln"], s.n)
                    for b in range(2):
                        ins = mm(ps_m[0:R, b, 0:HALF], center[:], Y[:, s.slot(2), HALF * b:HALF * b + HALF],
                                 start=True, stop=True)
                    ins.then_inc(S["cen"], 1)

            def variance(s):
                if s.real:
                    wait(pe, S["sq"], s.n + 1)
                    for b in range(2):
                        ins = mm(ps_m[0:R, b, 0:HALF], spread[:], sq[:, HALF * b:HALF * b + HALF],
                                 start=True, stop=True)
                    ins.then_inc(S["var"], 1)

            def fc1(s, t):
                if s.real:
                    if t == 0:
                        wait(pe, S["hi"], s.n + 1)
                        wait(pe, S["lo"], s.n + 1)
                    wait(pe, S["ge"], 3 * s.n + t - 1)
                    r = s.slot(2)
                    ps = ps_f[(s.raw + t) % 2]
                    for k, (w, m) in enumerate(((0, 0), (0, 1), (1, 0))):
                        for b in range(2):
                            if t < 2:
                                lo = ROWB * b
                                ins = mm(ps[:, b, 0:HALF], w1_own[w][lo:lo + C + 1, :],
                                         xm[m][lo:lo + C + 1, r, HALF * t:HALF * t + HALF],
                                         start=(k == 0), stop=(k == 2))
                            else:
                                ins = mm(ps[:, b, 0:HALF], w1_both[w][:], xm[m][:, r, HALF * b:HALF * b + HALF],
                                         start=(k == 0), stop=(k == 2))
                    ins.then_inc(S["f1"], 1)

            def respond(s, part):
                if s.real and s.raw % STRIPS == 0:
                    img = s.raw // STRIPS if isinstance(s.i, int) else s.i // 2 + s.raw // STRIPS
                    if part == 0:
                        wait(pe, S["totals"], 2 * img + 2)
                        mm(ps_o[:, 0, HALF:HALF + 1], eye[:], total[:, 0:1], start=True, stop=True)
                        mm(ps_o[:, 0, HALF + 1:HALF + 2], twins[:], total[:, 2:3], start=True, stop=True
                           ).then_inc(S["pairs"], 1)
                    elif part == 1:
                        wait(pe, S["gx_made"], img + 1)
                        mm(ps_o[:, 0, HALF + 2:HALF + 3], mean_all[:], gx[:, 0:1], start=True, stop=False)
                        mm(ps_o[:, 0, HALF + 2:HALF + 3], mean_top[:], gx[:, 1:2], start=False, stop=True
                           ).then_inc(S["mean_ps"], 1)
                    else:
                        wait(pe, S["w2_scaled"], 2 * img + 2)

            def fc2(s):
                if s.real:
                    p = s.raw // STRIPS % 2
                    slot = s.raw % RING
                    wait(pe, S["out_made"], s.n)
                    for b in range(2):
                        cols = slice(HALF * b, HALF * b + HALF)
                        mm(ps_o[0:ROWB + C, b, 0:HALF], w2s_both[:, p, :], G[:, slot, 2, cols], start=True, stop=False)
                        for g in range(2):
                            lo = ROWB * g
                            ins = mm(ps_o[lo:lo + C, b, 0:HALF], w2s_own[:, p, :], G[:, slot, g, cols],
                                     start=False, stop=True)
                    ins.then_inc(S["f2"], 1)

            def step(s):
                nxt, old = s.at(2), s.at(-LAG)
                centre(nxt)
                fc1(s, 0)
                respond(old, 0)
                fc1(s, 1)
                variance(nxt)
                respond(old, 1)
                fc1(s, 2)
                respond(old, 2)
                fc2(old)

            steps(pe, step, N + LAG)

def constants():
    import numpy as np

    f = np.float32
    out = {}
    center = np.zeros((R, R), f)
    spread = [np.zeros((R, R), f) for _ in range(2)]
    for g in range(2):
        lo = ROWB * g
        center[lo:lo + C, lo:lo + C] = np.eye(C) - 1.0 / C
        center[lo + C, lo + C] = 1.0
        for a, eps in ((0, EPS0), (1, EPS1)):
            spread[a][lo:lo + C, lo:lo + C] = 1.0 / C
            spread[a][lo + C, lo + C] = 1.0 - eps
    out["center"] = center
    out["spread0"], out["spread1"] = spread
    out["eye_c"] = np.eye(C, C + 1, dtype=f)
    out["last_row"] = np.eye(1, C + 1, C, dtype=f)
    pick_q, pick_k = np.zeros((R, R), f), np.zeros((R, KEYS), f)
    ones, minus = np.zeros((R, KEYS), f), np.zeros((R, TOK), f)
    for j in range(TOK):
        for lo in (0, ROWB):
            pick_q[lo + j, [j, ROWB + j]] = 1
            pick_k[lo + j, [j, TOK + j]] = 1
            minus[lo + j, j] = -1
    for g in range(2):
        ones[ROWB * g:ROWB * g + TOK, TOK * g:TOK * g + TOK] = 1
    out["picks"] = np.concatenate([pick_q, pick_k, ones, minus], 1)
    key_ones = np.zeros((KEYS, 2 * DH), f)
    for g in range(2):
        key_ones[TOK * g:TOK * g + TOK, DH * g:DH * g + DH] = 1
    out["key_ones"] = key_ones
    out["eye"] = np.eye(128, dtype=f)
    p = np.arange(128)
    out["twins"] = (p[:, None] % F2 == p[None, :] % F2).astype(f)
    out["mean_all"] = np.full((128, 128), 1.0 / HID, f)
    out["mean_top"] = np.where(p[:, None] < F2, f(1.0 / HID), f(0)) * np.ones((1, 128), f)
    true_row = (np.arange(IMG) + SHIFT) % IMG
    dy = true_row[None, :] - true_row[:, None] + SHIFT
    one = 0x3F80
    out["bands"] = ((dy[None] == np.arange(WS)[:, None, None]) * one).astype(np.uint16)
    return out


def windows_first(x):
    import numpy as np

    b = x.shape[0]
    x = np.roll(x, (-SHIFT, -SHIFT), axis=(2, 3))
    x = x.reshape(b, C, 2, STRIPS, WS, WINS, WS)
    return np.ascontiguousarray(x.transpose(0, 3, 2, 1, 5, 4, 6)).reshape(b * STRIPS, 2, C, STRIP)


def program(nc, x_in, prm, con, out_dram, images):
    scratch = {}
    for name, shape in (("x2_scratch", (images, C, PLANE)), ("y_scratch", (images, C, PLANE)),
                        ("table_0", (HEADS, REL)), ("table_1", (HEADS, REL)),
                        ("table_runs_0", (HEADS, TOK, RUN)), ("table_runs_1", (HEADS, TOK, RUN))):
        scratch[name] = nc.dram_tensor(name, shape, F32, kind="Internal").ap()
    layer0 = {k[8:]: v for k, v in prm.items() if k.startswith("L0_conv_")}
    layer1 = {k[8:]: v for k, v in prm.items() if k.startswith("L1_conv_")}
    attention_phase(nc, x_in, layer0, con, [scratch[f"table_{side}"] for side in range(2)],
                    [scratch[f"table_runs_{side}"] for side in range(2)], scratch["x2_scratch"], STRIPS * images)
    convolution_phase(nc, layer1["dw_w"], con["bands"], scratch["x2_scratch"], scratch["y_scratch"], images)
    response_phase(nc, layer1, con, scratch["x2_scratch"], scratch["y_scratch"], out_dram, STRIPS * images)


def kernel(**inputs):
    import numpy as np
    import concourse.bacc as bacc
    from concourse.bass_utils import run_bass_kernel_spmd

    nc = bacc.Bacc("TRN2", target_bir_lowering=False, num_devices=1)
    images = inputs["x"].shape[0]
    arrays, prm, con = {}, {}, {}

    def give(name, a):
        arrays[name] = a
        return nc.dram_tensor(name, a.shape, mybir.dt.from_np(a.dtype), kind="ExternalInput").ap()

    x_in = give("x_windows", windows_first(np.asarray(inputs["x"])))
    for name, a in inputs.items():
        if name != "x":
            prm[name] = give(name, np.ascontiguousarray(a))
    for name, a in constants().items():
        con[name] = give("const_" + name, a)
    out = nc.dram_tensor("out_rolled", (images, C, PLANE), F32, kind="ExternalOutput").ap()
    program(nc, x_in, prm, con, out, images)
    result = run_bass_kernel_spmd(nc, [arrays], core_ids=[0]).results[0]["out_rolled"]
    return np.roll(result.reshape(images, C, IMG, IMG), (SHIFT, SHIFT), axis=(2, 3))
```

```python
from contextlib import ExitStack

import concourse.bass as bass
from concourse import mybir

F32 = mybir.dt.float32
BF16 = mybir.dt.bfloat16
ALU = mybir.AluOpType
ACT = mybir.ActivationFunctionType
AX_X = mybir.AxisListType.X

C = 48
HID = 192
IMG = 112
WS = 7
TOK = WS * WS
HEADS = 3
DH = C // HEADS
SHIFT = WS // 2
PLANE = IMG * IMG
STRIP = WS * IMG
WINS = IMG // WS
STRIPS = IMG // WS // 2
HALF = STRIP // 2
QUADS = 4
QP = WINS // QUADS
HQ = HEADS * TOK
ROWB = 64
ONE = C
R = ROWB + C + 1
KEYS = 2 * TOK
F1 = 128
F2 = HID - F1
EPS0 = 1e-5
EPS1 = 1e-6
PAD = IMG + 2 * SHIFT
SPAN = 2 * WS - 1
REL = SPAN ** 2
RUN = SPAN * (WS - 1) + WS


def wait(eng, sem, value):
    if not isinstance(value, int) or value > 0:
        eng.wait_ge(sem, value)


class Strip:

    def __init__(self, i, raw, total):
        self.i, self.raw, self.total = i, raw, total

    def at(self, d):
        return Strip(self.i, self.raw + d, self.total)

    @property
    def n(self):
        return 4 * self.i + self.raw

    @property
    def real(self):
        return not isinstance(self.i, int) or 0 <= self.raw < self.total

    def slot(self, ring):
        return self.raw % ring

    def turn(self, ring):
        return (4 // ring) * self.i + self.raw // ring


def attention_phase(nc, x_in, prm, con, tables, table_runs, x2_dram, strips, later):
    with ExitStack() as ctx:
        def sb(name, shape, dt=F32):
            return ctx.enter_context(nc.sbuf_tensor(name, shape, dt))

        def sem(name):
            return ctx.enter_context(nc.semaphore(name))

        ps_s = ctx.enter_context(nc.psum_tensor("ps_s", [128, 2, 512], F32))
        ps_t = ctx.enter_context(nc.psum_tensor("ps_t", [128, 2, 512], F32))
        ps_v = ctx.enter_context(nc.psum_tensor("ps_v", [128, 512], F32))
        ps_o = ctx.enter_context(nc.psum_tensor("ps_o", [128, 512], F32))
        ps_m = ctx.enter_context(nc.psum_tensor("ps_m", [128, 2, 512], F32))

        center = sb("center", [R, R])
        sums_f = sb("sums_f", [R, 2, R])
        sum_w = sb("sum_w", [R, 2, R], BF16)
        eye_c = sb("eye_c", [C, C + 1])
        last_row = sb("last_row", [1, C + 1])
        const_f = sb("const_f", [R, R + KEYS + KEYS + TOK])
        const_b = sb("const_b", [R, R + KEYS + KEYS + TOK], BF16)
        pick_q = const_b[:, 0:R]
        pick_k = const_b[:, R:R + KEYS]
        group_ones = const_b[:, R + KEYS:R + 2 * KEYS]
        minus_eye = const_b[:, R + 2 * KEYS:R + 2 * KEYS + TOK]
        key_ones = sb("key_ones", [KEYS, 2 * DH])
        qkv_w = sb("qkv_w", [C, 3 * C])
        fc1_w = sb("fc1_w", [C, HID])
        rows = sb("rows", [1, 3 * C + HID])
        norms = sb("norms", [C, 4])
        aug = sb("aug", [C, 2, C + 1])
        qk_aug = sb("qk_aug", [DH, 2 * HEADS, C + 1])
        gram = [sb(f"gram_{p}", [R, HEADS, R], BF16) for p in "hl"]
        wv = [sb(f"wv_{p}", [R, 2 * C], BF16) for p in "hl"]
        w1_own = [sb(f"w1_own_{p}", [R, F1], BF16) for p in "hl"]
        w1_both = [sb(f"w1_both_{p}", [R, 2 * F2], BF16) for p in "hl"]
        proj_w = sb("proj_w", [2 * C, R])
        proj_b = sb("proj_b", [R, 1])
        fc2_b = sb("fc2_b", [R, 1])
        out_b = sb("out_b", [R, 1])
        centred_b = sb("centred_b", [R, 1])
        w2_own = sb("w2_own", [F1, C])
        w2_both = sb("w2_both", [2 * F2, ROWB + C])
        bias_f = sb("bias_f", [R, 2, HQ])
        bias = sb("bias", [R, 2, HQ], BF16)
        eps = sb("eps", [R, 1])
        xb = [sb(f"xb_{p}", [R, STRIP], BF16) for p in "hl"]
        x1b = [sb(f"x1b_{p}", [R, STRIP], BF16) for p in "hl"]
        sqb = [[sb(f"sqb{a}_{p}", [R, STRIP], BF16) for p in "hl"] for a in range(2)]

        X = sb("X", [R, 4, STRIP])
        x1 = sb("x1", [R, 2, STRIP])
        x2 = sb("x2", [R, 2, STRIP])
        xc = [sb(f"xc{a}", [R, STRIP]) for a in range(2)]
        sq = [sb(f"sq{a}", [R, STRIP]) for a in range(2)]
        lnv = [sb(f"lnv{a}", [R, STRIP]) for a in range(2)]
        rs = [sb(f"rs{a}", [R, STRIP]) for a in range(2)]
        xh = [sb(f"xh{a}", [R, STRIP]) for a in range(2)]
        xm = [[sb(f"xm{a}_{p}", [R, 2, STRIP], BF16) for p in "hl"] for a in range(2)]
        xs = [sb(f"xs_{p}", [R, 2, WINS, KEYS], BF16) for p in "hl"]
        U = [sb(f"u_{p}", [R, 2, HEADS, STRIP], BF16) for p in "hl"]
        qmax = sb("qmax", [R, 2, QP * HEADS])
        shift = sb("shift", [R, 2, QP * HEADS, TOK], BF16)
        P = sb("P", [KEYS, 2, QP, HEADS, TOK])
        V = sb("V", [KEYS, 2, QP, 2 * C])
        lden = sb("lden", [2 * C, QP * TOK])
        rden = sb("rden", [2 * C, 2, QP * TOK])
        O = sb("O", [2 * C, 2, STRIP])
        G = sb("G", [128, 2, 3, STRIP])

        loaded = sem("loaded")
        norm_loaded = sem("norm_loaded")
        sums_ready = sem("sums_ready")
        bias_loaded = sem("bias_loaded")
        x_cleared = sem("x_cleared")
        xs_cleared = sem("xs_cleared")
        table_turned = sem("table_turned")
        runs_made = sem("runs_made")
        setup_v = sem("setup_v")
        setup_t = sem("setup_t")
        cleared = sem("cleared")
        x_loaded = [sem(f"x_loaded{r}") for r in range(4)]
        x2_stored = [sem(f"x2_stored{r}") for r in range(2)]
        names = ("cen var uu s_q st_q v_q pv_q proj f1 f2 xc xh hi xs_copied u_lo mx nrm x1_made "
                 "x2_made sq ln rs u_hi ex vev lnd rdn ge lo md x_hi x_lo x1_hi x1_lo sq_hi sq_lo").split()
        pair = {"cen", "var", "xc", "xh", "hi", "sq", "ln", "rs", "lo", "sq_hi", "sq_lo"}
        S = {}
        for nm in names:
            S[nm] = [sem(f"{nm}{a}_done") for a in range(2)] if nm in pair else sem(f"{nm}_done")

        def halves(ap):
            return ap.rearrange("p (b n) -> p b n", b=2)

        N = strips
        CLEARS = 13
        SETUP_V = 5 + 2 + 2 + 16
        BIAS_V = SETUP_V + 4

        LOOPED = 4
        TURNS = (N - 2 - LOOPED) // 4

        def steps(eng, step, first, last):
            for raw in range(first, LOOPED):
                step(Strip(0, raw, N))
            with eng.Fori(0, TURNS) as i:
                for u in range(4):
                    step(Strip(i, LOOPED + u, N))
            for raw in range(LOOPED + 4 * TURNS, last):
                step(Strip(0, raw, N))

        def unless_first(s):
            return s if not isinstance(s.n, int) or s.n != 0 else Strip(0, -1, N)

        x2_strips = x2_dram.rearrange("b c (g s n) -> b s g c n", g=2, s=STRIPS)

        norm_loads = [(sums_f[:].rearrange("p a c -> p (a c)"), con["sums"]), (eps[:], con["eps0"])]
        loads = [
            (center[:], con["center"]), (const_f[:], con["picks"]), (eye_c[:], con["eye_c"]), (last_row[:], con["last_row"]),
            (key_ones[:], con["key_ones"]), (qkv_w[:], prm["qkv_w"]), (fc1_w[:], prm["fc1_w"]), (w2_own[:], prm["fc2_w"][0:F1, :]),
            (rows[0:1, 0:3 * C], prm["qkv_b"].unsqueeze(0)), (rows[0:1, 3 * C:], prm["fc1_b"].unsqueeze(0)),
        ]
        loads += [(norms[:, k:k + 1], prm[nm].unsqueeze(1))
                  for k, nm in enumerate(("norm1_g", "norm1_b", "norm2_g", "norm2_b"))]
        for g in range(2):
            lo = ROWB * g
            loads += [(proj_b[lo:lo + C, :], prm["proj_b"].unsqueeze(1)),
                      (fc2_b[lo:lo + C, :], prm["fc2_b"].unsqueeze(1)),
                      (w2_both[F2 * g:F2 * g + F2, lo:lo + C], prm["fc2_w"][F1:HID, :])]
            loads += [(proj_w[2 * DH * h + DH * g:2 * DH * h + DH * g + DH, lo:lo + C],
                       prm["proj_w"][DH * h:DH * h + DH, :]) for h in range(HEADS)]
        runs_of_rows = []
        for side in range(2):
            for a in range(WS):
                src = bass.AP(tensor=tables[side].tensor, offset=(WS - 1 - a) * SPAN + WS - 1,
                              ap=[[REL, HEADS], [-1, WS], [1, RUN]])
                runs_of_rows.append((table_runs[side][:, WS * a:WS * a + WS, :], src))
        blocks = []
        for side in range(2):
            for h in range(HEADS):
                src = bass.AP(tensor=table_runs[side].tensor, offset=h * TOK * RUN,
                              ap=[[RUN, TOK], [SPAN, WS], [1, WS]])
                dst = bias_f[0:TOK, side, TOK * h:TOK * h + TOK]
                blocks.append((dst.rearrange("p (a b) -> p a b", a=WS), src))

        block = ctx.enter_context(nc.Block())

        @block.sync
        def _(sp):
            for tab, first, sign in ((tables[0], (REL - 1) * HEADS, -1), (tables[1], 0, 1)):
                sp.dma_start(tab, bass.AP(tensor=prm["rel_bias_table"].tensor, offset=first,
                                          ap=[[1, HEADS], [sign * HEADS, REL], [1, 1]]),
                             allow_slow_non_contiguous=True).then_inc(table_turned, 16)

            def x_load(s):
                if s.real:
                    wait(sp, S["x1_made"], 2 * (s.n - 3))
                    for g in range(2):
                        sp.dma_start(X[ROWB * g:ROWB * g + C, s.slot(4), :],
                                     x_in[s.n, g]).then_inc(x_loaded[s.slot(4)], 16)

            def x2_store(s):
                if s.real:
                    wait(sp, S["x2_made"], 2 * s.n + 2)
                    for g in range(2):
                        dst = x2_strips[s.n // STRIPS, s.n % STRIPS, g]
                        sp.dma_start(dst, x2[ROWB * g:ROWB * g + C, s.slot(2), :]
                                     ).then_inc(x2_stored[s.slot(2)], 16)

            sp.wait_ge(x_cleared, 4)
            x_load(Strip(0, 0, N))
            for dst, src in norm_loads:
                sp.dma_start(dst, src).then_inc(norm_loaded, 16)
            sp.wait_ge(cleared, CLEARS)
            for dst, src in loads:
                sp.dma_start(dst, src).then_inc(loaded, 16)
            sp.wait_ge(table_turned, 32)
            for dst, src in runs_of_rows:
                sp.dma_start(dst, src).then_inc(runs_made, 16)
            x_load(Strip(0, 1, N))
            sp.wait_ge(runs_made, 16 * len(runs_of_rows))
            for dst, src in blocks:
                sp.dma_start(dst, src).then_inc(bias_loaded, 16)
            sp.wait_ge(later["cleared"], len(later["zeros"]))
            for dst, src in later["loads"]:
                sp.dma_start(dst, src).then_inc(later["loaded"], 16)

            def step(s):
                x_load(s.at(2))
                x2_store(s.at(-2))

            steps(sp, step, 0, N + 2)
            for r in range(2):
                sp.wait_ge(x2_stored[r], 32 * (N // 2))

        @block.gpsimd
        def _(pool):
            for t in (proj_w, proj_b, fc2_b, w2_both, bias_f, *gram, *wv, *w1_own, *w1_both):
                nc.gpsimd.memset(t[:], 0.0).then_inc(cleared, 1)
            for t in xs:
                nc.gpsimd.memset(t[:], 0.0).then_inc(xs_cleared, 1)
            for t in later["zeros"]:
                nc.gpsimd.memset(t, 0.0).then_inc(later["cleared"], 1)

            def low(a, s):
                if s.real:
                    wait(pool, S["hi"][a], s.n + 1)
                    wait(pool, (S["uu"], S["f1"])[a], 6 * (s.n - 1))
                    if a == 0:
                        wait(pool, S["xs_copied"], 4 * (s.n - 1))
                    r = s.slot(2)
                    nc.gpsimd.tensor_tensor(xm[a][1][:, r, :], xh[a][:], xm[a][0][:, r, :],
                                            ALU.subtract).then_inc(S["lo"][a], 1)

            def make_shift(s, j):
                if s.real:
                    q = 4 * s.n + j
                    wait(pool, S["mx"], q + 1)
                    wait(pool, S["st_q"], q - 1)
                    m = qmax[:, j % 2, :].unsqueeze(2).to_broadcast([R, QP * HEADS, TOK])
                    e = minus_eye.unsqueeze(1).to_broadcast([R, QP * HEADS, TOK])
                    nc.gpsimd.tensor_tensor(shift[:, j % 2], e, m, ALU.mult).then_inc(S["md"], 1)

            def x_low(s):
                if s.real:
                    wait(pool, S["x_hi"], s.n + 1)
                    wait(pool, S["cen"][0], 2 * s.n)
                    nc.gpsimd.tensor_tensor(xb[1][:], X[:, s.slot(4), :], xb[0][:], ALU.subtract
                                            ).then_inc(S["x_lo"], 1)

            def squares_low(a, s):
                if s.real:
                    wait(pool, S["var"][a], 2 * s.n)
                    for b in range(2):
                        cols = slice(HALF * b, HALF * b + HALF)
                        wait(pool, S["sq_hi"][a], 2 * s.n + b + 1)
                        nc.gpsimd.tensor_tensor(sqb[a][1][:, cols], sq[a][:, cols], sqb[a][0][:, cols], ALU.subtract
                                                ).then_inc(S["sq_lo"][a], 1)

            def x1_low(s):
                if s.real:
                    wait(pool, S["cen"][1], 2 * s.n)
                    for b in range(2):
                        cols = slice(HALF * b, HALF * b + HALF)
                        wait(pool, S["x1_hi"], 2 * s.n + b + 1)
                        nc.gpsimd.tensor_tensor(x1b[1][:, cols], x1[:, s.slot(2), cols], x1b[0][:, cols], ALU.subtract
                                                ).then_inc(S["x1_lo"], 1)

            x_low(Strip(0, 0, N))
            squares_low(0, Strip(0, 0, N))

            def step(s):
                old, prv, nxt, nx2 = s.at(-2), s.at(-1), s.at(1), s.at(2)
                low(0, nxt)
                x1_low(prv)
                make_shift(s, 2)
                squares_low(1, prv)
                x_low(unless_first(nx2))
                make_shift(s, 3)
                low(1, prv)
                make_shift(nxt, 0)
                squares_low(0, unless_first(nx2))
                make_shift(nxt, 1)

            steps(pool, step, -1, N + 2)

        @block.vector
        def _(dve):
            chain = [0]

            def link(ins):
                chain[0] += 1
                ins.then_inc(setup_v, 1)
                return chain[0]

            def x_high(s):
                if s.real:
                    wait(dve, x_loaded[s.slot(4)], 32 * (s.turn(4) + 1))
                    wait(dve, S["cen"][0], 2 * s.n)
                    nc.vector.tensor_copy(xb[0][:], X[:, s.slot(4), :]).then_inc(S["x_hi"], 1)

            def subtract_mean(a, s):
                if s.real:
                    for b in range(2):
                        wait(dve, S["cen"][a], 2 * s.n + b + 1)
                        cols = slice(HALF * b, HALF * b + HALF)
                        src = (X[:, s.slot(4), cols], x1[:, s.slot(2), cols])[a]
                        nc.vector.scalar_tensor_tensor(
                            out=xc[a][:, cols], in0=ps_m[0:R, b, 0:HALF], scalar=-1.0 / C, in1=src,
                            op0=ALU.mult, op1=ALU.add).then_inc(S["xc"][a], 1)

            def squares_high(a, s):
                if s.real:
                    wait(dve, S["var"][a], 2 * s.n)
                    for b in range(2):
                        cols = slice(HALF * b, HALF * b + HALF)
                        wait(dve, S["sq"][a], 2 * s.n + b + 1)
                        nc.vector.tensor_copy(sqb[a][0][:, cols], sq[a][:, cols]).then_inc(S["sq_hi"][a], 1)

            def normalise(a, s):
                if s.real:
                    wait(dve, S["rs"][a], s.n + 1)
                    wait(dve, S["lo"][a], s.n)
                    if a == 0:
                        ins = nc.vector.tensor_tensor(xh[0][:], xc[0][:], rs[0][:], ALU.mult)
                    else:
                        ins = nc.vector.scalar_tensor_tensor(out=xh[1][:], in0=xc[1][:], scalar=centred_b[:, 0:1],
                                                             in1=rs[1][:], op0=ALU.add, op1=ALU.mult)
                    ins.then_inc(S["xh"][a], 1)
                    wait(dve, S["xh"][a], s.n + 1)
                    if a == 0:
                        wait(dve, S["s_q"], 4 * (s.n - 1))
                    else:
                        wait(dve, S["f1"], 6 * (s.n - 1))
                    nc.vector.tensor_copy(xm[a][0][:, s.slot(2), :], xh[a][:]).then_inc(S["hi"][a], 1)

            for r in range(4):
                nc.vector.memset(X[:, r, :], 1.0).then_inc(x_cleared, 1)
            dve.wait_ge(norm_loaded, 16 * len(norm_loads))
            nc.vector.tensor_copy(sum_w[:], sums_f[:]).then_inc(sums_ready, 1)
            x_high(Strip(0, 0, N))
            subtract_mean(0, Strip(0, 0, N))
            squares_high(0, Strip(0, 0, N))
            dve.wait_ge(cleared, CLEARS)
            dve.wait_ge(loaded, 16 * len(loads))
            link(nc.vector.tensor_copy(const_b[:], const_f[:]))
            for a in range(2):
                link(nc.vector.tensor_scalar(aug[:, a, 0:C], eye_c[:, 0:C], norms[:, 2 * a:2 * a + 1], None, ALU.mult))
                link(nc.vector.tensor_copy(aug[:, a, C:C + 1], norms[:, 2 * a + 1:2 * a + 2]))
            dve.wait_ge(setup_t, 1)
            qk = ps_t[0:DH, 0, 0:6 * (C + 1)].rearrange("p (a c) -> p a c", a=6)
            k = link(nc.vector.tensor_scalar(qk_aug[:, 0:HEADS, :], qk[:, 0:HEADS, :], DH ** -0.5, None, ALU.mult))
            k = link(nc.vector.tensor_copy(qk_aug[:, HEADS:, :], qk[:, HEADS:, :]))
            dve.wait_ge(setup_t, 2)
            link(nc.vector.tensor_scalar(centred_b[:], ps_v[0:R, 0:1], -1.0, None, ALU.mult))
            link(nc.vector.tensor_tensor(out_b[:], proj_b[:], fc2_b[:], ALU.add))
            splits = []
            for g in range(2):
                lo = ROWB * g
                src_g = ps_s[lo:lo + C + 1, 0, 0:HEADS * (C + 1)].rearrange("p (h c) -> p h c", h=HEADS)
                splits.append((gram, lambda t, lo=lo: t[lo:lo + C + 1, :, lo:lo + C + 1], src_g))
                src_v = ps_s[lo:lo + C + 1, 1, 0:C].rearrange("p (h d) -> p h d", h=HEADS)
                splits.append((wv, lambda t, lo=lo, g=g: t[lo:lo + C + 1, :].rearrange(
                    "p (h g d) -> p h g d", h=HEADS, g=2)[:, :, g, :], src_v))
                splits.append((w1_own, lambda t, lo=lo: t[lo:lo + C + 1, :], ps_s[lo:lo + C + 1, 1, C:C + F1]))
                splits.append((w1_both, lambda t, lo=lo, g=g: t[lo:lo + C + 1, F2 * g:F2 * g + F2],
                               ps_s[lo:lo + C + 1, 1, C + F1:C + HID]))
            for pair_, view, src in splits:
                k = link(nc.vector.tensor_copy(view(pair_[0]), src))
                dve.wait_ge(setup_v, k)
                k = link(nc.vector.tensor_tensor(view(pair_[1]), src, view(pair_[0]), ALU.subtract))
            normalise(0, Strip(0, 0, N))
            dve.wait_ge(bias_loaded, 16 * len(blocks))
            k = link(nc.vector.tensor_copy(bias_f[ROWB:ROWB + TOK], bias_f[0:TOK]))
            dve.wait_ge(setup_v, k)
            link(nc.vector.tensor_copy(bias[:], bias_f[:]))
            dve.wait_ge(setup_v, k + 1)
            k = link(nc.vector.tensor_tensor(bias_f[ROWB:R], bias_f[ROWB:R], bias[ROWB:R], ALU.subtract))
            dve.wait_ge(setup_v, k)
            k = link(nc.vector.tensor_copy(bias[ROWB:R], bias_f[ROWB:R]))

            def block_diagonal(p, s):
                if s.real:
                    if isinstance(s.n, int) and s.n < 2:
                        wait(dve, xs_cleared, 2)
                    wait(dve, (S["hi"], S["lo"])[p][0], s.n + 1)
                    wait(dve, S["st_q"], 4 * (s.n - 1))
                    wait(dve, S["v_q"], 4 * (s.n - 1))
                    for g in range(2):
                        lo = ROWB * g
                        nc.vector.tensor_copy(
                            xs[p][lo:lo + C + 1, s.slot(2), :, TOK * g:TOK * g + TOK],
                            xm[0][p][lo:lo + C + 1, s.slot(2), :].rearrange("p (w t) -> p w t", t=TOK),
                        ).then_inc(S["xs_copied"], 1)

            def u_low(s, h):
                if s.real:
                    r = s.slot(2)
                    for b in range(2):
                        wait(dve, S["u_hi"], 6 * s.n + 2 * h + b + 1)
                        cols = slice(HALF * b, HALF * b + HALF)
                        nc.vector.tensor_tensor(U[1][:, r, h, cols], ps_m[0:R, b, 0:HALF], U[0][:, r, h, cols],
                                                ALU.subtract).then_inc(S["u_lo"], 1)

            def query_max(s, j):
                if s.real:
                    q = 4 * s.n + j
                    wait(dve, S["s_q"], q + 1)
                    wait(dve, S["md"], q - 1)
                    nc.vector.tensor_reduce(
                        qmax[:, j % 2, :].rearrange("p (b n) -> p b n", b=2),
                        ps_s[0:R, :, 0:2 * HQ].rearrange("p b (n t) -> p b n t", t=TOK),
                        AX_X, ALU.max).then_inc(S["mx"], 1)

            def divide(s, j):
                if s.real:
                    q = 4 * s.n + j
                    wait(dve, S["rdn"], q + 1)
                    wait(dve, S["proj"], 2 * (s.n - 1))
                    W = QP * TOK
                    nc.vector.tensor_tensor(O[:, s.slot(2), W * j:W * j + W], ps_o[0:2 * C, 0:W],
                                            rden[:, j % 2, :], ALU.mult).then_inc(S["nrm"], 1)

            def first_residual(s):
                if s.real:
                    wait(dve, S["cen"][1], 2 * s.n)
                    for b in range(2):
                        wait(dve, S["proj"], 2 * s.n + b + 1)
                        cols = slice(HALF * b, HALF * b + HALF)
                        half = x1[:, s.slot(2), cols]
                        nc.vector.scalar_tensor_tensor(
                            out=half, in0=ps_m[0:R, b, 0:HALF], scalar=out_b[:, 0:1],
                            in1=X[:, s.slot(4), cols], op0=ALU.add, op1=ALU.add).then_inc(S["x1_made"], 1)
                        wait(dve, S["x1_made"], 2 * s.n + b + 1)
                        nc.vector.tensor_copy(x1b[0][:, cols], half).then_inc(S["x1_hi"], 1)

            def second_residual(s):
                if s.real:
                    wait(dve, x2_stored[s.slot(2)], 32 * s.turn(2))
                    n = ROWB + C
                    for b in range(2):
                        wait(dve, S["f2"], 2 * s.n + b + 1)
                        win = slice(WINS // 2 * b, WINS // 2 * b + WINS // 2)
                        out = x2[0:n, s.slot(2), :].rearrange("p (i w j) -> p w i j", i=WS, j=WS)[:, win]
                        nc.vector.tensor_tensor(
                            out, ps_m[0:n, b, 0:HALF].rearrange("p (w i j) -> p w i j", i=WS, j=WS),
                            x1[0:n, s.slot(2), :].rearrange("p (w i j) -> p w i j", i=WS, j=WS)[:, win],
                            ALU.add).then_inc(S["x2_made"], 1)

            def step(s):
                old, prv, nxt, nx2 = s.at(-2), s.at(-1), s.at(1), s.at(2)
                second_residual(old)
                first_residual(prv)
                query_max(s, 2)
                u_low(nxt, 0)
                divide(s, 0)
                subtract_mean(1, prv)
                block_diagonal(1, nxt)
                squares_high(1, prv)
                x_high(unless_first(nx2))
                u_low(nxt, 1)
                block_diagonal(0, nxt)
                query_max(s, 3)
                divide(s, 1)
                normalise(1, prv)
                u_low(nxt, 2)
                subtract_mean(0, unless_first(nx2))
                divide(s, 2)
                query_max(nxt, 0)
                squares_high(0, unless_first(nx2))
                query_max(nxt, 1)
                normalise(0, unless_first(nx2))
                divide(s, 3)

            steps(dve, step, -1, N + 2)

        @block.scalar
        def _(act):
            act.wait_ge(norm_loaded, 16 * len(norm_loads))

            def square(a, s):
                if s.real:
                    wait(act, S["sq_lo"][a], 2 * s.n)
                    for b in range(2):
                        wait(act, S["xc"][a], 2 * s.n + b + 1)
                        cols = slice(HALF * b, HALF * b + HALF)
                        if a == 0:
                            ins = nc.scalar.activation(sq[0][:, cols], xc[0][:, cols], ACT.Square)
                        else:
                            ins = nc.scalar.activation(sq[1][:, cols], xc[1][:, cols], ACT.Square,
                                                       bias=centred_b[:, 0:1])
                        ins.then_inc(S["sq"][a], 1)

            def root(a, s):
                if s.real:
                    for b in range(2):
                        wait(act, S["var"][a], 2 * s.n + b + 1)
                        nc.scalar.activation(lnv[a][:, HALF * b:HALF * b + HALF], ps_m[0:R, b, 0:HALF], ACT.Ln,
                                             scale=1.0 / C, bias=eps[:, 0:1]).then_inc(S["ln"][a], 1)
                    wait(act, S["ln"][a], 2 * s.n + 2)
                    nc.scalar.activation(rs[a][:], lnv[a][:], ACT.Exp, scale=-0.5).then_inc(S["rs"][a], 1)

            def u_high(s, h):
                if s.real:
                    wait(act, S["st_q"], 4 * (s.n - 1))
                    for b in range(2):
                        wait(act, S["uu"], 6 * s.n + 2 * h + b + 1)
                        nc.scalar.copy(U[0][:, s.slot(2), h, HALF * b:HALF * b + HALF], ps_m[0:R, b, 0:HALF]
                                       ).then_inc(S["u_hi"], 1)

            def exp_scores(s, j):
                if s.real:
                    q = 4 * s.n + j
                    wait(act, S["st_q"], q + 1)
                    wait(act, S["pv_q"], q - 1)
                    nc.scalar.activation(P[:, j % 2].rearrange("p (b n) h t -> p b (n h t)", b=2),
                                         ps_t[0:KEYS, :, 0:2 * HQ], ACT.Exp).then_inc(S["ex"], 1)

            def keep_values(s, j):
                if s.real:
                    q = 4 * s.n + j
                    wait(act, S["v_q"], q + 1)
                    wait(act, S["pv_q"], q - 1)
                    nc.scalar.copy(V[:, j % 2].rearrange("p n c -> p (n c)"),
                                   ps_v[0:KEYS, 0:QP * 2 * C]).then_inc(S["vev"], 1)

            def invert_sums(s, j):
                if s.real:
                    q = 4 * s.n + j
                    W = QP * TOK
                    wait(act, S["pv_q"], q + 1)
                    nc.scalar.activation(lden[:], ps_o[0:2 * C, W:2 * W], ACT.Ln).then_inc(S["lnd"], 1)
                    wait(act, S["lnd"], q + 1)
                    wait(act, S["nrm"], q - 1)
                    nc.scalar.activation(rden[:, j % 2, :], lden[:], ACT.Exp, scale=-1.0).then_inc(S["rdn"], 1)

            def gelu(s, t):
                if s.real:
                    wait(act, S["f2"], 2 * (s.n - 1))
                    r = s.slot(2)
                    for b in range(2):
                        wait(act, S["f1"], 6 * s.n + 2 * t + b + 1)
                        if t < 2:
                            out = G[:, r, b, HALF * t:HALF * t + HALF]
                        else:
                            out = G[:, r, 2, HALF * b:HALF * b + HALF]
                        nc.scalar.activation(out, ps_m[:, b, 0:HALF], ACT.Gelu).then_inc(S["ge"], 1)

            def step(s):
                old, prv, nxt, nx2 = s.at(-2), s.at(-1), s.at(1), s.at(2)
                keep_values(s, 0)
                square(0, unless_first(nxt))
                gelu(old, 1)
                gelu(old, 2)
                nc.scalar.preload_act_table_set("natural_log_exp_and_others")
                root(0, unless_first(nxt))
                keep_values(s, 1)
                exp_scores(s, 0)
                invert_sums(prv, 3)
                exp_scores(s, 1)
                invert_sums(s, 0)
                u_high(nxt, 0)
                square(1, prv)
                invert_sums(s, 1)
                u_high(nxt, 1)
                exp_scores(s, 2)
                keep_values(s, 2)
                root(1, prv)
                u_high(nxt, 2)
                keep_values(s, 3)
                exp_scores(s, 3)
                invert_sums(s, 2)
                nc.scalar.preload_act_table_set("gelu_and_others")
                gelu(prv, 0)

            nc.scalar.preload_act_table_set("natural_log_exp_and_others")
            square(0, Strip(0, 0, N))
            root(0, Strip(0, 0, N))
            steps(act, step, -1, N + 2)

        @block.tensor
        def _(pe):
            mm = nc.tensor.matmul
            last = [None, None]

            def free_m(b):
                if last[b] is not None:
                    wait(pe, *last[b])

            def channel_sums(kind, parts, done, s, feeder, emptied):
                for b in range(2):
                    if feeder is not None:
                        wait(pe, feeder, 2 * s.n + b + 1)
                    free_m(b)
                    for m in range(2):
                        ins = mm(ps_m[0:R, b, 0:HALF], sum_w[:, kind, :], parts[m][:, HALF * b:HALF * b + HALF],
                                 start=(m == 0), stop=(m == 1))
                    ins.then_inc(done, 1)
                    last[b] = (emptied, 2 * s.n + b + 1)

            def centre(a, s):
                if s.real:
                    if a == 0:
                        wait(pe, S["x_lo"], s.n + 1)
                        channel_sums(0, xb, S["cen"][0], s, None, S["xc"][0])
                    else:
                        channel_sums(0, x1b, S["cen"][1], s, S["x1_lo"], S["xc"][1])

            def variance(a, s):
                if s.real:
                    channel_sums(1, sqb[a], S["var"][a], s, S["sq_lo"][a], S["ln"][a])

            pe.wait_ge(sums_ready, 1)
            centre(0, Strip(0, 0, N))
            variance(0, Strip(0, 0, N))
            pe.wait_ge(setup_v, 5)
            for k in range(2 * HEADS):
                out = ps_t[0:DH, 0, (C + 1) * k:(C + 1) * (k + 1)]
                mm(out, qkv_w[:, DH * k:DH * k + DH], aug[:, 0, :], start=True, stop=False)
                ins = mm(out, rows[0:1, DH * k:DH * k + DH], last_row[:], start=False, stop=True)
            ins.then_inc(setup_t, 1)
            pe.wait_ge(setup_v, 7)
            mm(ps_v[0:R, 0:1], center[:], fc2_b[:], start=True, stop=True)
            for g in range(2):
                lo = ROWB * g
                for h in range(HEADS):
                    mm(ps_s[lo:lo + C + 1, 0, (C + 1) * h:(C + 1) * (h + 1)], qk_aug[:, h, :],
                       qk_aug[:, HEADS + h, :], start=True, stop=True)
                out = ps_s[lo:lo + C + 1, 1, 0:C]
                mm(out, aug[:, 0, :], qkv_w[:, 2 * C:3 * C], start=True, stop=False)
                mm(out, last_row[:], rows[0:1, 2 * C:3 * C], start=False, stop=True)
                out = ps_s[lo:lo + C + 1, 1, C:C + HID]
                mm(out, aug[:, 1, :], fc1_w[:], start=True, stop=False)
                ins = mm(out, last_row[:], rows[0:1, 3 * C:], start=False, stop=True)
            ins.then_inc(setup_t, 1)
            pe.wait_ge(setup_v, SETUP_V)

            def u_product(s, h):
                if s.real:
                    wait(pe, S["hi"][0], s.n + 1)
                    wait(pe, S["lo"][0], s.n + 1)
                    r = s.slot(2)
                    for b in range(2):
                        free_m(b)
                        for k, (w, m) in enumerate(((0, 0), (0, 1), (1, 0))):
                            ins = mm(ps_m[0:R, b, 0:HALF], gram[w][:, h, :],
                                     xm[0][m][:, r, HALF * b:HALF * b + HALF], start=(k == 0), stop=(k == 2))
                        ins.then_inc(S["uu"], 1)
                        last[b] = (S["u_lo"], 6 * s.n + 2 * h + b + 1)

            def scores_q(s, j):
                if s.real:
                    q = 4 * s.n + j
                    if j == 0:
                        if isinstance(s.n, int) and s.n == 0:
                            wait(pe, setup_v, BIAS_V)
                        wait(pe, S["u_hi"], 6 * s.n + 6)
                        wait(pe, S["hi"][0], s.n + 1)
                    wait(pe, S["mx"], q)
                    r = s.slot(2)
                    for b in range(2):
                        mm(ps_s[0:R, b, 0:2 * HQ], pick_q,
                           bias[:, 0, :].unsqueeze(1).to_broadcast([R, 2, HQ]), start=True, stop=False)
                        for k in range(2):
                            w = QP * j + 2 * b + k
                            for h in range(HEADS):
                                for g in range(2):
                                    lo = ROWB * g
                                    at = HQ * k + TOK * h
                                    ins = mm(ps_s[lo:lo + TOK, b, at:at + TOK],
                                             U[0][lo:lo + C + 1, r, h, TOK * w:TOK * w + TOK],
                                             xm[0][0][lo:lo + C + 1, r, TOK * w:TOK * w + TOK],
                                             start=False, stop=(k == 1 and h == HEADS - 1))
                    ins.then_inc(S["s_q"], 1)

            def scores_k(s, j):
                if s.real:
                    q = 4 * s.n + j
                    if j == 0:
                        wait(pe, S["u_lo"], 6 * s.n + 6)
                        wait(pe, S["xs_copied"], 4 * s.n + 4)
                    wait(pe, S["ex"], q)
                    r = s.slot(2)
                    for b in range(2):
                        mm(ps_t[0:KEYS, b, 0:2 * HQ], pick_k,
                           bias[:, 1, :].unsqueeze(1).to_broadcast([R, 2, HQ]), start=True, stop=False)
                        for k in range(2):
                            w = QP * j + 2 * b + k
                            for ws, ms in ((0, 0), (0, 1), (1, 0)):
                                mm(ps_t[0:KEYS, b, HQ * k:HQ * k + HQ], xs[ws][:, r, w, :],
                                   U[ms][:, r, :, TOK * w:TOK * w + TOK], start=False, stop=False)

            def shift_scores(s, j):
                if s.real:
                    q = 4 * s.n + j
                    wait(pe, S["md"], q + 1)
                    for b in range(2):
                        ins = mm(ps_t[0:KEYS, b, 0:2 * HQ], group_ones,
                                 shift[:, j % 2, 2 * HEADS * b:2 * HEADS * (b + 1), :], start=False, stop=True)
                    ins.then_inc(S["st_q"], 1)

            def values(s, j):
                if s.real:
                    q = 4 * s.n + j
                    if j == 0:
                        wait(pe, S["xs_copied"], 4 * s.n + 4)
                    wait(pe, S["vev"], q)
                    r = s.slot(2)
                    for k in range(QP):
                        for n, (ws, ms) in enumerate(((0, 0), (1, 0), (0, 1))):
                            ins = mm(ps_v[0:KEYS, 2 * C * k:2 * C * (k + 1)], xs[ws][:, r, QP * j + k, :], wv[ms][:],
                                     start=(n == 0), stop=(n == 2))
                    ins.then_inc(S["v_q"], 1)

            def weigh(s, j):
                if s.real:
                    q = 4 * s.n + j
                    wait(pe, S["ex"], q + 1)
                    wait(pe, S["vev"], q + 1)
                    wait(pe, S["nrm"], q)
                    W = QP * TOK
                    for k in range(QP):
                        for h in range(HEADS):
                            lo = 2 * DH * h
                            mm(ps_o[lo:lo + 2 * DH, TOK * k:TOK * k + TOK], V[:, j % 2, k, lo:lo + 2 * DH],
                               P[:, j % 2, k, h, :], start=True, stop=True)
                    for h in range(HEADS):
                        lo = 2 * DH * h
                        ins = mm(ps_o[lo:lo + 2 * DH, W:2 * W], key_ones[:], P[:, j % 2, :, h, :],
                                 start=True, stop=True)
                    ins.then_inc(S["pv_q"], 1)

            def project(s):
                if s.real:
                    wait(pe, S["nrm"], 4 * s.n + 4)
                    for b in range(2):
                        free_m(b)
                        mm(ps_m[0:R, b, 0:HALF], proj_w[:], O[:, s.slot(2), HALF * b:HALF * b + HALF],
                           start=True, stop=True).then_inc(S["proj"], 1)
                        last[b] = (S["x1_made"], 2 * s.n + b + 1)

            def fc1(s, t):
                if s.real:
                    if t == 0:
                        wait(pe, S["hi"][1], s.n + 1)
                        wait(pe, S["lo"][1], s.n + 1)
                    r = s.slot(2)
                    for b in range(2):
                        free_m(b)
                        for k, (w, m) in enumerate(((0, 0), (0, 1), (1, 0))):
                            if t < 2:
                                lo = ROWB * b
                                ins = mm(ps_m[:, b, 0:HALF], w1_own[w][lo:lo + C + 1, :],
                                         xm[1][m][lo:lo + C + 1, r, HALF * t:HALF * t + HALF],
                                         start=(k == 0), stop=(k == 2))
                            else:
                                ins = mm(ps_m[:, b, 0:HALF], w1_both[w][:],
                                         xm[1][m][:, r, HALF * b:HALF * b + HALF],
                                         start=(k == 0), stop=(k == 2))
                        ins.then_inc(S["f1"], 1)
                        last[b] = (S["ge"], 6 * s.n + 2 * t + b + 1)

            def fc2(s):
                if s.real:
                    wait(pe, S["ge"], 6 * s.n + 6)
                    r = s.slot(2)
                    for b in range(2):
                        free_m(b)
                        cols = slice(HALF * b, HALF * b + HALF)
                        mm(ps_m[0:ROWB + C, b, 0:HALF], w2_both[:], G[:, r, 2, cols], start=True, stop=False)
                        for g in range(2):
                            lo = ROWB * g
                            ins = mm(ps_m[lo:lo + C, b, 0:HALF], w2_own[:], G[:, r, g, cols],
                                     start=False, stop=True)
                        ins.then_inc(S["f2"], 1)
                        last[b] = (S["x2_made"], 2 * s.n + b + 1)

            def step(s):
                old, prv, nxt, nx2 = s.at(-2), s.at(-1), s.at(1), s.at(2)
                if old.real:
                    for b in range(2):
                        last[b] = (S["ge"], 6 * old.n + 4 + b + 1)
                scores_k(s, 0)
                variance(0, unless_first(nxt))
                shift_scores(s, 0)
                values(s, 1)
                scores_q(s, 2)
                fc2(old)
                scores_k(s, 1)
                project(prv)
                shift_scores(s, 1)
                weigh(s, 0)
                u_product(nxt, 0)
                scores_k(s, 2)
                centre(1, prv)
                weigh(s, 1)
                u_product(nxt, 1)
                values(s, 2)
                shift_scores(s, 2)
                scores_q(s, 3)
                variance(1, prv)
                values(s, 3)
                scores_k(s, 3)
                u_product(nxt, 2)
                shift_scores(s, 3)
                weigh(s, 2)
                values(nxt, 0)
                centre(0, unless_first(nx2))
                scores_q(nxt, 0)
                fc1(prv, 0)
                weigh(s, 3)
                fc1(prv, 1)
                scores_q(nxt, 1)
                fc1(prv, 2)

            steps(pe, step, -1, N + 2)


PIECES = 3
ROWS = 32 * (PIECES - 1) + WS


def convolution_weights(nc, sb, dw_w, bands):
    hot = sb("hot", [ROWS, IMG, IMG], BF16)
    taps = sb("taps", [ROWS, C * WS], F32)
    loads = []
    for k in range(PIECES):
        loads += [(hot[32 * k:32 * k + WS], bands.bitcast(BF16)),
                  (taps[32 * k:32 * k + WS, :].rearrange("p (c b) -> p c b", b=WS),
                   dw_w.rearrange("c o a b -> a (c o) b"))]
    return {"hot": hot, "taps": taps, "zeros": [hot[:], taps[:]]}, loads


def convolution_phase(nc, weights, later, x2_dram, y_dram, images):
    with ExitStack() as ctx:
        def sb(name, shape, dt=F32):
            return ctx.enter_context(nc.sbuf_tensor(name, shape, dt))

        def sem(name):
            return ctx.enter_context(nc.semaphore(name))

        THIRDS = 3
        GROUP = C * WS // THIRDS
        PER = 4
        FILLS = IMG // PER
        TURN = 7
        FILL_TURNS = FILLS // TURN
        FILLED = (THIRDS - 1) * FILL_TURNS
        half = images // 2
        back = IMG - SHIFT

        ps = [ctx.enter_context(nc.psum_tensor(f"conv_ps{r}", [128, 2, 512], F32)) for r in range(4)]
        hot, taps = weights["hot"], weights["taps"]
        rest = sb("rest", [ROWS, C * WS])
        piece = [sb(f"piece{k}", [ROWS, C * WS], BF16) for k in range(PIECES)]
        split = sb("split", [ROWS, C * WS], BF16)
        band = [sb(f"band_{p}", [IMG, C * WS, IMG], BF16) for p in "hl"]
        xin = sb("xin", [IMG, 2, images, IMG])
        xp = [sb(f"xp_{p}", [IMG, 2, images, PAD], BF16) for p in "hl"]
        y = sb("y", [IMG, 2, images, IMG])

        conv_cleared = sem("conv_cleared")
        split_made = sem("split_made")
        band_filled = sem("band_filled")
        band_high = sem("band_high")
        band_low = sem("band_low")
        xin_loaded = [sem(f"xin_loaded{r}") for r in range(2)]
        xp_high = sem("xp_high")
        xp_low = sem("xp_low")
        convolved = sem("convolved")
        y_made = sem("y_made")
        y_stored = [sem(f"y_stored{r}") for r in range(2)]
        block = ctx.enter_context(nc.Block())

        def fills(i, r, fill):
            for u in range(*((0, TURN // 2 + 1), (TURN // 2 + 1, TURN))[r]):
                fill(1 + i // FILL_TURNS, TURN * (i % FILL_TURNS) + u, u, FILLS + TURN * i + u)

        def pairs_of_channels(eng, two, last):
            for i in range(2):
                two(i, True)
            with eng.Fori(2, FILLED) as i:
                two(i, True)
            with eng.Fori(FILLED, last) as i:
                two(i, False)

        def fill_ps(u):
            return ps[2 + u % 4 // 2][0:IMG, u % 2, 0:PER * GROUP]

        def fill_view(w, third, block_):
            by_third = band[w][:].rearrange("i (t k) (b o) -> i t b o k", t=THIRDS, o=PER)
            return by_third[:, third, block_]

        def runs(r, padded, rolled):
            return ((padded[:, r, :, 2 * SHIFT:2 * SHIFT + back], rolled[:, r, :, 0:back]),
                    (padded[:, r, :, SHIFT:2 * SHIFT], rolled[:, r, :, back:IMG]))

        @block.sync
        def _(sp):
            def load(c, r):
                wait(sp, xp_low, 2 * c - 2)
                sp.dma_start(xin[:, r], x2_dram[:, c].rearrange("b (h w) -> h b w", h=IMG)
                             ).then_inc(xin_loaded[r], 16)

            def two(i, filling):
                for r in range(2):
                    load(2 * i + r, r)

            pairs_of_channels(sp, two, C // 2)

        @block.gpsimd
        def _(pool):
            for p in range(2):
                nc.gpsimd.memset(xp[p][:], 0.0).then_inc(conv_cleared, 1)

            def store(c, r):
                wait(pool, y_made, 2 * c + 2)
                pool.dma_start(y_dram[:, c].rearrange("b (h w) -> h b w", h=IMG), y[:, r]
                               ).then_inc(y_stored[r], 16)

            def two(i, filling):
                for r in range(2):
                    store(2 * i + r, r)

            pairs_of_channels(pool, two, C // 2)
            for r in range(2):
                pool.wait_ge(y_stored[r], 16 * (C // 2))

        @block.vector
        def _(dve):
            dve.wait_ge(later["loaded"], 16 * len(later["loads"]))
            k = 0
            for n in range(PIECES):
                src = taps if n == 0 else rest
                nc.vector.tensor_copy(piece[n][:], src[:]).then_inc(split_made, 1)
                k += 1
                dve.wait_ge(split_made, k)
                if n < PIECES - 1:
                    nc.vector.tensor_tensor(rest[:], src[:], piece[n][:], ALU.subtract).then_inc(split_made, 1)
                    k += 1
                    dve.wait_ge(split_made, k)
            for n in range(PIECES):
                lo, hi = 32 * n, min(32 * n + 32, ROWS)
                nc.vector.tensor_copy(split[lo:hi], piece[n][lo:hi]).then_inc(split_made, 1)

            def fill(third, block_, u, count):
                wait(dve, band_high, count + 1)
                nc.vector.tensor_tensor(fill_view(1, third, block_), fill_ps(u).rearrange("i (o k) -> i o k", o=PER),
                                        fill_view(0, third, block_), ALU.subtract).then_inc(band_low, 1)

            def low(c, r):
                wait(dve, xp_high, 2 * c + 2)
                wait(dve, convolved, c - 1)
                for k, (dst, src) in enumerate(runs(r, xp[1], xin)):
                    nc.vector.tensor_tensor(dst, src, runs(r, xp[0], xin)[k][0], ALU.subtract).then_inc(xp_low, 1)

            for f in range(FILLS):
                fill(0, f, f, f)
            dve.wait_ge(conv_cleared, 2)
            low(0, 0)

            def two(i, filling):
                low(2 * i + 1, 1)
                if filling:
                    fills(i, 0, fill)
                low(2 * i + 2, 0)
                if filling:
                    fills(i, 1, fill)

            pairs_of_channels(dve, two, C // 2 - 1)
            low(C - 1, 1)

        @block.scalar
        def _(act):
            def fill(third, block_, u, count):
                wait(act, band_filled, count + 1)
                nc.scalar.copy(fill_view(0, third, block_), fill_ps(u).rearrange("i (o k) -> i o k", o=PER)
                               ).then_inc(band_high, 1)

            def high(c, r, turn):
                wait(act, xin_loaded[r], 16 * (turn + 1))
                wait(act, convolved, c - 1)
                for dst, src in runs(r, xp[0], xin):
                    nc.scalar.copy(dst, src).then_inc(xp_high, 1)

            def keep(c, r, turn):
                wait(act, convolved, c + 1)
                wait(act, y_stored[r], 16 * turn)
                full = ps[r][0:IMG, :, 0:half * IMG].rearrange("h k (b w) -> h k b w", w=IMG)
                out = y[:, r].rearrange("h (k b) w -> h k b w", k=2)
                nc.scalar.copy(out[:, :, :, 0:back], full[:, :, :, SHIFT:IMG]).then_inc(y_made, 1)
                nc.scalar.copy(out[:, :, :, back:IMG], full[:, :, :, 0:SHIFT]).then_inc(y_made, 1)

            act.wait_ge(conv_cleared, 2)
            high(0, 0, 0)
            for f in range(FILLS):
                fill(0, f, f, f)
            high(1, 1, 0)

            def two(i, filling):
                keep(2 * i, 0, i)
                if filling:
                    fills(i, 0, fill)
                high(2 * i + 2, 0, i + 1)
                keep(2 * i + 1, 1, i)
                if filling:
                    fills(i, 1, fill)
                high(2 * i + 3, 1, i + 1)

            pairs_of_channels(act, two, C // 2 - 1)
            for r in range(2):
                keep(C - 2 + r, r, C // 2 - 1)

        @block.tensor
        def _(pe):
            mm = nc.tensor.matmul
            pe.wait_ge(split_made, 8)
            def fill(third, block_, u, count):
                wait(pe, band_low, count - (3 if u >= 3 else 2))
                columns = split[:].rearrange("p (t k) -> p t k", t=THIRDS)[:, third]
                for o in range(PER):
                    ins = mm(fill_ps(u)[:, GROUP * o:GROUP * (o + 1)], hot[:, PER * block_ + o, :], columns,
                             start=True, stop=True)
                ins.then_inc(band_filled, 1)

            for f in range(FILLS):
                fill(0, f, f, f)
            pe.wait_ge(band_low, FILLS)

            def convolve(c, r):
                wait(pe, xp_low, 2 * c + 2)
                wait(pe, y_made, 2 * c - 2)
                parts = ((0, 0), (0, 1), (1, 0))
                for dx in range(WS):
                    for n, (w, m) in enumerate(parts):
                        for k in range(2):
                            ins = mm(ps[r][0:IMG, k, 0:half * IMG], band[w][:, c * WS + dx, :],
                                     xp[m][:, r, half * k:half * (k + 1), dx:dx + IMG],
                                     start=(dx == 0 and n == 0), stop=(dx == WS - 1 and n == 2))
                ins.then_inc(convolved, 1)

            def two(i, filling):
                for r in range(2):
                    convolve(2 * i + r, r)
                    if filling:
                        fills(i, r, fill)

            pairs_of_channels(pe, two, C // 2)


RESPONSE_TILES = ("center spread eye_c last_row eye twins mean_all mean_top w1 w1t w2 rows norm aug "
                  "dw_b shift_c w1_own w1_both w2_own w2_both w2s_own w2s_both grn_g grn_b out_b b2 eps").split()


def response_weights(nc, sb, prm, con):
    center = sb("r_center", [R, R])
    spread = sb("r_spread", [R, R])
    eye_c = sb("r_eye_c", [C, C + 1])
    last_row = sb("r_last_row", [1, C + 1])
    eye = sb("r_eye", [128, 128])
    twins = sb("r_twins", [128, 128])
    mean_all = sb("r_mean_all", [128, 128])
    mean_top = sb("r_mean_top", [128, 128])
    w1 = sb("r_w1", [128, 2, C])
    w1t = sb("r_w1t", [C, HID])
    w2 = sb("r_w2", [C, 2 * F1])
    rows = sb("r_rows", [1, HID])
    norm = sb("r_norm", [C, 2])
    aug = sb("r_aug", [C, C + 1])
    dw_b = sb("r_dw_b", [R, 1])
    shift_c = sb("r_shift_c", [R, 1])
    w1_own = [sb(f"r_w1_own_{p}", [R, F1], BF16) for p in "hl"]
    w1_both = [sb(f"r_w1_both_{p}", [R, 2 * F2], BF16) for p in "hl"]
    w2_own = sb("r_w2_own", [F1, C])
    w2_both = sb("r_w2_both", [2 * F2, ROWB + C])
    w2s_own = sb("r_w2s_own", [F1, 2, C])
    w2s_both = sb("r_w2s_both", [2 * F2, 2, ROWB + C])
    grn_g = sb("r_grn_g", [128, 2])
    grn_b = sb("r_grn_b", [128, 2])
    out_b = sb("r_out_b", [ROWB + C, 1])
    b2 = sb("r_b2", [ROWB + C, 1])
    eps = sb("r_eps", [R, 1])

    loads = [
        (center[:], con["center"]), (spread[:], con["spread1"]), (eye_c[:], con["eye_c"]),
        (last_row[:], con["last_row"]), (eye[:], con["eye"]), (twins[:], con["twins"]),
        (mean_all[:], con["mean_all"]), (mean_top[:], con["mean_top"]),
        (w1[:, 0, :], prm["w1"][0:F1, :]), (w1[0:F2, 1, :], prm["w1"][F1:HID, :]),
        (w2[:, 0:HID], prm["w2"]), (w2[:, HID:], prm["w2"][:, F1:HID]),
        (rows[:], prm["b1"].unsqueeze(0)), (norm[:, 0:1], prm["ln_g"].unsqueeze(1)),
        (norm[:, 1:2], prm["ln_b"].unsqueeze(1)),
    ]
    for t, nm in ((grn_g, "grn_g"), (grn_b, "grn_b")):
        loads += [(t[0:F1, 0:1], prm[nm][0:F1].unsqueeze(1)), (t[0:F2, 1:2], prm[nm][F1:HID].unsqueeze(1)),
                  (t[F2:2 * F2, 1:2], prm[nm][F1:HID].unsqueeze(1))]
    for g in range(2):
        loads += [(dw_b[ROWB * g:ROWB * g + C, :], prm["dw_b"].unsqueeze(1)),
                  (b2[ROWB * g:ROWB * g + C, :], prm["b2"].unsqueeze(1))]
    tiles = dict(zip(RESPONSE_TILES, (center, spread, eye_c, last_row, eye, twins, mean_all, mean_top, w1, w1t, w2, rows, norm, aug,
                                      dw_b, shift_c, w1_own, w1_both, w2_own, w2_both, w2s_own, w2s_both, grn_g, grn_b, out_b, b2, eps)))
    return tiles, [dw_b[:], b2[:]], loads


def response_phase(nc, weights, later, x2_dram, y_dram, out_dram, strips):
    with ExitStack() as ctx:
        def sb(name, shape, dt=F32):
            return ctx.enter_context(nc.sbuf_tensor(name, shape, dt))

        def sem(name):
            return ctx.enter_context(nc.semaphore(name))

        N = strips
        RING = 2 * STRIPS
        LAG = STRIPS + 1
        by_strip = [t.rearrange("b c (g s n) -> b s g c n", g=2, s=STRIPS) for t in (y_dram, x2_dram, out_dram)]

        ps_m = ctx.enter_context(nc.psum_tensor("r_ps_m", [128, 2, 512], F32))
        ps_f = [ctx.enter_context(nc.psum_tensor(f"r_ps_f{r}", [128, 2, 512], F32)) for r in range(2)]
        ps_o = ctx.enter_context(nc.psum_tensor("r_ps_o", [128, 2, 512], F32))

        (center, spread, eye_c, last_row, eye, twins, mean_all, mean_top, w1, w1t, w2, rows, norm, aug,
         dw_b, shift_c, w1_own, w1_both, w2_own, w2_both, w2s_own, w2s_both, grn_g, grn_b, out_b, b2, eps) = (
            weights[k] for k in RESPONSE_TILES)
        Y = sb("r_Y", [R, 2, STRIP])
        X2 = sb("r_X2", [ROWB + C, 2, STRIP])
        OUT = sb("r_OUT", [ROWB + C, 2, STRIP])
        xc = sb("r_xc", [R, STRIP])
        sq = sb("r_sq", [R, STRIP])
        lnv = sb("r_lnv", [R, STRIP])
        rs = sb("r_rs", [R, STRIP])
        xh = sb("r_xh", [R, STRIP])
        xm = [sb(f"r_xm_{p}", [R, 2, STRIP], BF16) for p in "hl"]
        G = sb("r_G", [128, RING, 3, STRIP])
        junk = sb("r_junk", [128, STRIP])
        sums = sb("r_sums", [128, 3, RING])
        total = sb("r_total", [128, 3])
        both = sb("r_both", [128, 2])
        gx = sb("r_gx", [128, 2])
        mean = sb("r_mean", [128, 1])
        inv = sb("r_inv", [128, 1])
        scale = sb("r_scale", [128, 2])

        def sems(text):
            return {nm: sem("r_" + nm) for nm in text.split()}

        S = sems("cleared y_cleared setup_v setup_t cen var f1 f2 pairs mean_ps xc xh hi summed totals both_made "
                 "gx_made inv_made scaled w2_scaled out_made sq ln rs ge lo")
        y_loaded = [sem(f"r_y_loaded{r}") for r in range(2)]
        x2_loaded = [sem(f"r_x2_loaded{r}") for r in range(2)]
        stored = [sem(f"r_stored{r}") for r in range(2)]
        block = ctx.enter_context(nc.Block())

        CLEARS = 8
        SETUP_V = 17

        def halves(ap):
            return ap.rearrange("p (b n) -> p b n", b=2)

        def steps(eng, step, last):
            turns = max((N - RING - 2) // RING, 0)
            for raw in range(-2, RING):
                step(Strip(0, raw, N))
            if turns:
                with eng.Fori(0, turns) as i:
                    for u in range(RING):
                        step(Strip(RING // 4 * i, RING + u, N))
            for raw in range(RING + RING * turns, last):
                step(Strip(0, raw, N))

        @block.sync
        def _(sp):
            sp.wait_ge(S["y_cleared"], 1)

            def step(s):
                nxt, old = s.at(2), s.at(-LAG)
                if nxt.real:
                    wait(sp, S["cen"], nxt.n - 1)
                    for g in range(2):
                        sp.dma_start(Y[ROWB * g:ROWB * g + C, nxt.slot(2), :],
                                     by_strip[0][nxt.n // STRIPS, nxt.n % STRIPS, g]
                                     ).then_inc(y_loaded[nxt.slot(2)], 16)
                if old.real:
                    if isinstance(old.n, int) and old.n == 0:
                        wait(sp, S["cleared"], CLEARS)
                    wait(sp, S["out_made"], old.n - 1)
                    for g in range(2):
                        sp.dma_start(X2[ROWB * g:ROWB * g + C, old.slot(2), :],
                                     by_strip[1][old.n // STRIPS, old.n % STRIPS, g]
                                     ).then_inc(x2_loaded[old.slot(2)], 16)

            steps(sp, step, N + LAG)

        @block.gpsimd
        def _(pool):
            nc.gpsimd.memset(eps[:], EPS1).then_inc(S["cleared"], 1)
            for t in (*w1_own, *w1_both, w2_both, out_b, X2):
                nc.gpsimd.memset(t[:], 0.0).then_inc(S["cleared"], 1)

            def step(s):
                nxt, old = s.at(2), s.at(-LAG)
                if nxt.real:
                    wait(pool, S["hi"], nxt.n + 1)
                    wait(pool, S["f1"], 3 * (nxt.n - 1))
                    nc.gpsimd.tensor_tensor(xm[1][:, nxt.slot(2), :], xh[:], xm[0][:, nxt.slot(2), :],
                                            ALU.subtract).then_inc(S["lo"], 1)
                if old.real:
                    wait(pool, S["out_made"], old.n + 1)
                    for g in range(2):
                        pool.dma_start(by_strip[2][old.n // STRIPS, old.n % STRIPS, g],
                                       OUT[ROWB * g:ROWB * g + C, old.slot(2), :]
                                       ).then_inc(stored[old.slot(2)], 16)

            steps(pool, step, N + LAG)
            for r in range(2):
                pool.wait_ge(stored[r], 32 * (N // 2))

        @block.vector
        def _(dve):
            chain = [0]

            def link(ins):
                chain[0] += 1
                ins.then_inc(S["setup_v"], 1)
                return chain[0]

            nc.vector.memset(Y[:], 1.0).then_inc(S["y_cleared"], 1)
            dve.wait_ge(S["cleared"], CLEARS)
            dve.wait_ge(later["loaded"], 16 * len(later["loads"]))
            link(nc.vector.tensor_scalar(aug[:, 0:C], eye_c[:, 0:C], norm[:, 0:1], None, ALU.mult))
            link(nc.vector.tensor_copy(aug[:, C:C + 1], norm[:, 1:2]))
            dve.wait_ge(S["setup_t"], 1)
            link(nc.vector.tensor_copy(w1t[:], ps_f[0][0:C, 0, 0:HID]))
            link(nc.vector.tensor_copy(w2_own[:], ps_f[0][:, 1, 0:C]))
            for g in range(2):
                at = F2 * g
                link(nc.vector.tensor_copy(w2_both[at:at + F2, ROWB * g:ROWB * g + C],
                                           ps_f[0][at:at + F2, 1, C:2 * C]))
            dve.wait_ge(S["setup_t"], 2)
            link(nc.vector.tensor_copy(shift_c[:], ps_m[0:R, 0, 0:1]))
            link(nc.vector.tensor_tensor(out_b[0:C, :], ps_m[0:C, 1, 0:1], b2[0:C, :], ALU.add))
            link(nc.vector.tensor_tensor(out_b[ROWB:ROWB + C, :], ps_m[ROWB:ROWB + C, 1, 0:1], b2[ROWB:ROWB + C, :], ALU.add))
            for g in range(2):
                lo = ROWB * g
                for pair_, view, src in (
                        (w1_own, lambda t: t[lo:lo + C + 1, :], ps_f[1][lo:lo + C + 1, 0, 0:F1]),
                        (w1_both, lambda t: t[lo:lo + C + 1, F2 * g:F2 * g + F2], ps_f[1][lo:lo + C + 1, 0, F1:HID])):
                    k = link(nc.vector.tensor_copy(view(pair_[0]), src))
                    dve.wait_ge(S["setup_v"], k)
                    k = link(nc.vector.tensor_tensor(view(pair_[1]), src, view(pair_[0]), ALU.subtract))

            def copy_centered(s):
                if s.real:
                    wait(dve, S["cen"], s.n + 1)
                    nc.vector.tensor_scalar(halves(xc[:]), ps_m[0:R, :, 0:HALF], shift_c[:, 0:1], None,
                                            ALU.add).then_inc(S["xc"], 1)

            def normalise(s):
                if s.real:
                    wait(dve, S["rs"], s.n + 1)
                    wait(dve, S["lo"], s.n)
                    nc.vector.tensor_tensor(xh[:], xc[:], rs[:], ALU.mult).then_inc(S["xh"], 1)
                    wait(dve, S["xh"], s.n + 1)
                    wait(dve, S["f1"], 3 * (s.n - 1))
                    nc.vector.tensor_copy(xm[0][:, s.slot(2), :], xh[:]).then_inc(S["hi"], 1)

            def sum_squares(s, t):
                if s.real:
                    wait(dve, S["ge"], 3 * s.n + (2 if t < 2 else 3))
                    g = G[:, s.raw % RING, t, :]
                    wait(dve, S["summed"], 3 * s.n + t)
                    nc.vector.tensor_tensor_reduce(out=junk[:], in0=g, in1=g, scale=1.0, scalar=0.0, op0=ALU.mult,
                                                   op1=ALU.add, accum_out=sums[:, t, s.raw % RING:s.raw % RING + 1]
                                                   ).then_inc(S["summed"], 1)

            def respond(s):
                if s.real and s.raw % STRIPS == 0:
                    m = s.raw // STRIPS if isinstance(s.i, int) else None
                    img = s.i // 2 + s.raw // STRIPS if m is None else m
                    p = s.raw // STRIPS % 2
                    wait(dve, S["summed"], 3 * (s.n + STRIPS))
                    nc.vector.tensor_reduce(total[:], sums[:, :, STRIPS * p:STRIPS * (p + 1)], AX_X, ALU.add).then_inc(S["totals"], 1)
                    wait(dve, S["totals"], 2 * img + 1)
                    nc.vector.tensor_tensor(total[:, 0:1], total[:, 0:1], total[:, 1:2], ALU.add).then_inc(S["totals"], 1)
                    wait(dve, S["mean_ps"], img + 1)
                    nc.vector.tensor_scalar(mean[:], ps_o[:, 0, HALF + 2:HALF + 3], EPS1, None, ALU.add).then_inc(S["inv_made"], 1)
                    wait(dve, S["inv_made"], 2 * img + 1)
                    nc.vector.reciprocal(inv[:], mean[:]).then_inc(S["inv_made"], 1)
                    wait(dve, S["inv_made"], 2 * img + 2)
                    nc.vector.scalar_tensor_tensor(out=scale[:], in0=gx[:], scalar=inv[:, 0:1], in1=grn_g[:],
                                                   op0=ALU.mult, op1=ALU.mult).then_inc(S["scaled"], 1)
                    wait(dve, S["scaled"], 2 * img + 1)
                    nc.vector.tensor_scalar(scale[:], scale[:], 1.0, None, ALU.add).then_inc(S["scaled"], 1)
                    wait(dve, S["scaled"], 2 * img + 2)
                    nc.vector.tensor_scalar(w2s_own[:, p, :], w2_own[:], scale[:, 0:1], None, ALU.mult
                                            ).then_inc(S["w2_scaled"], 1)
                    nc.vector.tensor_scalar(w2s_both[:, p, :], w2_both[:], scale[:, 1:2], None, ALU.mult
                                            ).then_inc(S["w2_scaled"], 1)

            def finish(s):
                if s.real:
                    wait(dve, S["f2"], s.n + 1)
                    wait(dve, x2_loaded[s.slot(2)], 32 * (s.turn(2) + 1))
                    wait(dve, stored[s.slot(2)], 32 * s.turn(2))
                    n = ROWB + C
                    nc.vector.scalar_tensor_tensor(
                        out=halves(OUT[:, s.slot(2), :]), in0=ps_o[0:n, :, 0:HALF], scalar=out_b[:, 0:1],
                        in1=halves(X2[:, s.slot(2), :]), op0=ALU.add, op1=ALU.add).then_inc(S["out_made"], 1)

            def step(s):
                nxt, old = s.at(2), s.at(-LAG)
                copy_centered(nxt)
                respond(old)
                sum_squares(s.at(-1), 2)
                sum_squares(s, 0)
                sum_squares(s, 1)
                normalise(nxt)
                finish(old)

            steps(dve, step, N + LAG)

        @block.scalar
        def _(act):
            act.wait_ge(S["cleared"], CLEARS)

            def features(s, t):
                if s.real:
                    wait(act, S["f1"], 3 * s.n + t + 1)
                    if t == 0:
                        wait(act, S["f2"], s.n - RING + 1)
                        wait(act, S["summed"], 3 * (s.n - RING + 1))
                    src = ps_f[(s.raw + t) % 2][:, :, 0:HALF]
                    slot = s.raw % RING
                    out = G[:, slot, 0:2, HALF * t:HALF * t + HALF] if t < 2 else halves(G[:, slot, 2, :])
                    nc.scalar.activation(out, src, ACT.Gelu).then_inc(S["ge"], 1)

            def step(s):
                nxt, old = s.at(2), s.at(-LAG)
                if old.real and old.raw % STRIPS == 0:
                    img = old.raw // STRIPS if isinstance(old.i, int) else old.i // 2 + old.raw // STRIPS
                    wait(act, S["pairs"], img + 1)
                    nc.scalar.activation(gx[:], ps_o[:, 0, HALF:HALF + 2], ACT.Sqrt).then_inc(S["gx_made"], 1)
                features(s.at(-1), 2)
                if nxt.real:
                    wait(act, S["xc"], nxt.n + 1)
                    nc.scalar.activation(sq[:], xc[:], ACT.Square).then_inc(S["sq"], 1)
                features(s, 0)
                features(s, 1)
                if nxt.real:
                    nc.scalar.preload_act_table_set("natural_log_exp_and_others")
                    wait(act, S["var"], nxt.n + 1)
                    nc.scalar.activation(halves(lnv[:]), ps_m[0:R, :, 0:HALF], ACT.Ln, bias=eps[:, 0:1]
                                         ).then_inc(S["ln"], 1)
                    wait(act, S["ln"], nxt.n + 1)
                    nc.scalar.activation(rs[:], lnv[:], ACT.Exp, scale=-0.5).then_inc(S["rs"], 1)

            steps(act, step, N + LAG)

        @block.tensor
        def _(pe):
            mm = nc.tensor.matmul
            pe.wait_ge(later["loaded"], 16 * len(later["loads"]))
            nc.tensor.transpose(ps_f[0][0:C, 0, 0:F1], w1[:, 0, :], eye[:])
            nc.tensor.transpose(ps_f[0][0:C, 0, F1:HID], w1[0:F2, 1, :], eye[0:F2, 0:F2])
            nc.tensor.transpose(ps_f[0][:, 1, 0:C], w2[:, 0:F1], eye[0:C, 0:C])
            nc.tensor.transpose(ps_f[0][:, 1, C:2 * C], w2[:, F1:2 * F1], eye[0:C, 0:C]).then_inc(S["setup_t"], 1)
            pe.wait_ge(S["setup_v"], 6)
            mm(ps_m[0:R, 0, 0:1], center[:], dw_b[:], start=True, stop=True)
            for g in range(2):
                lo = ROWB * g
                out = ps_m[lo:lo + C, 1, 0:1]
                mm(out, w2_own[:], grn_b[:, 0:1], start=True, stop=False)
                mm(out, w2_both[0:F2, 0:C], grn_b[0:F2, 1:2], start=False, stop=True)
                out = ps_f[1][lo:lo + C + 1, 0, 0:HID]
                mm(out, aug[:], w1t[:], start=True, stop=False)
                ins = mm(out, last_row[:], rows[:], start=False, stop=True)
            ins.then_inc(S["setup_t"], 1)
            pe.wait_ge(S["setup_v"], SETUP_V)

            def centre(s):
                if s.real:
                    wait(pe, y_loaded[s.slot(2)], 32 * (s.turn(2) + 1))
                    wait(pe, S["ln"], s.n)
                    for b in range(2):
                        ins = mm(ps_m[0:R, b, 0:HALF], center[:], Y[:, s.slot(2), HALF * b:HALF * b + HALF],
                                 start=True, stop=True)
                    ins.then_inc(S["cen"], 1)

            def variance(s):
                if s.real:
                    wait(pe, S["sq"], s.n + 1)
                    for b in range(2):
                        ins = mm(ps_m[0:R, b, 0:HALF], spread[:], sq[:, HALF * b:HALF * b + HALF],
                                 start=True, stop=True)
                    ins.then_inc(S["var"], 1)

            def fc1(s, t):
                if s.real:
                    if t == 0:
                        wait(pe, S["hi"], s.n + 1)
                        wait(pe, S["lo"], s.n + 1)
                    wait(pe, S["ge"], 3 * s.n + t - 1)
                    r = s.slot(2)
                    ps = ps_f[(s.raw + t) % 2]
                    for k, (w, m) in enumerate(((0, 0), (0, 1), (1, 0))):
                        for b in range(2):
                            if t < 2:
                                lo = ROWB * b
                                ins = mm(ps[:, b, 0:HALF], w1_own[w][lo:lo + C + 1, :],
                                         xm[m][lo:lo + C + 1, r, HALF * t:HALF * t + HALF],
                                         start=(k == 0), stop=(k == 2))
                            else:
                                ins = mm(ps[:, b, 0:HALF], w1_both[w][:], xm[m][:, r, HALF * b:HALF * b + HALF],
                                         start=(k == 0), stop=(k == 2))
                    ins.then_inc(S["f1"], 1)

            def respond(s, part):
                if s.real and s.raw % STRIPS == 0:
                    img = s.raw // STRIPS if isinstance(s.i, int) else s.i // 2 + s.raw // STRIPS
                    if part == 0:
                        wait(pe, S["totals"], 2 * img + 2)
                        mm(ps_o[:, 0, HALF:HALF + 1], eye[:], total[:, 0:1], start=True, stop=True)
                        mm(ps_o[:, 0, HALF + 1:HALF + 2], twins[:], total[:, 2:3], start=True, stop=True
                           ).then_inc(S["pairs"], 1)
                    elif part == 1:
                        wait(pe, S["gx_made"], img + 1)
                        mm(ps_o[:, 0, HALF + 2:HALF + 3], mean_all[:], gx[:, 0:1], start=True, stop=False)
                        mm(ps_o[:, 0, HALF + 2:HALF + 3], mean_top[:], gx[:, 1:2], start=False, stop=True
                           ).then_inc(S["mean_ps"], 1)
                    else:
                        wait(pe, S["w2_scaled"], 2 * img + 2)

            def fc2(s):
                if s.real:
                    p = s.raw // STRIPS % 2
                    slot = s.raw % RING
                    wait(pe, S["out_made"], s.n)
                    for b in range(2):
                        cols = slice(HALF * b, HALF * b + HALF)
                        mm(ps_o[0:ROWB + C, b, 0:HALF], w2s_both[:, p, :], G[:, slot, 2, cols], start=True, stop=False)
                        for g in range(2):
                            lo = ROWB * g
                            ins = mm(ps_o[lo:lo + C, b, 0:HALF], w2s_own[:, p, :], G[:, slot, g, cols],
                                     start=False, stop=True)
                    ins.then_inc(S["f2"], 1)

            def step(s):
                nxt, old = s.at(2), s.at(-LAG)
                centre(nxt)
                fc1(s, 0)
                respond(old, 0)
                fc1(s, 1)
                variance(nxt)
                respond(old, 1)
                fc1(s, 2)
                respond(old, 2)
                fc2(old)

            steps(pe, step, N + LAG)

def constants():
    import numpy as np

    f = np.float32
    out = {}
    center = np.zeros((R, R), f)
    spread = [np.zeros((R, R), f) for _ in range(2)]
    for g in range(2):
        lo = ROWB * g
        center[lo:lo + C, lo:lo + C] = np.eye(C) - 1.0 / C
        center[lo + C, lo + C] = 1.0
        for a, eps in ((0, EPS0), (1, EPS1)):
            spread[a][lo:lo + C, lo:lo + C] = 1.0 / C
            spread[a][lo + C, lo + C] = 1.0 - eps
    out["center"] = center
    sums = np.zeros((R, 2, R), f)
    eps0 = np.full((R, 1), EPS0, f)
    for g in range(2):
        lo = ROWB * g
        sums[lo:lo + C, :, lo:lo + C] = 1
        sums[lo + C, 1, lo + C] = C
        eps0[lo + C] = 0
    out["sums"] = sums.reshape(R, 2 * R)
    out["eps0"] = eps0
    out["spread0"], out["spread1"] = spread
    out["eye_c"] = np.eye(C, C + 1, dtype=f)
    out["last_row"] = np.eye(1, C + 1, C, dtype=f)
    pick_q, pick_k = np.zeros((R, R), f), np.zeros((R, KEYS), f)
    ones, minus = np.zeros((R, KEYS), f), np.zeros((R, TOK), f)
    for j in range(TOK):
        for lo in (0, ROWB):
            pick_q[lo + j, [j, ROWB + j]] = 1
            pick_k[lo + j, [j, TOK + j]] = 1
            minus[lo + j, j] = -1
    for g in range(2):
        ones[ROWB * g:ROWB * g + TOK, TOK * g:TOK * g + TOK] = 1
    out["picks"] = np.concatenate([pick_q, pick_k, ones, minus], 1)
    key_ones = np.zeros((KEYS, 2 * DH), f)
    for g in range(2):
        key_ones[TOK * g:TOK * g + TOK, DH * g:DH * g + DH] = 1
    out["key_ones"] = key_ones
    out["eye"] = np.eye(128, dtype=f)
    p = np.arange(128)
    out["twins"] = (p[:, None] % F2 == p[None, :] % F2).astype(f)
    out["mean_all"] = np.full((128, 128), 1.0 / HID, f)
    out["mean_top"] = np.where(p[:, None] < F2, f(1.0 / HID), f(0)) * np.ones((1, 128), f)
    true_row = (np.arange(IMG) + SHIFT) % IMG
    dy = true_row[None, :] - true_row[:, None] + SHIFT
    one = 0x3F80
    out["bands"] = ((dy[None] == np.arange(WS)[:, None, None]) * one).astype(np.uint16)
    return out


def windows_first(x):
    import numpy as np

    b = x.shape[0]
    x = np.roll(x, (-SHIFT, -SHIFT), axis=(2, 3))
    x = x.reshape(b, C, 2, STRIPS, WS, WINS, WS)
    return np.ascontiguousarray(x.transpose(0, 3, 2, 1, 5, 4, 6)).reshape(b * STRIPS, 2, C, STRIP)


def program(nc, x_in, prm, con, out_dram, images):
    scratch = {}
    for name, shape in (("x2_scratch", (images, C, PLANE)), ("y_scratch", (images, C, PLANE)),
                        ("table_0", (HEADS, REL)), ("table_1", (HEADS, REL)),
                        ("table_runs_0", (HEADS, TOK, RUN)), ("table_runs_1", (HEADS, TOK, RUN))):
        scratch[name] = nc.dram_tensor(name, shape, F32, kind="Internal").ap()
    layer0 = {k[8:]: v for k, v in prm.items() if k.startswith("L0_conv_")}
    layer1 = {k[8:]: v for k, v in prm.items() if k.startswith("L1_conv_")}
    with ExitStack() as ctx:
        def sb(name, shape, dt=F32):
            return ctx.enter_context(nc.sbuf_tensor(name, shape, dt))

        tiles, zeros, loads = response_weights(nc, sb, layer1, con)
        later = {name: ctx.enter_context(nc.semaphore("later_" + name)) for name in ("cleared", "loaded")}
        with ExitStack() as inner:
            bands, taps = convolution_weights(
                nc, lambda name, shape, dt: inner.enter_context(nc.sbuf_tensor(name, shape, dt)),
                layer1["dw_w"], con["bands"])
            later["zeros"] = bands["zeros"] + zeros
            later["loads"] = taps + loads
            attention_phase(nc, x_in, layer0, con, [scratch[f"table_{side}"] for side in range(2)],
                            [scratch[f"table_runs_{side}"] for side in range(2)], scratch["x2_scratch"],
                            STRIPS * images, later)
            convolution_phase(nc, bands, later, scratch["x2_scratch"], scratch["y_scratch"], images)
        response_phase(nc, tiles, later, scratch["x2_scratch"], scratch["y_scratch"], out_dram, STRIPS * images)


def kernel(**inputs):
    import numpy as np
    import concourse.bacc as bacc
    from concourse.bass_utils import run_bass_kernel_spmd

    nc = bacc.Bacc("TRN2", target_bir_lowering=False, num_devices=1)
    images = inputs["x"].shape[0]
    arrays, prm, con = {}, {}, {}

    def give(name, a):
        arrays[name] = a
        return nc.dram_tensor(name, a.shape, mybir.dt.from_np(a.dtype), kind="ExternalInput").ap()

    x_in = give("x_windows", windows_first(np.asarray(inputs["x"])))
    for name, a in inputs.items():
        if name != "x":
            prm[name] = give(name, np.ascontiguousarray(a))
    for name, a in constants().items():
        con[name] = give("const_" + name, a)
    out = nc.dram_tensor("out_rolled", (images, C, PLANE), F32, kind="ExternalOutput").ap()
    program(nc, x_in, prm, con, out, images)
    result = run_bass_kernel_spmd(nc, [arrays], core_ids=[0]).results[0]["out_rolled"]
    return np.roll(result.reshape(images, C, IMG, IMG), (SHIFT, SHIFT), axis=(2, 3))
```

```python
from contextlib import ExitStack

import concourse.bass as bass
from concourse import mybir

F32 = mybir.dt.float32
BF16 = mybir.dt.bfloat16
ALU = mybir.AluOpType
ACT = mybir.ActivationFunctionType
AX_X = mybir.AxisListType.X

C = 48
HID = 192
IMG = 112
WS = 7
TOK = WS * WS
HEADS = 3
DH = C // HEADS
SHIFT = WS // 2
PLANE = IMG * IMG
STRIP = WS * IMG
WINS = IMG // WS
STRIPS = IMG // WS // 2
HALF = STRIP // 2
QUADS = 4
QP = WINS // QUADS
HQ = HEADS * TOK
ROWB = 64
ONE = C
R = ROWB + C + 1
KEYS = 2 * TOK
F1 = 128
F2 = HID - F1
EPS0 = 1e-5
EPS1 = 1e-6
PAD = IMG + 2 * SHIFT
SPAN = 2 * WS - 1
REL = SPAN ** 2
RUN = SPAN * (WS - 1) + WS


def wait(eng, sem, value):
    if not isinstance(value, int) or value > 0:
        eng.wait_ge(sem, value)


class Strip:

    def __init__(self, i, raw, total):
        self.i, self.raw, self.total = i, raw, total

    def at(self, d):
        return Strip(self.i, self.raw + d, self.total)

    @property
    def n(self):
        return 4 * self.i + self.raw

    @property
    def real(self):
        return not isinstance(self.i, int) or 0 <= self.raw < self.total

    def slot(self, ring):
        return self.raw % ring

    def turn(self, ring):
        return (4 // ring) * self.i + self.raw // ring


def attention_phase(nc, x_in, prm, con, tables, table_runs, x2_dram, strips, later):
    with ExitStack() as ctx:
        def sb(name, shape, dt=F32):
            return ctx.enter_context(nc.sbuf_tensor(name, shape, dt))

        def sem(name):
            return ctx.enter_context(nc.semaphore(name))

        ps_s = ctx.enter_context(nc.psum_tensor("ps_s", [128, 2, 512], F32))
        ps_t = ctx.enter_context(nc.psum_tensor("ps_t", [128, 2, 512], F32))
        ps_v = ctx.enter_context(nc.psum_tensor("ps_v", [128, 512], F32))
        ps_o = ctx.enter_context(nc.psum_tensor("ps_o", [128, 512], F32))
        ps_m = ctx.enter_context(nc.psum_tensor("ps_m", [128, 2, 512], F32))

        center = sb("center", [R, R])
        sums_f = sb("sums_f", [R, 2, R])
        sum_w = later["sum_w"]
        eye_c = sb("eye_c", [C, C + 1])
        last_row = sb("last_row", [1, C + 1])
        const_f = sb("const_f", [R, R + KEYS + KEYS + TOK])
        const_b = sb("const_b", [R, R + KEYS + KEYS + TOK], BF16)
        pick_q = const_b[:, 0:R]
        pick_k = const_b[:, R:R + KEYS]
        group_ones = const_b[:, R + KEYS:R + 2 * KEYS]
        minus_eye = const_b[:, R + 2 * KEYS:R + 2 * KEYS + TOK]
        key_ones = sb("key_ones", [KEYS, 2 * DH])
        qkv_w = sb("qkv_w", [C, 3 * C])
        fc1_w = sb("fc1_w", [C, HID])
        rows = sb("rows", [1, 3 * C + HID])
        norms = sb("norms", [C, 4])
        aug = sb("aug", [C, 2, C + 1])
        qk_aug = sb("qk_aug", [DH, 2 * HEADS, C + 1])
        gram = [sb(f"gram_{p}", [R, HEADS, R], BF16) for p in "hl"]
        wv = [sb(f"wv_{p}", [R, 2 * C], BF16) for p in "hl"]
        w1_own = [sb(f"w1_own_{p}", [R, F1], BF16) for p in "hl"]
        w1_both = [sb(f"w1_both_{p}", [R, 2 * F2], BF16) for p in "hl"]
        proj_w = sb("proj_w", [2 * C, R])
        proj_b = sb("proj_b", [R, 1])
        fc2_b = sb("fc2_b", [R, 1])
        out_b = sb("out_b", [R, 1])
        centred_b = sb("centred_b", [R, 1])
        w2_own = sb("w2_own", [F1, C])
        w2_both = sb("w2_both", [2 * F2, ROWB + C])
        bias_f = sb("bias_f", [R, 2, HQ])
        bias = sb("bias", [R, 2, HQ], BF16)
        eps = sb("eps", [R, 1])
        xb = [sb(f"xb_{p}", [R, STRIP], BF16) for p in "hl"]
        x1b = [sb(f"x1b_{p}", [R, STRIP], BF16) for p in "hl"]
        sqb = [[sb(f"sqb{a}_{p}", [R, STRIP], BF16) for p in "hl"] for a in range(2)]

        X = sb("X", [R, 4, STRIP])
        x1 = sb("x1", [R, 2, STRIP])
        x2 = sb("x2", [R, 2, STRIP])
        xc = [sb(f"xc{a}", [R, STRIP]) for a in range(2)]
        sq = [sb(f"sq{a}", [R, STRIP]) for a in range(2)]
        lnv = [sb(f"lnv{a}", [R, STRIP]) for a in range(2)]
        rs = [sb(f"rs{a}", [R, STRIP]) for a in range(2)]
        xh = [sb(f"xh{a}", [R, STRIP]) for a in range(2)]
        xm = [[sb(f"xm{a}_{p}", [R, 2, STRIP], BF16) for p in "hl"] for a in range(2)]
        xs = [sb(f"xs_{p}", [R, 2, WINS, KEYS], BF16) for p in "hl"]
        U = [sb(f"u_{p}", [R, 2, HEADS, STRIP], BF16) for p in "hl"]
        qmax = sb("qmax", [R, 2, QP * HEADS])
        shift = sb("shift", [R, 2, QP * HEADS, TOK], BF16)
        P = sb("P", [KEYS, 2, QP, HEADS, TOK])
        V = sb("V", [KEYS, 2, QP, 2 * C])
        lden = sb("lden", [2 * C, QP * TOK])
        rden = sb("rden", [2 * C, 2, QP * TOK])
        O = sb("O", [2 * C, 2, STRIP])
        G = sb("G", [128, 2, 3, STRIP])

        loaded = sem("loaded")
        norm_loaded = sem("norm_loaded")
        sums_ready = sem("sums_ready")
        bias_loaded = sem("bias_loaded")
        x_cleared = sem("x_cleared")
        xs_cleared = sem("xs_cleared")
        table_turned = sem("table_turned")
        runs_made = sem("runs_made")
        setup_v = sem("setup_v")
        setup_t = sem("setup_t")
        cleared = sem("cleared")
        x_loaded = [sem(f"x_loaded{r}") for r in range(4)]
        x2_stored = [sem(f"x2_stored{r}") for r in range(2)]
        names = ("cen var uu s_q st_q v_q pv_q proj f1 f2 xc xh hi xs_copied u_lo mx nrm x1_made "
                 "x2_made sq ln rs u_hi ex vev lnd rdn ge lo md x_hi x_lo x1_hi x1_lo sq_hi sq_lo").split()
        pair = {"cen", "var", "xc", "xh", "hi", "sq", "ln", "rs", "lo", "sq_hi", "sq_lo"}
        S = {}
        for nm in names:
            S[nm] = [sem(f"{nm}{a}_done") for a in range(2)] if nm in pair else sem(f"{nm}_done")

        def halves(ap):
            return ap.rearrange("p (b n) -> p b n", b=2)

        N = strips
        CLEARS = 13
        SETUP_V = 5 + 2 + 2 + 16
        BIAS_V = SETUP_V + 4

        LOOPED = 4
        TURNS = (N - 2 - LOOPED) // 4

        def steps(eng, step, first, last):
            for raw in range(first, LOOPED):
                step(Strip(0, raw, N))
            with eng.Fori(0, TURNS) as i:
                for u in range(4):
                    step(Strip(i, LOOPED + u, N))
            for raw in range(LOOPED + 4 * TURNS, last):
                step(Strip(0, raw, N))

        def unless_first(s):
            return s if not isinstance(s.n, int) or s.n != 0 else Strip(0, -1, N)

        x2_strips = x2_dram.rearrange("b c (g s n) -> b s g c n", g=2, s=STRIPS)

        norm_loads = [(sums_f[:].rearrange("p a c -> p (a c)"), con["sums"]), (eps[:], con["eps0"])]
        loads = [
            (center[:], con["center"]), (const_f[:], con["picks"]), (eye_c[:], con["eye_c"]), (last_row[:], con["last_row"]),
            (key_ones[:], con["key_ones"]), (qkv_w[:], prm["qkv_w"]), (fc1_w[:], prm["fc1_w"]), (w2_own[:], prm["fc2_w"][0:F1, :]),
            (rows[0:1, 0:3 * C], prm["qkv_b"].unsqueeze(0)), (rows[0:1, 3 * C:], prm["fc1_b"].unsqueeze(0)),
        ]
        loads += [(norms[:, k:k + 1], prm[nm].unsqueeze(1))
                  for k, nm in enumerate(("norm1_g", "norm1_b", "norm2_g", "norm2_b"))]
        for g in range(2):
            lo = ROWB * g
            loads += [(proj_b[lo:lo + C, :], prm["proj_b"].unsqueeze(1)),
                      (fc2_b[lo:lo + C, :], prm["fc2_b"].unsqueeze(1)),
                      (w2_both[F2 * g:F2 * g + F2, lo:lo + C], prm["fc2_w"][F1:HID, :])]
            loads += [(proj_w[2 * DH * h + DH * g:2 * DH * h + DH * g + DH, lo:lo + C],
                       prm["proj_w"][DH * h:DH * h + DH, :]) for h in range(HEADS)]
        runs_of_rows = []
        for side in range(2):
            for a in range(WS):
                src = bass.AP(tensor=tables[side].tensor, offset=(WS - 1 - a) * SPAN + WS - 1,
                              ap=[[REL, HEADS], [-1, WS], [1, RUN]])
                runs_of_rows.append((table_runs[side][:, WS * a:WS * a + WS, :], src))
        blocks = []
        for side in range(2):
            for h in range(HEADS):
                src = bass.AP(tensor=table_runs[side].tensor, offset=h * TOK * RUN,
                              ap=[[RUN, TOK], [SPAN, WS], [1, WS]])
                dst = bias_f[0:TOK, side, TOK * h:TOK * h + TOK]
                blocks.append((dst.rearrange("p (a b) -> p a b", a=WS), src))

        block = ctx.enter_context(nc.Block())

        @block.sync
        def _(sp):
            for tab, first, sign in ((tables[0], (REL - 1) * HEADS, -1), (tables[1], 0, 1)):
                sp.dma_start(tab, bass.AP(tensor=prm["rel_bias_table"].tensor, offset=first,
                                          ap=[[1, HEADS], [sign * HEADS, REL], [1, 1]]),
                             allow_slow_non_contiguous=True).then_inc(table_turned, 16)

            def x_load(s):
                if s.real:
                    wait(sp, S["x1_made"], 2 * (s.n - 3))
                    for g in range(2):
                        sp.dma_start(X[ROWB * g:ROWB * g + C, s.slot(4), :],
                                     x_in[s.n, g]).then_inc(x_loaded[s.slot(4)], 16)

            def x2_store(s):
                if s.real:
                    wait(sp, S["x2_made"], 2 * s.n + 2)
                    for g in range(2):
                        dst = x2_strips[s.n // STRIPS, s.n % STRIPS, g]
                        sp.dma_start(dst, x2[ROWB * g:ROWB * g + C, s.slot(2), :]
                                     ).then_inc(x2_stored[s.slot(2)], 16)

            sp.wait_ge(x_cleared, 4)
            x_load(Strip(0, 0, N))
            for dst, src in norm_loads:
                sp.dma_start(dst, src).then_inc(norm_loaded, 16)
            sp.wait_ge(cleared, CLEARS)
            for dst, src in loads:
                sp.dma_start(dst, src).then_inc(loaded, 16)
            sp.wait_ge(table_turned, 32)
            for dst, src in runs_of_rows:
                sp.dma_start(dst, src).then_inc(runs_made, 16)
            x_load(Strip(0, 1, N))
            sp.wait_ge(runs_made, 16 * len(runs_of_rows))
            for dst, src in blocks:
                sp.dma_start(dst, src).then_inc(bias_loaded, 16)
            sp.wait_ge(later["cleared"], len(later["zeros"]))
            for dst, src in later["loads"]:
                sp.dma_start(dst, src).then_inc(later["loaded"], 16)

            def step(s):
                x_load(s.at(2))
                x2_store(s.at(-2))

            steps(sp, step, 0, N + 2)
            for r in range(2):
                sp.wait_ge(x2_stored[r], 32 * (N // 2))

        @block.gpsimd
        def _(pool):
            for t in (proj_w, proj_b, fc2_b, w2_both, bias_f, *gram, *wv, *w1_own, *w1_both):
                nc.gpsimd.memset(t[:], 0.0).then_inc(cleared, 1)
            for t in xs:
                nc.gpsimd.memset(t[:], 0.0).then_inc(xs_cleared, 1)
            for t in later["zeros"]:
                nc.gpsimd.memset(t, 0.0).then_inc(later["cleared"], 1)

            def low(a, s):
                if s.real:
                    wait(pool, S["hi"][a], s.n + 1)
                    wait(pool, (S["uu"], S["f1"])[a], 6 * (s.n - 1))
                    if a == 0:
                        wait(pool, S["xs_copied"], 4 * (s.n - 1))
                    r = s.slot(2)
                    nc.gpsimd.tensor_tensor(xm[a][1][:, r, :], xh[a][:], xm[a][0][:, r, :],
                                            ALU.subtract).then_inc(S["lo"][a], 1)

            def make_shift(s, j):
                if s.real:
                    q = 4 * s.n + j
                    wait(pool, S["mx"], q + 1)
                    wait(pool, S["st_q"], q - 1)
                    m = qmax[:, j % 2, :].unsqueeze(2).to_broadcast([R, QP * HEADS, TOK])
                    e = minus_eye.unsqueeze(1).to_broadcast([R, QP * HEADS, TOK])
                    nc.gpsimd.tensor_tensor(shift[:, j % 2], e, m, ALU.mult).then_inc(S["md"], 1)

            def x_low(s):
                if s.real:
                    wait(pool, S["x_hi"], s.n + 1)
                    wait(pool, S["cen"][0], 2 * s.n)
                    nc.gpsimd.tensor_tensor(xb[1][:], X[:, s.slot(4), :], xb[0][:], ALU.subtract
                                            ).then_inc(S["x_lo"], 1)

            def squares_low(a, s):
                if s.real:
                    wait(pool, S["var"][a], 2 * s.n)
                    for b in range(2):
                        cols = slice(HALF * b, HALF * b + HALF)
                        wait(pool, S["sq_hi"][a], 2 * s.n + b + 1)
                        nc.gpsimd.tensor_tensor(sqb[a][1][:, cols], sq[a][:, cols], sqb[a][0][:, cols], ALU.subtract
                                                ).then_inc(S["sq_lo"][a], 1)

            def x1_low(s):
                if s.real:
                    wait(pool, S["cen"][1], 2 * s.n)
                    for b in range(2):
                        cols = slice(HALF * b, HALF * b + HALF)
                        wait(pool, S["x1_hi"], 2 * s.n + b + 1)
                        nc.gpsimd.tensor_tensor(x1b[1][:, cols], x1[:, s.slot(2), cols], x1b[0][:, cols], ALU.subtract
                                                ).then_inc(S["x1_lo"], 1)

            x_low(Strip(0, 0, N))
            squares_low(0, Strip(0, 0, N))

            def step(s):
                old, prv, nxt, nx2 = s.at(-2), s.at(-1), s.at(1), s.at(2)
                low(0, nxt)
                x1_low(prv)
                make_shift(s, 2)
                squares_low(1, prv)
                x_low(unless_first(nx2))
                make_shift(s, 3)
                low(1, prv)
                make_shift(nxt, 0)
                squares_low(0, unless_first(nx2))
                make_shift(nxt, 1)

            steps(pool, step, -1, N + 2)

        @block.vector
        def _(dve):
            chain = [0]

            def link(ins):
                chain[0] += 1
                ins.then_inc(setup_v, 1)
                return chain[0]

            def x_high(s):
                if s.real:
                    wait(dve, x_loaded[s.slot(4)], 32 * (s.turn(4) + 1))
                    wait(dve, S["cen"][0], 2 * s.n)
                    nc.vector.tensor_copy(xb[0][:], X[:, s.slot(4), :]).then_inc(S["x_hi"], 1)

            def subtract_mean(a, s):
                if s.real:
                    for b in range(2):
                        wait(dve, S["cen"][a], 2 * s.n + b + 1)
                        cols = slice(HALF * b, HALF * b + HALF)
                        src = (X[:, s.slot(4), cols], x1[:, s.slot(2), cols])[a]
                        nc.vector.scalar_tensor_tensor(
                            out=xc[a][:, cols], in0=ps_m[0:R, b, 0:HALF], scalar=-1.0 / C, in1=src,
                            op0=ALU.mult, op1=ALU.add).then_inc(S["xc"][a], 1)

            def squares_high(a, s):
                if s.real:
                    wait(dve, S["var"][a], 2 * s.n)
                    for b in range(2):
                        cols = slice(HALF * b, HALF * b + HALF)
                        wait(dve, S["sq"][a], 2 * s.n + b + 1)
                        nc.vector.tensor_copy(sqb[a][0][:, cols], sq[a][:, cols]).then_inc(S["sq_hi"][a], 1)

            def normalise(a, s):
                if s.real:
                    wait(dve, S["rs"][a], s.n + 1)
                    wait(dve, S["lo"][a], s.n)
                    if a == 0:
                        ins = nc.vector.tensor_tensor(xh[0][:], xc[0][:], rs[0][:], ALU.mult)
                    else:
                        ins = nc.vector.scalar_tensor_tensor(out=xh[1][:], in0=xc[1][:], scalar=centred_b[:, 0:1],
                                                             in1=rs[1][:], op0=ALU.add, op1=ALU.mult)
                    ins.then_inc(S["xh"][a], 1)
                    wait(dve, S["xh"][a], s.n + 1)
                    if a == 0:
                        wait(dve, S["s_q"], 4 * (s.n - 1))
                    else:
                        wait(dve, S["f1"], 6 * (s.n - 1))
                    nc.vector.tensor_copy(xm[a][0][:, s.slot(2), :], xh[a][:]).then_inc(S["hi"][a], 1)

            for r in range(4):
                nc.vector.memset(X[:, r, :], 1.0).then_inc(x_cleared, 1)
            dve.wait_ge(norm_loaded, 16 * len(norm_loads))
            nc.vector.tensor_copy(sum_w[:], sums_f[:]).then_inc(sums_ready, 1)
            x_high(Strip(0, 0, N))
            subtract_mean(0, Strip(0, 0, N))
            squares_high(0, Strip(0, 0, N))
            dve.wait_ge(cleared, CLEARS)
            dve.wait_ge(loaded, 16 * len(loads))
            link(nc.vector.tensor_copy(const_b[:], const_f[:]))
            for a in range(2):
                link(nc.vector.tensor_scalar(aug[:, a, 0:C], eye_c[:, 0:C], norms[:, 2 * a:2 * a + 1], None, ALU.mult))
                link(nc.vector.tensor_copy(aug[:, a, C:C + 1], norms[:, 2 * a + 1:2 * a + 2]))
            dve.wait_ge(setup_t, 1)
            qk = ps_t[0:DH, 0, 0:6 * (C + 1)].rearrange("p (a c) -> p a c", a=6)
            k = link(nc.vector.tensor_scalar(qk_aug[:, 0:HEADS, :], qk[:, 0:HEADS, :], DH ** -0.5, None, ALU.mult))
            k = link(nc.vector.tensor_copy(qk_aug[:, HEADS:, :], qk[:, HEADS:, :]))
            dve.wait_ge(setup_t, 2)
            link(nc.vector.tensor_scalar(centred_b[:], ps_v[0:R, 0:1], -1.0, None, ALU.mult))
            link(nc.vector.tensor_tensor(out_b[:], proj_b[:], fc2_b[:], ALU.add))
            splits = []
            for g in range(2):
                lo = ROWB * g
                src_g = ps_s[lo:lo + C + 1, 0, 0:HEADS * (C + 1)].rearrange("p (h c) -> p h c", h=HEADS)
                splits.append((gram, lambda t, lo=lo: t[lo:lo + C + 1, :, lo:lo + C + 1], src_g))
                src_v = ps_s[lo:lo + C + 1, 1, 0:C].rearrange("p (h d) -> p h d", h=HEADS)
                splits.append((wv, lambda t, lo=lo, g=g: t[lo:lo + C + 1, :].rearrange(
                    "p (h g d) -> p h g d", h=HEADS, g=2)[:, :, g, :], src_v))
                splits.append((w1_own, lambda t, lo=lo: t[lo:lo + C + 1, :], ps_s[lo:lo + C + 1, 1, C:C + F1]))
                splits.append((w1_both, lambda t, lo=lo, g=g: t[lo:lo + C + 1, F2 * g:F2 * g + F2],
                               ps_s[lo:lo + C + 1, 1, C + F1:C + HID]))
            for pair_, view, src in splits:
                k = link(nc.vector.tensor_copy(view(pair_[0]), src))
                dve.wait_ge(setup_v, k)
                k = link(nc.vector.tensor_tensor(view(pair_[1]), src, view(pair_[0]), ALU.subtract))
            normalise(0, Strip(0, 0, N))
            dve.wait_ge(bias_loaded, 16 * len(blocks))
            k = link(nc.vector.tensor_copy(bias_f[ROWB:ROWB + TOK], bias_f[0:TOK]))
            dve.wait_ge(setup_v, k)
            link(nc.vector.tensor_copy(bias[:], bias_f[:]))
            dve.wait_ge(setup_v, k + 1)
            k = link(nc.vector.tensor_tensor(bias_f[ROWB:R], bias_f[ROWB:R], bias[ROWB:R], ALU.subtract))
            dve.wait_ge(setup_v, k)
            k = link(nc.vector.tensor_copy(bias[ROWB:R], bias_f[ROWB:R]))

            def block_diagonal(p, s):
                if s.real:
                    if isinstance(s.n, int) and s.n < 2:
                        wait(dve, xs_cleared, 2)
                    wait(dve, (S["hi"], S["lo"])[p][0], s.n + 1)
                    wait(dve, S["st_q"], 4 * (s.n - 1))
                    wait(dve, S["v_q"], 4 * (s.n - 1))
                    for g in range(2):
                        lo = ROWB * g
                        nc.vector.tensor_copy(
                            xs[p][lo:lo + C + 1, s.slot(2), :, TOK * g:TOK * g + TOK],
                            xm[0][p][lo:lo + C + 1, s.slot(2), :].rearrange("p (w t) -> p w t", t=TOK),
                        ).then_inc(S["xs_copied"], 1)

            def u_low(s, h):
                if s.real:
                    r = s.slot(2)
                    for b in range(2):
                        wait(dve, S["u_hi"], 6 * s.n + 2 * h + b + 1)
                        cols = slice(HALF * b, HALF * b + HALF)
                        nc.vector.tensor_tensor(U[1][:, r, h, cols], ps_m[0:R, b, 0:HALF], U[0][:, r, h, cols],
                                                ALU.subtract).then_inc(S["u_lo"], 1)

            def query_max(s, j):
                if s.real:
                    q = 4 * s.n + j
                    wait(dve, S["s_q"], q + 1)
                    wait(dve, S["md"], q - 1)
                    nc.vector.tensor_reduce(
                        qmax[:, j % 2, :].rearrange("p (b n) -> p b n", b=2),
                        ps_s[0:R, :, 0:2 * HQ].rearrange("p b (n t) -> p b n t", t=TOK),
                        AX_X, ALU.max).then_inc(S["mx"], 1)

            def divide(s, j):
                if s.real:
                    q = 4 * s.n + j
                    wait(dve, S["rdn"], q + 1)
                    wait(dve, S["proj"], 2 * (s.n - 1))
                    W = QP * TOK
                    nc.vector.tensor_tensor(O[:, s.slot(2), W * j:W * j + W], ps_o[0:2 * C, 0:W],
                                            rden[:, j % 2, :], ALU.mult).then_inc(S["nrm"], 1)

            def first_residual(s):
                if s.real:
                    wait(dve, S["cen"][1], 2 * s.n)
                    for b in range(2):
                        wait(dve, S["proj"], 2 * s.n + b + 1)
                        cols = slice(HALF * b, HALF * b + HALF)
                        half = x1[:, s.slot(2), cols]
                        nc.vector.scalar_tensor_tensor(
                            out=half, in0=ps_m[0:R, b, 0:HALF], scalar=out_b[:, 0:1],
                            in1=X[:, s.slot(4), cols], op0=ALU.add, op1=ALU.add).then_inc(S["x1_made"], 1)
                        wait(dve, S["x1_made"], 2 * s.n + b + 1)
                        nc.vector.tensor_copy(x1b[0][:, cols], half).then_inc(S["x1_hi"], 1)

            def second_residual(s):
                if s.real:
                    wait(dve, x2_stored[s.slot(2)], 32 * s.turn(2))
                    n = ROWB + C
                    for b in range(2):
                        wait(dve, S["f2"], 2 * s.n + b + 1)
                        win = slice(WINS // 2 * b, WINS // 2 * b + WINS // 2)
                        out = x2[0:n, s.slot(2), :].rearrange("p (i w j) -> p w i j", i=WS, j=WS)[:, win]
                        nc.vector.tensor_tensor(
                            out, ps_m[0:n, b, 0:HALF].rearrange("p (w i j) -> p w i j", i=WS, j=WS),
                            x1[0:n, s.slot(2), :].rearrange("p (w i j) -> p w i j", i=WS, j=WS)[:, win],
                            ALU.add).then_inc(S["x2_made"], 1)

            def step(s):
                old, prv, nxt, nx2 = s.at(-2), s.at(-1), s.at(1), s.at(2)
                second_residual(old)
                first_residual(prv)
                query_max(s, 2)
                u_low(nxt, 0)
                divide(s, 0)
                subtract_mean(1, prv)
                block_diagonal(1, nxt)
                squares_high(1, prv)
                x_high(unless_first(nx2))
                u_low(nxt, 1)
                block_diagonal(0, nxt)
                query_max(s, 3)
                divide(s, 1)
                normalise(1, prv)
                u_low(nxt, 2)
                subtract_mean(0, unless_first(nx2))
                divide(s, 2)
                query_max(nxt, 0)
                squares_high(0, unless_first(nx2))
                query_max(nxt, 1)
                normalise(0, unless_first(nx2))
                divide(s, 3)

            steps(dve, step, -1, N + 2)

        @block.scalar
        def _(act):
            act.wait_ge(norm_loaded, 16 * len(norm_loads))

            def square(a, s):
                if s.real:
                    wait(act, S["sq_lo"][a], 2 * s.n)
                    for b in range(2):
                        wait(act, S["xc"][a], 2 * s.n + b + 1)
                        cols = slice(HALF * b, HALF * b + HALF)
                        if a == 0:
                            ins = nc.scalar.activation(sq[0][:, cols], xc[0][:, cols], ACT.Square)
                        else:
                            ins = nc.scalar.activation(sq[1][:, cols], xc[1][:, cols], ACT.Square,
                                                       bias=centred_b[:, 0:1])
                        ins.then_inc(S["sq"][a], 1)

            def root(a, s):
                if s.real:
                    for b in range(2):
                        wait(act, S["var"][a], 2 * s.n + b + 1)
                        nc.scalar.activation(lnv[a][:, HALF * b:HALF * b + HALF], ps_m[0:R, b, 0:HALF], ACT.Ln,
                                             scale=1.0 / C, bias=eps[:, 0:1]).then_inc(S["ln"][a], 1)
                    wait(act, S["ln"][a], 2 * s.n + 2)
                    nc.scalar.activation(rs[a][:], lnv[a][:], ACT.Exp, scale=-0.5).then_inc(S["rs"][a], 1)

            def u_high(s, h):
                if s.real:
                    wait(act, S["st_q"], 4 * (s.n - 1))
                    for b in range(2):
                        wait(act, S["uu"], 6 * s.n + 2 * h + b + 1)
                        nc.scalar.copy(U[0][:, s.slot(2), h, HALF * b:HALF * b + HALF], ps_m[0:R, b, 0:HALF]
                                       ).then_inc(S["u_hi"], 1)

            def exp_scores(s, j):
                if s.real:
                    q = 4 * s.n + j
                    wait(act, S["st_q"], q + 1)
                    wait(act, S["pv_q"], q - 1)
                    nc.scalar.activation(P[:, j % 2].rearrange("p (b n) h t -> p b (n h t)", b=2),
                                         ps_t[0:KEYS, :, 0:2 * HQ], ACT.Exp).then_inc(S["ex"], 1)

            def keep_values(s, j):
                if s.real:
                    q = 4 * s.n + j
                    wait(act, S["v_q"], q + 1)
                    wait(act, S["pv_q"], q - 1)
                    nc.scalar.copy(V[:, j % 2].rearrange("p n c -> p (n c)"),
                                   ps_v[0:KEYS, 0:QP * 2 * C]).then_inc(S["vev"], 1)

            def invert_sums(s, j):
                if s.real:
                    q = 4 * s.n + j
                    W = QP * TOK
                    wait(act, S["pv_q"], q + 1)
                    nc.scalar.activation(lden[:], ps_o[0:2 * C, W:2 * W], ACT.Ln).then_inc(S["lnd"], 1)
                    wait(act, S["lnd"], q + 1)
                    wait(act, S["nrm"], q - 1)
                    nc.scalar.activation(rden[:, j % 2, :], lden[:], ACT.Exp, scale=-1.0).then_inc(S["rdn"], 1)

            def gelu(s, t):
                if s.real:
                    wait(act, S["f2"], 2 * (s.n - 1))
                    r = s.slot(2)
                    for b in range(2):
                        wait(act, S["f1"], 6 * s.n + 2 * t + b + 1)
                        if t < 2:
                            out = G[:, r, b, HALF * t:HALF * t + HALF]
                        else:
                            out = G[:, r, 2, HALF * b:HALF * b + HALF]
                        nc.scalar.activation(out, ps_m[:, b, 0:HALF], ACT.Gelu).then_inc(S["ge"], 1)

            def step(s):
                old, prv, nxt, nx2 = s.at(-2), s.at(-1), s.at(1), s.at(2)
                keep_values(s, 0)
                square(0, unless_first(nxt))
                gelu(old, 1)
                gelu(old, 2)
                nc.scalar.preload_act_table_set("natural_log_exp_and_others")
                root(0, unless_first(nxt))
                keep_values(s, 1)
                exp_scores(s, 0)
                invert_sums(prv, 3)
                exp_scores(s, 1)
                invert_sums(s, 0)
                u_high(nxt, 0)
                square(1, prv)
                invert_sums(s, 1)
                u_high(nxt, 1)
                exp_scores(s, 2)
                keep_values(s, 2)
                root(1, prv)
                u_high(nxt, 2)
                keep_values(s, 3)
                exp_scores(s, 3)
                invert_sums(s, 2)
                nc.scalar.preload_act_table_set("gelu_and_others")
                gelu(prv, 0)

            nc.scalar.preload_act_table_set("natural_log_exp_and_others")
            square(0, Strip(0, 0, N))
            root(0, Strip(0, 0, N))
            steps(act, step, -1, N + 2)

        @block.tensor
        def _(pe):
            mm = nc.tensor.matmul
            last = [None, None]

            def free_m(b):
                if last[b] is not None:
                    wait(pe, *last[b])

            def channel_sums(kind, parts, done, s, feeder, emptied):
                for b in range(2):
                    if feeder is not None:
                        wait(pe, feeder, 2 * s.n + b + 1)
                    free_m(b)
                    for m in range(2):
                        ins = mm(ps_m[0:R, b, 0:HALF], sum_w[:, kind, :], parts[m][:, HALF * b:HALF * b + HALF],
                                 start=(m == 0), stop=(m == 1))
                    ins.then_inc(done, 1)
                    last[b] = (emptied, 2 * s.n + b + 1)

            def centre(a, s):
                if s.real:
                    if a == 0:
                        wait(pe, S["x_lo"], s.n + 1)
                        channel_sums(0, xb, S["cen"][0], s, None, S["xc"][0])
                    else:
                        channel_sums(0, x1b, S["cen"][1], s, S["x1_lo"], S["xc"][1])

            def variance(a, s):
                if s.real:
                    channel_sums(1, sqb[a], S["var"][a], s, S["sq_lo"][a], S["ln"][a])

            pe.wait_ge(sums_ready, 1)
            centre(0, Strip(0, 0, N))
            variance(0, Strip(0, 0, N))
            pe.wait_ge(setup_v, 5)
            for k in range(2 * HEADS):
                out = ps_t[0:DH, 0, (C + 1) * k:(C + 1) * (k + 1)]
                mm(out, qkv_w[:, DH * k:DH * k + DH], aug[:, 0, :], start=True, stop=False)
                ins = mm(out, rows[0:1, DH * k:DH * k + DH], last_row[:], start=False, stop=True)
            ins.then_inc(setup_t, 1)
            pe.wait_ge(setup_v, 7)
            mm(ps_v[0:R, 0:1], center[:], fc2_b[:], start=True, stop=True)
            for g in range(2):
                lo = ROWB * g
                for h in range(HEADS):
                    mm(ps_s[lo:lo + C + 1, 0, (C + 1) * h:(C + 1) * (h + 1)], qk_aug[:, h, :],
                       qk_aug[:, HEADS + h, :], start=True, stop=True)
                out = ps_s[lo:lo + C + 1, 1, 0:C]
                mm(out, aug[:, 0, :], qkv_w[:, 2 * C:3 * C], start=True, stop=False)
                mm(out, last_row[:], rows[0:1, 2 * C:3 * C], start=False, stop=True)
                out = ps_s[lo:lo + C + 1, 1, C:C + HID]
                mm(out, aug[:, 1, :], fc1_w[:], start=True, stop=False)
                ins = mm(out, last_row[:], rows[0:1, 3 * C:], start=False, stop=True)
            ins.then_inc(setup_t, 1)
            pe.wait_ge(setup_v, SETUP_V)

            def u_product(s, h):
                if s.real:
                    wait(pe, S["hi"][0], s.n + 1)
                    wait(pe, S["lo"][0], s.n + 1)
                    r = s.slot(2)
                    for b in range(2):
                        free_m(b)
                        for k, (w, m) in enumerate(((0, 0), (0, 1), (1, 0))):
                            ins = mm(ps_m[0:R, b, 0:HALF], gram[w][:, h, :],
                                     xm[0][m][:, r, HALF * b:HALF * b + HALF], start=(k == 0), stop=(k == 2))
                        ins.then_inc(S["uu"], 1)
                        last[b] = (S["u_lo"], 6 * s.n + 2 * h + b + 1)

            def scores_q(s, j):
                if s.real:
                    q = 4 * s.n + j
                    if j == 0:
                        if isinstance(s.n, int) and s.n == 0:
                            wait(pe, setup_v, BIAS_V)
                        wait(pe, S["u_hi"], 6 * s.n + 6)
                        wait(pe, S["hi"][0], s.n + 1)
                    wait(pe, S["mx"], q)
                    r = s.slot(2)
                    for b in range(2):
                        mm(ps_s[0:R, b, 0:2 * HQ], pick_q,
                           bias[:, 0, :].unsqueeze(1).to_broadcast([R, 2, HQ]), start=True, stop=False)
                        for k in range(2):
                            w = QP * j + 2 * b + k
                            for h in range(HEADS):
                                for g in range(2):
                                    lo = ROWB * g
                                    at = HQ * k + TOK * h
                                    ins = mm(ps_s[lo:lo + TOK, b, at:at + TOK],
                                             U[0][lo:lo + C + 1, r, h, TOK * w:TOK * w + TOK],
                                             xm[0][0][lo:lo + C + 1, r, TOK * w:TOK * w + TOK],
                                             start=False, stop=(k == 1 and h == HEADS - 1))
                    ins.then_inc(S["s_q"], 1)

            def scores_k(s, j):
                if s.real:
                    q = 4 * s.n + j
                    if j == 0:
                        wait(pe, S["u_lo"], 6 * s.n + 6)
                        wait(pe, S["xs_copied"], 4 * s.n + 4)
                    wait(pe, S["ex"], q)
                    r = s.slot(2)
                    for b in range(2):
                        mm(ps_t[0:KEYS, b, 0:2 * HQ], pick_k,
                           bias[:, 1, :].unsqueeze(1).to_broadcast([R, 2, HQ]), start=True, stop=False)
                        for k in range(2):
                            w = QP * j + 2 * b + k
                            for ws, ms in ((0, 0), (0, 1), (1, 0)):
                                mm(ps_t[0:KEYS, b, HQ * k:HQ * k + HQ], xs[ws][:, r, w, :],
                                   U[ms][:, r, :, TOK * w:TOK * w + TOK], start=False, stop=False)

            def shift_scores(s, j):
                if s.real:
                    q = 4 * s.n + j
                    wait(pe, S["md"], q + 1)
                    for b in range(2):
                        ins = mm(ps_t[0:KEYS, b, 0:2 * HQ], group_ones,
                                 shift[:, j % 2, 2 * HEADS * b:2 * HEADS * (b + 1), :], start=False, stop=True)
                    ins.then_inc(S["st_q"], 1)

            def values(s, j):
                if s.real:
                    q = 4 * s.n + j
                    if j == 0:
                        wait(pe, S["xs_copied"], 4 * s.n + 4)
                    wait(pe, S["vev"], q)
                    r = s.slot(2)
                    for k in range(QP):
                        for n, (ws, ms) in enumerate(((0, 0), (1, 0), (0, 1))):
                            ins = mm(ps_v[0:KEYS, 2 * C * k:2 * C * (k + 1)], xs[ws][:, r, QP * j + k, :], wv[ms][:],
                                     start=(n == 0), stop=(n == 2))
                    ins.then_inc(S["v_q"], 1)

            def weigh(s, j):
                if s.real:
                    q = 4 * s.n + j
                    wait(pe, S["ex"], q + 1)
                    wait(pe, S["vev"], q + 1)
                    wait(pe, S["nrm"], q)
                    W = QP * TOK
                    for k in range(QP):
                        for h in range(HEADS):
                            lo = 2 * DH * h
                            mm(ps_o[lo:lo + 2 * DH, TOK * k:TOK * k + TOK], V[:, j % 2, k, lo:lo + 2 * DH],
                               P[:, j % 2, k, h, :], start=True, stop=True)
                    for h in range(HEADS):
                        lo = 2 * DH * h
                        ins = mm(ps_o[lo:lo + 2 * DH, W:2 * W], key_ones[:], P[:, j % 2, :, h, :],
                                 start=True, stop=True)
                    ins.then_inc(S["pv_q"], 1)

            def project(s):
                if s.real:
                    wait(pe, S["nrm"], 4 * s.n + 4)
                    for b in range(2):
                        free_m(b)
                        mm(ps_m[0:R, b, 0:HALF], proj_w[:], O[:, s.slot(2), HALF * b:HALF * b + HALF],
                           start=True, stop=True).then_inc(S["proj"], 1)
                        last[b] = (S["x1_made"], 2 * s.n + b + 1)

            def fc1(s, t):
                if s.real:
                    if t == 0:
                        wait(pe, S["hi"][1], s.n + 1)
                        wait(pe, S["lo"][1], s.n + 1)
                    r = s.slot(2)
                    for b in range(2):
                        free_m(b)
                        for k, (w, m) in enumerate(((0, 0), (0, 1), (1, 0))):
                            if t < 2:
                                lo = ROWB * b
                                ins = mm(ps_m[:, b, 0:HALF], w1_own[w][lo:lo + C + 1, :],
                                         xm[1][m][lo:lo + C + 1, r, HALF * t:HALF * t + HALF],
                                         start=(k == 0), stop=(k == 2))
                            else:
                                ins = mm(ps_m[:, b, 0:HALF], w1_both[w][:],
                                         xm[1][m][:, r, HALF * b:HALF * b + HALF],
                                         start=(k == 0), stop=(k == 2))
                        ins.then_inc(S["f1"], 1)
                        last[b] = (S["ge"], 6 * s.n + 2 * t + b + 1)

            def fc2(s):
                if s.real:
                    wait(pe, S["ge"], 6 * s.n + 6)
                    r = s.slot(2)
                    for b in range(2):
                        free_m(b)
                        cols = slice(HALF * b, HALF * b + HALF)
                        mm(ps_m[0:ROWB + C, b, 0:HALF], w2_both[:], G[:, r, 2, cols], start=True, stop=False)
                        for g in range(2):
                            lo = ROWB * g
                            ins = mm(ps_m[lo:lo + C, b, 0:HALF], w2_own[:], G[:, r, g, cols],
                                     start=False, stop=True)
                        ins.then_inc(S["f2"], 1)
                        last[b] = (S["x2_made"], 2 * s.n + b + 1)

            def step(s):
                old, prv, nxt, nx2 = s.at(-2), s.at(-1), s.at(1), s.at(2)
                if old.real:
                    for b in range(2):
                        last[b] = (S["ge"], 6 * old.n + 4 + b + 1)
                scores_k(s, 0)
                variance(0, unless_first(nxt))
                shift_scores(s, 0)
                values(s, 1)
                scores_q(s, 2)
                fc2(old)
                scores_k(s, 1)
                project(prv)
                shift_scores(s, 1)
                weigh(s, 0)
                u_product(nxt, 0)
                scores_k(s, 2)
                centre(1, prv)
                weigh(s, 1)
                u_product(nxt, 1)
                values(s, 2)
                shift_scores(s, 2)
                scores_q(s, 3)
                variance(1, prv)
                values(s, 3)
                scores_k(s, 3)
                u_product(nxt, 2)
                shift_scores(s, 3)
                weigh(s, 2)
                values(nxt, 0)
                centre(0, unless_first(nx2))
                scores_q(nxt, 0)
                fc1(prv, 0)
                weigh(s, 3)
                fc1(prv, 1)
                scores_q(nxt, 1)
                fc1(prv, 2)

            steps(pe, step, -1, N + 2)


PIECES = 3
ROWS = 32 * (PIECES - 1) + WS
BLOCK = IMG // 2
SEEN = BLOCK + 2 * SHIFT
SIDE = 64
TAPS = WS + 1


def convolution_weights(nc, sb, dw_w, bands):
    hot = sb("hot", [ROWS, BLOCK, SIDE], BF16)
    taps = sb("taps", [ROWS, C, TAPS], F32)
    loads = []
    for k in range(PIECES):
        loads += [(hot[32 * k:32 * k + WS], bands.bitcast(BF16)),
                  (taps[32 * k:32 * k + WS, :, 0:WS], dw_w.rearrange("c o a b -> a (c o) b"))]
    return {"hot": hot, "taps": taps, "zeros": [hot[:], taps[:]]}, loads


def convolution_phase(nc, weights, later, x2_dram, y_dram, images):
    with ExitStack() as ctx:
        def sb(name, shape, dt=F32):
            return ctx.enter_context(nc.sbuf_tensor(name, shape, dt))

        def sem(name):
            return ctx.enter_context(nc.semaphore(name))

        PER = 2
        FILLS = BLOCK // PER
        RING = 4
        AHEAD = RING - 1
        PAIRS = TAPS // 2
        half = images // 2
        back = IMG - SHIFT
        K = SIDE + SEEN

        ps = [ctx.enter_context(nc.psum_tensor(f"conv_ps{r}", [128, 2, 512], F32)) for r in range(4)]
        hot, taps = weights["hot"], weights["taps"]
        rest = sb("rest", [ROWS, C, TAPS])
        piece = [sb(f"piece{k}", [ROWS, C, TAPS], BF16) for k in range(PIECES)]
        split = sb("split", [ROWS, C, TAPS], BF16)
        band = sb("band", [128, 2, C, PAIRS, SIDE], BF16)
        band_now = sb("band_now", [128, RING, 2, PAIRS, SIDE], BF16)
        xin = [sb(f"xin{k}", [SEEN, RING, images, IMG]) for k in range(2)]
        xp = [[sb(f"xp{k}_{p}", [128, RING, images, PAD], BF16) for p in "hl"] for k in range(2)]
        y = sb("y", [128, RING, images, IMG])

        xin_cleared = sem("xin_cleared")
        xp_cleared = sem("xp_cleared")
        band_cleared = sem("band_cleared")
        split_made = sem("split_made")
        band_filled = sem("band_filled")
        band_high = sem("band_high")
        band_low = sem("band_low")
        xin_loaded = [sem(f"xin_loaded{s}") for s in range(RING)]
        xp_high = sem("xp_high")
        xp_low = sem("xp_low")
        xp_shifted = sem("xp_shifted")
        convolved = sem("convolved")
        y_made = sem("y_made")
        y_stored = [sem(f"y_stored{s}") for s in range(RING)]
        block = ctx.enter_context(nc.Block())

        def channels(eng, step, last=C):
            for c in range(RING):
                step(c, c, 0)
            with eng.Fori(1, last // RING) as i:
                for r in range(RING):
                    step(RING * i + r, r, i)

        def runs(k, p, r):
            padded, rolled = xp[k][p][0:SEEN, r], xin[k][:, r]
            return ((padded[:, :, 2 * SHIFT:2 * SHIFT + back], rolled[:, :, 0:back]),
                    (padded[:, :, SHIFT:2 * SHIFT], rolled[:, :, back:IMG]))

        def fill_ps(f):
            return ps[f // 2 % 4][:, f % 2, 0:PER * C * PAIRS]

        def fill_view(w, f):
            return band[:, w, :, :, PER * f:PER * (f + 1)].rearrange("p c m o -> p o (c m)")

        @block.sync
        def _(sp):
            sp.wait_ge(xin_cleared, 2)

            def load(c, s, turn):
                wait(sp, xp_low, 4 * (c - RING + 1))
                rows_ = x2_dram[:, c].rearrange("b (h w) -> h b w", h=IMG)
                for dst, src in ((xin[0][SHIFT:2 * SHIFT, s], rows_[back:IMG]),
                                 (xin[0][2 * SHIFT:SEEN, s], rows_[0:BLOCK]),
                                 (xin[1][0:SEEN - SHIFT, s], rows_[BLOCK - 2 * SHIFT:back])):
                    sp.dma_start(dst, src).then_inc(xin_loaded[s], 16)

            channels(sp, load)

        @block.gpsimd
        def _(pool):
            for k in range(2):
                nc.gpsimd.memset(xin[k][:], 0.0).then_inc(xin_cleared, 1)
            for p in range(2):
                nc.gpsimd.memset(xp[1][p][:], 0.0).then_inc(xp_cleared, 1)
            for p in range(2):
                nc.gpsimd.memset(band[:, p, :, :, BLOCK:SIDE], 0.0).then_inc(band_cleared, 1)

            def store(c, s, turn):
                wait(pool, y_made, 2 * c + 2)
                rows_ = y_dram[:, c].rearrange("b (h w) -> h b w", h=IMG)
                for dst, src in ((rows_[back:IMG], y[0:SHIFT, s]), (rows_[0:BLOCK - SHIFT], y[SHIFT:BLOCK, s]),
                                 (rows_[BLOCK - SHIFT:back], y[SIDE:SIDE + BLOCK, s])):
                    pool.dma_start(dst, src).then_inc(y_stored[s], 16)

            channels(pool, store)
            for s in range(RING):
                pool.wait_ge(y_stored[s], 48 * (C // RING))

        @block.vector
        def _(dve):
            dve.wait_ge(later["loaded"], 16 * len(later["loads"]))
            k = 0
            for n in range(PIECES):
                src = taps if n == 0 else rest
                nc.vector.tensor_copy(piece[n][:], src[:]).then_inc(split_made, 1)
                k += 1
                dve.wait_ge(split_made, k)
                if n < PIECES - 1:
                    nc.vector.tensor_tensor(rest[:], src[:], piece[n][:], ALU.subtract).then_inc(split_made, 1)
                    k += 1
                    dve.wait_ge(split_made, k)
            for n in range(PIECES):
                lo, hi = 32 * n, min(32 * n + 32, ROWS)
                nc.vector.tensor_copy(split[lo:hi], piece[n][lo:hi]).then_inc(split_made, 1)
            for p in range(2):
                nc.vector.memset(xp[0][p][:], 0.0).then_inc(xp_cleared, 1)

            for f in range(FILLS):
                dve.wait_ge(band_high, f + 1)
                nc.vector.tensor_tensor(fill_view(1, f), fill_ps(f).rearrange("p (o k) -> p o k", o=PER),
                                        fill_view(0, f), ALU.subtract).then_inc(band_low, 1)

            def low(c, s, turn):
                for k in range(2):
                    for n in range(2):
                        wait(dve, xp_high, 4 * c + 2 * k + n + 1)
                        (dst, src), high = runs(k, 1, s)[n], runs(k, 0, s)[n][0]
                        nc.vector.tensor_tensor(dst, src, high, ALU.subtract).then_inc(xp_low, 1)
                nc.vector.tensor_copy(band_now[:, s], band[:, :, c]).then_inc(xp_shifted, 1)
                for k in range(2):
                    wait(dve, xp_low, 4 * c + 2 * k + 2)
                    for p in range(2):
                        nc.vector.tensor_copy(xp[k][p][SIDE:K, s, :, 0:PAD - 1], xp[k][p][0:SEEN, s, :, 1:PAD]
                                              ).then_inc(xp_shifted, 1)

            dve.wait_ge(band_cleared, 2)
            dve.wait_ge(band_low, FILLS)
            channels(dve, low)

        @block.scalar
        def _(act):
            act.wait_ge(xp_cleared, 4)

            def high(c, s, turn):
                wait(act, xin_loaded[s], 48 * (turn + 1))
                wait(act, convolved, c - RING + 1)
                for k in range(2):
                    for dst, src in runs(k, 0, s):
                        nc.scalar.copy(dst, src).then_inc(xp_high, 1)

            def keep(c, s, turn):
                wait(act, convolved, c + 1)
                wait(act, y_stored[s], 48 * turn)
                full = ps[s][:, :, 0:half * IMG].rearrange("h k (b w) -> h k b w", w=IMG)
                out = y[:, s].rearrange("h (k b) w -> h k b w", k=2)
                nc.scalar.copy(out[:, :, :, 0:back], full[:, :, :, SHIFT:IMG]).then_inc(y_made, 1)
                nc.scalar.copy(out[:, :, :, back:IMG], full[:, :, :, 0:SHIFT]).then_inc(y_made, 1)

            for f in range(FILLS):
                act.wait_ge(band_filled, f + 1)
                nc.scalar.copy(fill_view(0, f), fill_ps(f).rearrange("p (o k) -> p o k", o=PER)
                               ).then_inc(band_high, 1)
            for c in range(AHEAD):
                high(c, c, 0)

            def step(c, s, turn):
                keep(c, s, turn)
                high(c + AHEAD, (s + AHEAD) % RING, turn + (s + AHEAD) // RING)

            channels(act, step, C - RING)
            for c in range(C - RING, C):
                if c + AHEAD < C:
                    step(c, c % RING, c // RING)
                else:
                    keep(c, c % RING, c // RING)

        @block.tensor
        def _(pe):
            mm = nc.tensor.matmul
            pe.wait_ge(split_made, 8)
            for f in range(FILLS):
                wait(pe, band_low, f - 7)
                for o in range(PER):
                    for side in range(2):
                        ins = mm(fill_ps(f)[SIDE * side:SIDE * side + SIDE, C * PAIRS * o:C * PAIRS * (o + 1)],
                                 hot[:, PER * f + o, :],
                                 split[:].rearrange("p c (m t) -> p t c m", t=2)[:, side], start=True, stop=True)
                ins.then_inc(band_filled, 1)

            def convolve(c, s, turn):
                wait(pe, xp_shifted, 5 * c + 5)
                wait(pe, y_made, 2 * (c - RING + 1))
                parts = ((0, 0), (0, 1), (1, 0))
                for m in range(PAIRS):
                    rows_ = K if m < PAIRS - 1 else SEEN
                    for n, (w, part) in enumerate(parts):
                        for k in range(2):
                            for side in range(2):
                                ins = mm(ps[s][SIDE * side:SIDE * side + SIDE, k, 0:half * IMG],
                                         band_now[0:rows_, s, w, m, :],
                                         xp[side][part][0:rows_, s, half * k:half * (k + 1), 2 * m:2 * m + IMG],
                                         start=(m == 0 and n == 0), stop=(m == PAIRS - 1 and n == 2))
                ins.then_inc(convolved, 1)

            channels(pe, convolve)


RESPONSE_TILES = ("center sum_w eye_c last_row eye twins mean_all mean_top w1 w1t w2 rows norm aug "
                  "dw_b shift_c w1_own w1_both w2_own w2_both w2s_own w2s_both grn_g grn_b out_b b2 eps").split()


def response_weights(nc, sb, prm, con):
    center = sb("r_center", [R, R])
    sum_w = sb("sum_w", [R, 2, R], BF16)
    eye_c = sb("r_eye_c", [C, C + 1])
    last_row = sb("r_last_row", [1, C + 1])
    eye = sb("r_eye", [128, 128])
    twins = sb("r_twins", [128, 128])
    mean_all = sb("r_mean_all", [128, 128])
    mean_top = sb("r_mean_top", [128, 128])
    w1 = sb("r_w1", [128, 2, C])
    w1t = sb("r_w1t", [C, HID])
    w2 = sb("r_w2", [C, 2 * F1])
    rows = sb("r_rows", [1, HID])
    norm = sb("r_norm", [C, 2])
    aug = sb("r_aug", [C, C + 1])
    dw_b = sb("r_dw_b", [R, 1])
    shift_c = sb("r_shift_c", [R, 1])
    w1_own = [sb(f"r_w1_own_{p}", [R, F1], BF16) for p in "hl"]
    w1_both = [sb(f"r_w1_both_{p}", [R, 2 * F2], BF16) for p in "hl"]
    w2_own = sb("r_w2_own", [F1, C])
    w2_both = sb("r_w2_both", [2 * F2, ROWB + C])
    w2s_own = sb("r_w2s_own", [F1, 2, C])
    w2s_both = sb("r_w2s_both", [2 * F2, 2, ROWB + C])
    grn_g = sb("r_grn_g", [128, 2])
    grn_b = sb("r_grn_b", [128, 2])
    out_b = sb("r_out_b", [ROWB + C, 1])
    b2 = sb("r_b2", [ROWB + C, 1])
    eps = sb("r_eps", [R, 1])

    loads = [
        (center[:], con["center"]), (eps[:], con["eps1"]), (eye_c[:], con["eye_c"]),
        (last_row[:], con["last_row"]), (eye[:], con["eye"]), (twins[:], con["twins"]),
        (mean_all[:], con["mean_all"]), (mean_top[:], con["mean_top"]),
        (w1[:, 0, :], prm["w1"][0:F1, :]), (w1[0:F2, 1, :], prm["w1"][F1:HID, :]),
        (w2[:, 0:HID], prm["w2"]), (w2[:, HID:], prm["w2"][:, F1:HID]),
        (rows[:], prm["b1"].unsqueeze(0)), (norm[:, 0:1], prm["ln_g"].unsqueeze(1)),
        (norm[:, 1:2], prm["ln_b"].unsqueeze(1)),
    ]
    for t, nm in ((grn_g, "grn_g"), (grn_b, "grn_b")):
        loads += [(t[0:F1, 0:1], prm[nm][0:F1].unsqueeze(1)), (t[0:F2, 1:2], prm[nm][F1:HID].unsqueeze(1)),
                  (t[F2:2 * F2, 1:2], prm[nm][F1:HID].unsqueeze(1))]
    for g in range(2):
        loads += [(dw_b[ROWB * g:ROWB * g + C, :], prm["dw_b"].unsqueeze(1)),
                  (b2[ROWB * g:ROWB * g + C, :], prm["b2"].unsqueeze(1))]
    tiles = dict(zip(RESPONSE_TILES, (center, sum_w, eye_c, last_row, eye, twins, mean_all, mean_top, w1, w1t, w2, rows, norm, aug,
                                      dw_b, shift_c, w1_own, w1_both, w2_own, w2_both, w2s_own, w2s_both, grn_g, grn_b, out_b, b2, eps)))
    return tiles, [dw_b[:], b2[:]], loads


def response_phase(nc, weights, later, x2_dram, y_dram, out_dram, strips):
    with ExitStack() as ctx:
        def sb(name, shape, dt=F32):
            return ctx.enter_context(nc.sbuf_tensor(name, shape, dt))

        def sem(name):
            return ctx.enter_context(nc.semaphore(name))

        N = strips
        RING = 2 * STRIPS
        LAG = STRIPS + 2
        by_strip = [t.rearrange("b c (g s n) -> b s g c n", g=2, s=STRIPS) for t in (y_dram, x2_dram, out_dram)]

        ps_m = ctx.enter_context(nc.psum_tensor("r_ps_m", [128, 2, 512], F32))
        ps_f = [ctx.enter_context(nc.psum_tensor(f"r_ps_f{r}", [128, 2, 512], F32)) for r in range(2)]
        ps_o = ctx.enter_context(nc.psum_tensor("r_ps_o", [128, 2, 512], F32))

        (center, sum_w, eye_c, last_row, eye, twins, mean_all, mean_top, w1, w1t, w2, rows, norm, aug,
         dw_b, shift_c, w1_own, w1_both, w2_own, w2_both, w2s_own, w2s_both, grn_g, grn_b, out_b, b2, eps) = (
            weights[k] for k in RESPONSE_TILES)
        Y = sb("r_Y", [R, 2, STRIP])
        X2 = sb("r_X2", [ROWB + C, 2, STRIP])
        OUT = sb("r_OUT", [ROWB + C, 2, STRIP])
        xc = sb("r_xc", [R, STRIP])
        sq = sb("r_sq", [R, STRIP])
        sqb = [sb(f"r_sqb_{p}", [R, STRIP], BF16) for p in "hl"]
        lnv = sb("r_lnv", [R, STRIP])
        rs = sb("r_rs", [R, STRIP])
        xh = sb("r_xh", [R, STRIP])
        xm = [sb(f"r_xm_{p}", [R, 2, STRIP], BF16) for p in "hl"]
        G = sb("r_G", [128, RING, 3, STRIP])
        junk = sb("r_junk", [128, STRIP])
        sums = sb("r_sums", [128, 3, RING])
        total = sb("r_total", [128, 3])
        both = sb("r_both", [128, 2])
        gx = sb("r_gx", [128, 2])
        mean = sb("r_mean", [128, 1])
        inv = sb("r_inv", [128, 1])
        scale = sb("r_scale", [128, 2])

        def sems(text):
            return {nm: sem("r_" + nm) for nm in text.split()}

        S = sems("cleared y_cleared setup_v setup_t cen var f1 f2 pairs mean_ps xc xh hi summed totals both_made "
                 "sq_hi sq_lo gx_made inv_made scaled w2_scaled out_made sq ln rs ge lo")
        y_loaded = [sem(f"r_y_loaded{r}") for r in range(2)]
        x2_loaded = [sem(f"r_x2_loaded{r}") for r in range(2)]
        stored = [sem(f"r_stored{r}") for r in range(2)]
        block = ctx.enter_context(nc.Block())

        CLEARS = 7
        SETUP_V = 17

        def halves(ap):
            return ap.rearrange("p (b n) -> p b n", b=2)

        def steps(eng, step, last):
            turns = max((N - RING - 2) // RING, 0)
            for raw in range(-2, RING):
                step(Strip(0, raw, N))
            if turns:
                with eng.Fori(0, turns) as i:
                    for u in range(RING):
                        step(Strip(RING // 4 * i, RING + u, N))
            for raw in range(RING + RING * turns, last):
                step(Strip(0, raw, N))

        @block.sync
        def _(sp):
            sp.wait_ge(S["y_cleared"], 1)

            def step(s):
                nxt, old = s.at(2), s.at(-LAG)
                if nxt.real:
                    wait(sp, S["cen"], 2 * (nxt.n - 1))
                    for g in range(2):
                        sp.dma_start(Y[ROWB * g:ROWB * g + C, nxt.slot(2), :],
                                     by_strip[0][nxt.n // STRIPS, nxt.n % STRIPS, g]
                                     ).then_inc(y_loaded[nxt.slot(2)], 16)
                if old.real:
                    if isinstance(old.n, int) and old.n == 0:
                        wait(sp, S["cleared"], CLEARS)
                    wait(sp, S["out_made"], 2 * (old.n - 1))
                    for g in range(2):
                        sp.dma_start(X2[ROWB * g:ROWB * g + C, old.slot(2), :],
                                     by_strip[1][old.n // STRIPS, old.n % STRIPS, g]
                                     ).then_inc(x2_loaded[old.slot(2)], 16)

            steps(sp, step, N + LAG)

        @block.gpsimd
        def _(pool):
            for t in (*w1_own, *w1_both, w2_both, out_b, X2):
                nc.gpsimd.memset(t[:], 0.0).then_inc(S["cleared"], 1)

            def squares_low(s):
                if s.real:
                    wait(pool, S["var"], 2 * s.n)
                    for b in range(2):
                        cols = slice(HALF * b, HALF * b + HALF)
                        wait(pool, S["sq_hi"], 2 * s.n + b + 1)
                        nc.gpsimd.tensor_tensor(sqb[1][:, cols], sq[:, cols], sqb[0][:, cols], ALU.subtract
                                                ).then_inc(S["sq_lo"], 1)

            def low(s):
                if s.real:
                    wait(pool, S["hi"], s.n + 1)
                    wait(pool, S["f1"], 6 * (s.n - 1))
                    nc.gpsimd.tensor_tensor(xm[1][:, s.slot(2), :], xh[:], xm[0][:, s.slot(2), :],
                                            ALU.subtract).then_inc(S["lo"], 1)

            def store(s):
                if s.real:
                    wait(pool, S["out_made"], 2 * s.n + 2)
                    for g in range(2):
                        pool.dma_start(by_strip[2][s.n // STRIPS, s.n % STRIPS, g],
                                       OUT[ROWB * g:ROWB * g + C, s.slot(2), :]).then_inc(stored[s.slot(2)], 16)

            def step(s):
                squares_low(s.at(2))
                store(s.at(-LAG))
                low(s.at(2))

            steps(pool, step, N + LAG)
            for r in range(2):
                pool.wait_ge(stored[r], 32 * (N // 2))

        @block.vector
        def _(dve):
            chain = [0]

            def link(ins):
                chain[0] += 1
                ins.then_inc(S["setup_v"], 1)
                return chain[0]

            nc.vector.memset(Y[:], 1.0).then_inc(S["y_cleared"], 1)
            dve.wait_ge(S["cleared"], CLEARS)
            dve.wait_ge(later["loaded"], 16 * len(later["loads"]))
            link(nc.vector.tensor_scalar(aug[:, 0:C], eye_c[:, 0:C], norm[:, 0:1], None, ALU.mult))
            link(nc.vector.tensor_copy(aug[:, C:C + 1], norm[:, 1:2]))
            dve.wait_ge(S["setup_t"], 1)
            link(nc.vector.tensor_copy(w1t[:], ps_f[0][0:C, 0, 0:HID]))
            link(nc.vector.tensor_copy(w2_own[:], ps_f[0][:, 1, 0:C]))
            for g in range(2):
                at = F2 * g
                link(nc.vector.tensor_copy(w2_both[at:at + F2, ROWB * g:ROWB * g + C],
                                           ps_f[0][at:at + F2, 1, C:2 * C]))
            dve.wait_ge(S["setup_t"], 2)
            link(nc.vector.tensor_copy(shift_c[:], ps_m[0:R, 0, 0:1]))
            link(nc.vector.tensor_tensor(out_b[0:C, :], ps_m[0:C, 1, 0:1], b2[0:C, :], ALU.add))
            link(nc.vector.tensor_tensor(out_b[ROWB:ROWB + C, :], ps_m[ROWB:ROWB + C, 1, 0:1], b2[ROWB:ROWB + C, :], ALU.add))
            for g in range(2):
                lo = ROWB * g
                for pair_, view, src in (
                        (w1_own, lambda t: t[lo:lo + C + 1, :], ps_f[1][lo:lo + C + 1, 0, 0:F1]),
                        (w1_both, lambda t: t[lo:lo + C + 1, F2 * g:F2 * g + F2], ps_f[1][lo:lo + C + 1, 0, F1:HID])):
                    k = link(nc.vector.tensor_copy(view(pair_[0]), src))
                    dve.wait_ge(S["setup_v"], k)
                    k = link(nc.vector.tensor_tensor(view(pair_[1]), src, view(pair_[0]), ALU.subtract))

            def copy_centered(s):
                if s.real:
                    for b in range(2):
                        wait(dve, S["cen"], 2 * s.n + b + 1)
                        nc.vector.tensor_scalar(xc[:, HALF * b:HALF * b + HALF], ps_m[0:R, b, 0:HALF],
                                                shift_c[:, 0:1], None, ALU.add).then_inc(S["xc"], 1)

            def squares_high(s):
                if s.real:
                    wait(dve, S["var"], 2 * s.n)
                    for b in range(2):
                        cols = slice(HALF * b, HALF * b + HALF)
                        wait(dve, S["sq"], 2 * s.n + b + 1)
                        nc.vector.tensor_copy(sqb[0][:, cols], sq[:, cols]).then_inc(S["sq_hi"], 1)

            def normalise(s):
                if s.real:
                    wait(dve, S["rs"], s.n + 1)
                    wait(dve, S["lo"], s.n)
                    nc.vector.tensor_tensor(xh[:], xc[:], rs[:], ALU.mult).then_inc(S["xh"], 1)
                    wait(dve, S["xh"], s.n + 1)
                    wait(dve, S["f1"], 6 * (s.n - 1))
                    nc.vector.tensor_copy(xm[0][:, s.slot(2), :], xh[:]).then_inc(S["hi"], 1)

            def sum_squares(s, t):
                if s.real:
                    wait(dve, S["ge"], 6 * s.n + (4 if t < 2 else 6))
                    g = G[:, s.raw % RING, t, :]
                    wait(dve, S["summed"], 3 * s.n + t)
                    nc.vector.tensor_tensor_reduce(out=junk[:], in0=g, in1=g, scale=1.0, scalar=0.0, op0=ALU.mult,
                                                   op1=ALU.add, accum_out=sums[:, t, s.raw % RING:s.raw % RING + 1]
                                                   ).then_inc(S["summed"], 1)

            def image(s):
                return s.raw // STRIPS if isinstance(s.i, int) else s.i // 2 + s.raw // STRIPS

            def add_up(s):
                if s.real and s.raw % STRIPS == 0:
                    img, p = image(s), s.raw // STRIPS % 2
                    wait(dve, S["summed"], 3 * (s.n + STRIPS))
                    nc.vector.tensor_reduce(total[:], sums[:, :, STRIPS * p:STRIPS * (p + 1)], AX_X, ALU.add
                                            ).then_inc(S["totals"], 1)
                    wait(dve, S["totals"], 2 * img + 1)
                    nc.vector.tensor_tensor(total[:, 0:1], total[:, 0:1], total[:, 1:2], ALU.add
                                            ).then_inc(S["totals"], 1)

            def respond(s):
                if s.real and s.raw % STRIPS == 0:
                    img, p = image(s), s.raw // STRIPS % 2
                    wait(dve, S["mean_ps"], img + 1)
                    nc.vector.tensor_scalar(mean[:], ps_o[:, 0, HALF + 2:HALF + 3], EPS1, None, ALU.add
                                            ).then_inc(S["inv_made"], 1)
                    wait(dve, S["inv_made"], 2 * img + 1)
                    nc.vector.reciprocal(inv[:], mean[:]).then_inc(S["inv_made"], 1)
                    wait(dve, S["inv_made"], 2 * img + 2)
                    nc.vector.scalar_tensor_tensor(out=scale[:], in0=gx[:], scalar=inv[:, 0:1], in1=grn_g[:],
                                                   op0=ALU.mult, op1=ALU.mult).then_inc(S["scaled"], 1)
                    wait(dve, S["scaled"], 2 * img + 1)
                    nc.vector.tensor_scalar(scale[:], scale[:], 1.0, None, ALU.add).then_inc(S["scaled"], 1)
                    wait(dve, S["scaled"], 2 * img + 2)
                    nc.vector.tensor_scalar(w2s_own[:, p, :], w2_own[:], scale[:, 0:1], None, ALU.mult
                                            ).then_inc(S["w2_scaled"], 1)
                    nc.vector.tensor_scalar(w2s_both[:, p, :], w2_both[:], scale[:, 1:2], None, ALU.mult
                                            ).then_inc(S["w2_scaled"], 1)

            def finish(s):
                if s.real:
                    n = ROWB + C
                    wait(dve, x2_loaded[s.slot(2)], 32 * (s.turn(2) + 1))
                    wait(dve, stored[s.slot(2)], 32 * s.turn(2))
                    for b in range(2):
                        cols = slice(HALF * b, HALF * b + HALF)
                        wait(dve, S["f2"], 2 * s.n + b + 1)
                        nc.vector.scalar_tensor_tensor(
                            out=OUT[:, s.slot(2), cols], in0=ps_o[0:n, b, 0:HALF], scalar=out_b[:, 0:1],
                            in1=X2[:, s.slot(2), cols], op0=ALU.add, op1=ALU.add).then_inc(S["out_made"], 1)

            def step(s):
                nx2, prv = s.at(2), s.at(-1)
                respond(s.at(-LAG))
                copy_centered(nx2)
                squares_high(nx2)
                sum_squares(s.at(-2), 2)
                add_up(s.at(-LAG + 1))
                finish(s.at(-LAG))
                sum_squares(prv, 0)
                sum_squares(prv, 1)
                normalise(nx2)

            steps(dve, step, N + LAG)

        @block.scalar
        def _(act):
            act.wait_ge(S["cleared"], CLEARS)

            def square(s):
                if s.real:
                    wait(act, S["sq_lo"], 2 * s.n)
                    for b in range(2):
                        cols = slice(HALF * b, HALF * b + HALF)
                        wait(act, S["xc"], 2 * s.n + b + 1)
                        nc.scalar.activation(sq[:, cols], xc[:, cols], ACT.Square).then_inc(S["sq"], 1)

            def root(s):
                if s.real:
                    nc.scalar.preload_act_table_set("natural_log_exp_and_others")
                    for b in range(2):
                        wait(act, S["var"], 2 * s.n + b + 1)
                        nc.scalar.activation(lnv[:, HALF * b:HALF * b + HALF], ps_m[0:R, b, 0:HALF], ACT.Ln,
                                             scale=1.0 / C, bias=eps[:, 0:1]).then_inc(S["ln"], 1)
                    wait(act, S["ln"], 2 * s.n + 2)
                    nc.scalar.activation(rs[:], lnv[:], ACT.Exp, scale=-0.5).then_inc(S["rs"], 1)

            def features(s, t):
                if s.real:
                    slot = s.raw % RING
                    if t == 0:
                        wait(act, S["f2"], 2 * (s.n - RING + 1))
                        wait(act, S["summed"], 3 * (s.n - RING + 1))
                    for b in range(2):
                        wait(act, S["f1"], 6 * s.n + 2 * t + b + 1)
                        cols = slice(HALF * (t if t < 2 else b), HALF * (t if t < 2 else b) + HALF)
                        nc.scalar.activation(G[:, slot, b if t < 2 else 2, cols],
                                             ps_f[(s.raw + t) % 2][:, b, 0:HALF], ACT.Gelu).then_inc(S["ge"], 1)

            def norms_root(s):
                if s.real and s.raw % STRIPS == 0:
                    img = s.raw // STRIPS if isinstance(s.i, int) else s.i // 2 + s.raw // STRIPS
                    wait(act, S["pairs"], img + 1)
                    nc.scalar.activation(gx[:], ps_o[:, 0, HALF:HALF + 2], ACT.Sqrt).then_inc(S["gx_made"], 1)

            def step(s):
                nx2 = s.at(2)
                features(s, 0)
                square(nx2)
                features(s, 1)
                norms_root(s.at(-LAG + 1))
                root(nx2)
                features(s, 2)

            steps(act, step, N + LAG)

        @block.tensor
        def _(pe):
            mm = nc.tensor.matmul
            pe.wait_ge(later["loaded"], 16 * len(later["loads"]))
            nc.tensor.transpose(ps_f[0][0:C, 0, 0:F1], w1[:, 0, :], eye[:])
            nc.tensor.transpose(ps_f[0][0:C, 0, F1:HID], w1[0:F2, 1, :], eye[0:F2, 0:F2])
            nc.tensor.transpose(ps_f[0][:, 1, 0:C], w2[:, 0:F1], eye[0:C, 0:C])
            nc.tensor.transpose(ps_f[0][:, 1, C:2 * C], w2[:, F1:2 * F1], eye[0:C, 0:C]).then_inc(S["setup_t"], 1)
            pe.wait_ge(S["setup_v"], 6)
            mm(ps_m[0:R, 0, 0:1], center[:], dw_b[:], start=True, stop=True)
            for g in range(2):
                lo = ROWB * g
                out = ps_m[lo:lo + C, 1, 0:1]
                mm(out, w2_own[:], grn_b[:, 0:1], start=True, stop=False)
                mm(out, w2_both[0:F2, 0:C], grn_b[0:F2, 1:2], start=False, stop=True)
                out = ps_f[1][lo:lo + C + 1, 0, 0:HID]
                mm(out, aug[:], w1t[:], start=True, stop=False)
                ins = mm(out, last_row[:], rows[:], start=False, stop=True)
            ins.then_inc(S["setup_t"], 1)
            pe.wait_ge(S["setup_v"], SETUP_V)

            def centre(s):
                if s.real:
                    wait(pe, y_loaded[s.slot(2)], 32 * (s.turn(2) + 1))
                    for b in range(2):
                        wait(pe, S["ln"], 2 * (s.n - 1) + b + 1)
                        mm(ps_m[0:R, b, 0:HALF], center[:], Y[:, s.slot(2), HALF * b:HALF * b + HALF],
                           start=True, stop=True).then_inc(S["cen"], 1)

            def variance(s):
                if s.real:
                    for b in range(2):
                        wait(pe, S["sq_lo"], 2 * s.n + b + 1)
                        for m in range(2):
                            ins = mm(ps_m[0:R, b, 0:HALF], sum_w[:, 1, :], sqb[m][:, HALF * b:HALF * b + HALF],
                                     start=(m == 0), stop=(m == 1))
                        ins.then_inc(S["var"], 1)

            def fc1(s, t):
                if s.real:
                    if t == 0:
                        wait(pe, S["hi"], s.n + 1)
                        wait(pe, S["lo"], s.n + 1)
                    r = s.slot(2)
                    ps = ps_f[(s.raw + t) % 2]
                    for b in range(2):
                        wait(pe, S["ge"], 2 * (3 * s.n + t - 2) + b + 1)
                        for k, (w, m) in enumerate(((0, 0), (0, 1), (1, 0))):
                            if t < 2:
                                lo = ROWB * b
                                ins = mm(ps[:, b, 0:HALF], w1_own[w][lo:lo + C + 1, :],
                                         xm[m][lo:lo + C + 1, r, HALF * t:HALF * t + HALF],
                                         start=(k == 0), stop=(k == 2))
                            else:
                                ins = mm(ps[:, b, 0:HALF], w1_both[w][:], xm[m][:, r, HALF * b:HALF * b + HALF],
                                         start=(k == 0), stop=(k == 2))
                        ins.then_inc(S["f1"], 1)

            def respond(s, part):
                if s.real and s.raw % STRIPS == 0:
                    img = s.raw // STRIPS if isinstance(s.i, int) else s.i // 2 + s.raw // STRIPS
                    if part == 0:
                        wait(pe, S["totals"], 2 * img + 2)
                        wait(pe, S["out_made"], 2 * s.n)
                        mm(ps_o[:, 0, HALF:HALF + 1], eye[:], total[:, 0:1], start=True, stop=True)
                        mm(ps_o[:, 0, HALF + 1:HALF + 2], twins[:], total[:, 2:3], start=True, stop=True
                           ).then_inc(S["pairs"], 1)
                    elif part == 1:
                        wait(pe, S["gx_made"], img + 1)
                        mm(ps_o[:, 0, HALF + 2:HALF + 3], mean_all[:], gx[:, 0:1], start=True, stop=False)
                        mm(ps_o[:, 0, HALF + 2:HALF + 3], mean_top[:], gx[:, 1:2], start=False, stop=True
                           ).then_inc(S["mean_ps"], 1)
                    else:
                        wait(pe, S["w2_scaled"], 2 * img + 2)

            def fc2(s):
                if s.real:
                    p = s.raw // STRIPS % 2
                    slot = s.raw % RING
                    for b in range(2):
                        wait(pe, S["out_made"], 2 * (s.n - 1) + b + 1)
                        cols = slice(HALF * b, HALF * b + HALF)
                        mm(ps_o[0:ROWB + C, b, 0:HALF], w2s_both[:, p, :], G[:, slot, 2, cols], start=True, stop=False)
                        for g in range(2):
                            lo = ROWB * g
                            ins = mm(ps_o[lo:lo + C, b, 0:HALF], w2s_own[:, p, :], G[:, slot, g, cols],
                                     start=False, stop=True)
                        ins.then_inc(S["f2"], 1)

            def step(s):
                old = s.at(-LAG)
                fc1(s, 0)
                respond(old, 1)
                variance(s.at(1))
                respond(old, 2)
                fc2(old)
                centre(s.at(2))
                fc1(s, 1)
                fc1(s, 2)
                respond(s.at(-LAG + 1), 0)

            steps(pe, step, N + LAG)

def constants():
    import numpy as np

    f = np.float32
    out = {}
    center = np.zeros((R, R), f)
    for g in range(2):
        lo = ROWB * g
        center[lo:lo + C, lo:lo + C] = np.eye(C) - 1.0 / C
        center[lo + C, lo + C] = 1.0
    out["center"] = center
    sums = np.zeros((R, 2, R), f)
    eps0 = np.full((R, 1), EPS0, f)
    for g in range(2):
        lo = ROWB * g
        sums[lo:lo + C, :, lo:lo + C] = 1
        sums[lo + C, 1, lo + C] = C
        eps0[lo + C] = 0
    out["sums"] = sums.reshape(R, 2 * R)
    out["eps0"] = eps0
    out["eps1"] = np.where(eps0 == 0, f(0), f(EPS1))
    out["eye_c"] = np.eye(C, C + 1, dtype=f)
    out["last_row"] = np.eye(1, C + 1, C, dtype=f)
    pick_q, pick_k = np.zeros((R, R), f), np.zeros((R, KEYS), f)
    ones, minus = np.zeros((R, KEYS), f), np.zeros((R, TOK), f)
    for j in range(TOK):
        for lo in (0, ROWB):
            pick_q[lo + j, [j, ROWB + j]] = 1
            pick_k[lo + j, [j, TOK + j]] = 1
            minus[lo + j, j] = -1
    for g in range(2):
        ones[ROWB * g:ROWB * g + TOK, TOK * g:TOK * g + TOK] = 1
    out["picks"] = np.concatenate([pick_q, pick_k, ones, minus], 1)
    key_ones = np.zeros((KEYS, 2 * DH), f)
    for g in range(2):
        key_ones[TOK * g:TOK * g + TOK, DH * g:DH * g + DH] = 1
    out["key_ones"] = key_ones
    out["eye"] = np.eye(128, dtype=f)
    p = np.arange(128)
    out["twins"] = (p[:, None] % F2 == p[None, :] % F2).astype(f)
    out["mean_all"] = np.full((128, 128), 1.0 / HID, f)
    out["mean_top"] = np.where(p[:, None] < F2, f(1.0 / HID), f(0)) * np.ones((1, 128), f)
    one = 0x3F80
    dy = np.arange(SIDE)[None, :] - np.arange(BLOCK)[:, None]
    out["bands"] = ((dy[None] == np.arange(WS)[:, None, None]) * one).astype(np.uint16)
    return out


def windows_first(x):
    import numpy as np

    b = x.shape[0]
    x = np.roll(x, (-SHIFT, -SHIFT), axis=(2, 3))
    x = x.reshape(b, C, 2, STRIPS, WS, WINS, WS)
    return np.ascontiguousarray(x.transpose(0, 3, 2, 1, 5, 4, 6)).reshape(b * STRIPS, 2, C, STRIP)


def program(nc, x_in, prm, con, out_dram, images):
    scratch = {}
    for name, shape in (("x2_scratch", (images, C, PLANE)), ("y_scratch", (images, C, PLANE)),
                        ("table_0", (HEADS, REL)), ("table_1", (HEADS, REL)),
                        ("table_runs_0", (HEADS, TOK, RUN)), ("table_runs_1", (HEADS, TOK, RUN))):
        scratch[name] = nc.dram_tensor(name, shape, F32, kind="Internal").ap()
    layer0 = {k[8:]: v for k, v in prm.items() if k.startswith("L0_conv_")}
    layer1 = {k[8:]: v for k, v in prm.items() if k.startswith("L1_conv_")}
    with ExitStack() as ctx:
        def sb(name, shape, dt=F32):
            return ctx.enter_context(nc.sbuf_tensor(name, shape, dt))

        tiles, zeros, loads = response_weights(nc, sb, layer1, con)
        later = {name: ctx.enter_context(nc.semaphore("later_" + name)) for name in ("cleared", "loaded")}
        with ExitStack() as inner:
            bands, taps = convolution_weights(
                nc, lambda name, shape, dt: inner.enter_context(nc.sbuf_tensor(name, shape, dt)),
                layer1["dw_w"], con["bands"])
            later["sum_w"] = tiles["sum_w"]
            later["zeros"] = bands["zeros"] + zeros
            later["loads"] = taps + loads
            attention_phase(nc, x_in, layer0, con, [scratch[f"table_{side}"] for side in range(2)],
                            [scratch[f"table_runs_{side}"] for side in range(2)], scratch["x2_scratch"],
                            STRIPS * images, later)
            convolution_phase(nc, bands, later, scratch["x2_scratch"], scratch["y_scratch"], images)
        response_phase(nc, tiles, later, scratch["x2_scratch"], scratch["y_scratch"], out_dram, STRIPS * images)


def kernel(**inputs):
    import numpy as np
    import concourse.bacc as bacc
    from concourse.bass_utils import run_bass_kernel_spmd

    nc = bacc.Bacc("TRN2", target_bir_lowering=False, num_devices=1)
    images = inputs["x"].shape[0]
    arrays, prm, con = {}, {}, {}

    def give(name, a):
        arrays[name] = a
        return nc.dram_tensor(name, a.shape, mybir.dt.from_np(a.dtype), kind="ExternalInput").ap()

    x_in = give("x_windows", windows_first(np.asarray(inputs["x"])))
    for name, a in inputs.items():
        if name != "x":
            prm[name] = give(name, np.ascontiguousarray(a))
    for name, a in constants().items():
        con[name] = give("const_" + name, a)
    out = nc.dram_tensor("out_rolled", (images, C, PLANE), F32, kind="ExternalOutput").ap()
    program(nc, x_in, prm, con, out, images)
    result = run_bass_kernel_spmd(nc, [arrays], core_ids=[0]).results[0]["out_rolled"]
    return np.roll(result.reshape(images, C, IMG, IMG), (SHIFT, SHIFT), axis=(2, 3))
```
